# Optimizing a Trainium2 kernel written in Bass

```python
import numpy as np
import jax
import jax.numpy as jnp

def _softmax(x, axis=-1):
    return jax.nn.softmax(x, axis=axis)

def _gelu(x):
    return jax.nn.gelu(x, approximate=True)

def _silu(x):
    return jax.nn.silu(x)

def _sigmoid(x):
    return jax.nn.sigmoid(x)

def _layernorm(x, axis=-1, eps=1e-05):
    m = jnp.mean(x, axis=axis, keepdims=True)
    v = jnp.var(x, axis=axis, keepdims=True)
    return (x - m) / jnp.sqrt(v + eps)

def _scatter_add(tgt, idx, src, axis=0):
    return tgt.at[idx].add(src)

def _segment_sum(src, seg, n):
    return jax.ops.segment_sum(src, seg, n)
kernel_name = 'mk_gnn_preln_d4_gnn_r16_e0aee0'

def setup_inputs(seed: int=0):
    np.random.seed(seed)
    _w = jnp.asarray

    def _rec_inputs():
        import jax
        import jax.numpy as jnp
        _gk = jax.random.key(seed)
        x = -1.686e-05 + 1 * jax.random.normal(jax.random.fold_in(_gk, 1), (6250, 16), jnp.float32)
        _s = jax.random.randint(jax.random.fold_in(_gk, 2), (100000,), 0, 6250, jnp.int32)
        _d = jax.random.randint(jax.random.fold_in(_gk, 3), (100000,), 0, 6250, jnp.int32)
        _loop = jnp.arange(6250, dtype=jnp.int32)
        src = jnp.concatenate([_s, _d, _loop])
        dst = jnp.concatenate([_d, _s, _loop])
        _o = jnp.argsort(dst, stable=True)
        src = src[_o]
        dst = dst[_o]
        edge_attr_16 = -3.57403e-05 + 0.999761 * jax.random.normal(jax.random.fold_in(_gk, 12), (206250, 16), jnp.float32)
        edge_attr_6 = -1.02531e-05 + 0.999808 * jax.random.normal(jax.random.fold_in(_gk, 13), (206250, 6), jnp.float32)
        return (x, src, dst, edge_attr_16, edge_attr_6)
    x, src, dst, edge_attr_16, edge_attr_6 = _rec_inputs()

    def _L0_gnn_setup():
        import jax, jax.numpy as jnp
        import numpy as np
        N = 31250
        E = 500000
        C = 16

        def gcn_conv(x, edge_index, W):
            n = x.shape[0]
            h = x @ W
            loops = jnp.arange(n, dtype=edge_index.dtype)
            src = jnp.concatenate([edge_index[0], loops])
            dst = jnp.concatenate([edge_index[1], loops])
            deg = jax.ops.segment_sum(jnp.ones_like(dst, dtype=h.dtype), dst, num_segments=n)
            dinv = jnp.where(deg > 0, jax.lax.rsqrt(deg), 0.0)
            norm = dinv[src] * dinv[dst]
            msg = h[src] * norm[:, None]
            return jax.ops.segment_sum(msg, dst, num_segments=n)
        key = jax.random.key(seed)
        ks = jax.random.split(key, 8)
        xx = jax.random.normal(ks[0], (N, C), dtype=jnp.float32)
        edge_index = jax.random.randint(ks[1], (2, E), 0, N, dtype=jnp.int64)
        W_gcn = jax.random.normal(ks[2], (C, 3 * C), dtype=jnp.float32) / np.sqrt(C)
        W1 = jax.random.normal(ks[3], (3 * C, 32), dtype=jnp.float32) / np.sqrt(3 * C)
        b1 = jnp.zeros((32,), dtype=jnp.float32)
        W2 = jax.random.normal(ks[4], (32, C), dtype=jnp.float32) / np.sqrt(32)
        b2 = jnp.zeros((C,), dtype=jnp.float32)
        return {'xx': xx, 'edge_index': edge_index, 'W_gcn': W_gcn, 'W1': W1, 'b1': b1, 'W2': W2, 'b2': b2}
    _L0_gnn_all = _L0_gnn_setup()
    _L0_gnn_in = {k: v for k, v in _L0_gnn_all.items() if k in ('W_gcn', 'W1', 'b1', 'W2', 'b2')}
    del _L0_gnn_all

    def _L1_gnn_setup():
        import jax, jax.numpy as jnp
        import numpy as np
        N_NODES = 6250
        N_EDGES = 100000
        IN_DIM = 16
        OUT_DIM = 16
        E_DIM = 6
        EDGE_H = 64
        BN_EPS = 1e-05
        key = jax.random.key(seed)
        ks = jax.random.split(key, 8)
        h = jax.random.normal(ks[0], (N_NODES, IN_DIM), dtype=jnp.float32)
        efeat = jax.random.normal(ks[1], (N_EDGES, E_DIM), dtype=jnp.float32)
        src = jax.random.randint(ks[2], (N_EDGES,), 0, N_NODES, dtype=jnp.int32)
        dst = jax.random.randint(ks[3], (N_EDGES,), 0, N_NODES, dtype=jnp.int32)
        W1 = jax.random.normal(ks[4], (E_DIM, EDGE_H), dtype=jnp.float32) * 0.1
        b1 = jnp.zeros((EDGE_H,), dtype=jnp.float32)
        W2 = jax.random.normal(ks[5], (EDGE_H, IN_DIM * OUT_DIM), dtype=jnp.float32) * 0.1
        b2 = jnp.zeros((IN_DIM * OUT_DIM,), dtype=jnp.float32)
        bias = jnp.zeros((OUT_DIM,), dtype=jnp.float32)
        gamma = jnp.ones((OUT_DIM,), dtype=jnp.float32)
        beta = jnp.zeros((OUT_DIM,), dtype=jnp.float32)
        return {'h': h, 'efeat': efeat, 'src': src, 'dst': dst, 'W1': W1, 'b1': b1, 'W2': W2, 'b2': b2, 'bias': bias, 'gamma': gamma, 'beta': beta}
    _L1_gnn_all = _L1_gnn_setup()
    _L1_gnn_in = {k: v for k, v in _L1_gnn_all.items() if k in ('W1', 'b1', 'W2', 'b2', 'bias', 'gamma', 'beta')}
    del _L1_gnn_all

    def _L2_gnn_setup():
        import jax, jax.numpy as jnp
        import numpy as np
        STALK_DIM = 16
        N_NODES = 3125
        N_EDGES = 25000
        HIDDEN = 64
        key = jax.random.key(seed)
        k1, k2, k3, k4 = jax.random.split(key, 4)
        d = STALK_DIM
        x = jax.random.normal(k1, (N_NODES, d), dtype=jnp.float32)
        edge_index = jax.random.randint(k2, (2, N_EDGES), 0, N_NODES, dtype=jnp.int64)
        W1 = jax.random.normal(k3, (HIDDEN, 2 * d), dtype=jnp.float32) * (1.0 / np.sqrt(2 * d))
        b1 = jnp.zeros((HIDDEN,), dtype=jnp.float32)
        W2 = jax.random.normal(k4, (d, HIDDEN), dtype=jnp.float32) * (1.0 / np.sqrt(HIDDEN))
        b2 = jnp.zeros((d,), dtype=jnp.float32)
        return {'x': x, 'edge_index': edge_index, 'W1': W1, 'b1': b1, 'W2': W2, 'b2': b2}
    _L2_gnn_all = _L2_gnn_setup()
    _L2_gnn_in = {k: v for k, v in _L2_gnn_all.items() if k in ('W1', 'b1', 'W2', 'b2')}
    del _L2_gnn_all

    def _L3_gnn_setup():
        import jax, jax.numpy as jnp
        import numpy as np
        N_NODES = 1875
        N_EDGES = 18750
        IN_FEATS = 16
        OUT_FEATS = 16
        EDGE_DIM = 16
        key = jax.random.key(seed)
        ks = jax.random.split(key, 8)
        feat = jax.random.normal(ks[0], (N_NODES, IN_FEATS), dtype=jnp.float32)
        efeat = jax.random.normal(ks[1], (N_EDGES, EDGE_DIM), dtype=jnp.float32)
        W_msg = jax.random.normal(ks[2], (EDGE_DIM, IN_FEATS * OUT_FEATS), dtype=jnp.float32) * 0.1
        b_msg = jnp.zeros((IN_FEATS * OUT_FEATS,), dtype=jnp.float32)
        W_attn = jax.random.normal(ks[3], (EDGE_DIM, IN_FEATS * OUT_FEATS), dtype=jnp.float32) * 0.1
        b_attn = jnp.zeros((IN_FEATS * OUT_FEATS,), dtype=jnp.float32)
        src = jax.random.randint(ks[4], (N_EDGES,), 0, N_NODES, dtype=jnp.int32)
        dst = jax.random.randint(ks[5], (N_EDGES,), 0, N_NODES, dtype=jnp.int32)
        return {'feat': feat, 'efeat': efeat, 'W_msg': W_msg, 'b_msg': b_msg, 'W_attn': W_attn, 'b_attn': b_attn, 'src': src, 'dst': dst}
    _L3_gnn_all = _L3_gnn_setup()
    _L3_gnn_in = {k: v for k, v in _L3_gnn_all.items() if k in ('W_msg', 'b_msg', 'W_attn', 'b_attn')}
    del _L3_gnn_all
    return {'x': x, 'src': src, 'dst': dst, 'edge_attr_16': edge_attr_16, 'edge_attr_6': edge_attr_6, 'L0_gnn_W_gcn': _L0_gnn_in['W_gcn'], 'L0_gnn_W1': _L0_gnn_in['W1'], 'L0_gnn_b1': _L0_gnn_in['b1'], 'L0_gnn_W2': _L0_gnn_in['W2'], 'L0_gnn_b2': _L0_gnn_in['b2'], 'L1_gnn_W1': _L1_gnn_in['W1'], 'L1_gnn_b1': _L1_gnn_in['b1'], 'L1_gnn_W2': _L1_gnn_in['W2'], 'L1_gnn_b2': _L1_gnn_in['b2'], 'L1_gnn_bias': _L1_gnn_in['bias'], 'L1_gnn_gamma': _L1_gnn_in['gamma'], 'L1_gnn_beta': _L1_gnn_in['beta'], 'L2_gnn_W1': _L2_gnn_in['W1'], 'L2_gnn_b1': _L2_gnn_in['b1'], 'L2_gnn_W2': _L2_gnn_in['W2'], 'L2_gnn_b2': _L2_gnn_in['b2'], 'L3_gnn_W_msg': _L3_gnn_in['W_msg'], 'L3_gnn_b_msg': _L3_gnn_in['b_msg'], 'L3_gnn_W_attn': _L3_gnn_in['W_attn'], 'L3_gnn_b_attn': _L3_gnn_in['b_attn']}

def reference(x, src, dst, edge_attr_16, edge_attr_6, L0_gnn_W_gcn, L0_gnn_W1, L0_gnn_b1, L0_gnn_W2, L0_gnn_b2, L1_gnn_W1, L1_gnn_b1, L1_gnn_W2, L1_gnn_b2, L1_gnn_bias, L1_gnn_gamma, L1_gnn_beta, L2_gnn_W1, L2_gnn_b1, L2_gnn_W2, L2_gnn_b2, L3_gnn_W_msg, L3_gnn_b_msg, L3_gnn_W_attn, L3_gnn_b_attn):
    import jax
    import jax.numpy as jnp

    def _L0_gnn_ref(xx, edge_index, W_gcn, W1, b1, W2, b2):
        import jax, jax.numpy as jnp
        import numpy as np
        N = 31250
        E = 500000
        C = 16

        def gcn_conv(x, edge_index, W):
            n = x.shape[0]
            h = x @ W
            loops = jnp.arange(n, dtype=edge_index.dtype)
            src = jnp.concatenate([edge_index[0], loops])
            dst = jnp.concatenate([edge_index[1], loops])
            deg = jax.ops.segment_sum(jnp.ones_like(dst, dtype=h.dtype), dst, num_segments=n)
            dinv = jnp.where(deg > 0, jax.lax.rsqrt(deg), 0.0)
            norm = dinv[src] * dinv[dst]
            msg = h[src] * norm[:, None]
            return jax.ops.segment_sum(msg, dst, num_segments=n)
        features = gcn_conv(xx, edge_index, W_gcn)
        update = jax.nn.relu(features @ W1 + b1) @ W2 + b2
        return xx + update

    def _L1_gnn_ref(h, efeat, src, dst, W1, b1, W2, b2, bias, gamma, beta):
        import jax, jax.numpy as jnp
        import numpy as np
        N_NODES = 6250
        N_EDGES = 100000
        IN_DIM = 16
        OUT_DIM = 16
        E_DIM = 6
        EDGE_H = 64
        BN_EPS = 1e-05
        E = efeat.shape[0]
        N = h.shape[0]
        w = jax.nn.relu(efeat @ W1 + b1) @ W2 + b2
        w = w.reshape(E, IN_DIM, OUT_DIM)
        msg = jnp.einsum('ei,eio->eo', h[src], w)
        agg = jax.ops.segment_sum(msg, dst, num_segments=N)
        deg = jax.ops.segment_sum(jnp.ones((E,), h.dtype), dst, num_segments=N)
        out = agg / jnp.maximum(deg, 1.0)[:, None] + bias
        r = jax.nn.relu(out)
        mean = jnp.mean(r, axis=0)
        var = jnp.mean((r - mean) ** 2, axis=0)
        return (r - mean) * jax.lax.rsqrt(var + BN_EPS) * gamma + beta

    def _L2_gnn_ref(x, edge_index, W1, b1, W2, b2):
        import jax, jax.numpy as jnp
        import numpy as np
        STALK_DIM = 16
        N_NODES = 3125
        N_EDGES = 25000
        HIDDEN = 64
        d = x.shape[1]
        n = x.shape[0]
        src, dst = (edge_index[0], edge_index[1])
        xs, xd = (x[src], x[dst])

        def reflection(a, b):
            h = jax.nn.relu(jnp.concatenate([a, b], axis=1) @ W1.T + b1)
            return h @ W2.T + b2

        def householder(v):
            vn = v / jnp.maximum(jnp.linalg.norm(v, axis=1, keepdims=True), 1e-12)
            return jnp.eye(d, dtype=v.dtype)[None] - 2.0 * vn[:, :, None] * vn[:, None, :]
        F_s = householder(reflection(xs, xd))
        F_d = householder(reflection(xd, xs))
        L_sd = -jnp.einsum('eki,ekj->eij', F_s, F_d)
        ones_e = jnp.ones(src.shape[0], dtype=x.dtype)
        deg = jnp.zeros(n, dtype=x.dtype).at[src].add(ones_e).at[dst].add(ones_e)
        deg_inv_sqrt = 1.0 / jnp.sqrt(jnp.maximum(deg, 1e-05))
        coef = deg_inv_sqrt[src] * deg_inv_sqrt[dst]
        msg_s = coef[:, None] * jnp.einsum('eij,ej->ei', L_sd, xd)
        msg_d = coef[:, None] * jnp.einsum('eji,ej->ei', L_sd, xs)
        out = x - jnp.zeros_like(x).at[src].add(msg_s) - jnp.zeros_like(x).at[dst].add(msg_d)
        return jax.nn.relu(out)

    def _L3_gnn_ref(feat, efeat, W_msg, b_msg, W_attn, b_attn, src, dst):
        import jax, jax.numpy as jnp
        import numpy as np
        N_NODES = 1875
        N_EDGES = 18750
        IN_FEATS = 16
        OUT_FEATS = 16
        EDGE_DIM = 16
        N, in_f = feat.shape
        E = efeat.shape[0]
        w_m = (efeat @ W_msg + b_msg).reshape(E, in_f, -1)
        w_a = (efeat @ W_attn + b_attn).reshape(E, in_f, -1)
        h_src = feat[src][:, :, None]
        e1 = w_m * h_src
        e2 = w_a * h_src
        seg_max = jax.ops.segment_max(e2, dst, num_segments=N)
        ex = jnp.exp(e2 - seg_max[dst])
        denom = jax.ops.segment_sum(ex, dst, num_segments=N)
        attn = ex / denom[dst]
        ft = jax.ops.segment_sum(e1 * attn, dst, num_segments=N)
        return ft.sum(axis=1)
    edge_index = jnp.stack([src, dst])
    h = jnp.maximum(_layernorm(x, axis=-1), 0.0)
    x = x + _L0_gnn_ref(h, edge_index, L0_gnn_W_gcn, L0_gnn_W1, L0_gnn_b1, L0_gnn_W2, L0_gnn_b2)
    h = jnp.maximum(_layernorm(x, axis=-1), 0.0)
    x = x + _L1_gnn_ref(h, edge_attr_6, src, dst, L1_gnn_W1, L1_gnn_b1, L1_gnn_W2, L1_gnn_b2, L1_gnn_bias, L1_gnn_gamma, L1_gnn_beta)
    h = jnp.maximum(_layernorm(x, axis=-1), 0.0)
    x = x + _L2_gnn_ref(h, edge_index, L2_gnn_W1, L2_gnn_b1, L2_gnn_W2, L2_gnn_b2)
    h = jnp.maximum(_layernorm(x, axis=-1), 0.0)
    x = x + _L3_gnn_ref(h, edge_attr_16, L3_gnn_W_msg, L3_gnn_b_msg, L3_gnn_W_attn, L3_gnn_b_attn, src, dst)
    return x

_drawn_inputs = setup_inputs


def setup_inputs(seed=0):
    import zlib

    import numpy as np

    out = dict(_drawn_inputs(seed))
    spreads = {'L0_gnn_b1': (0.0, 0.1),
     'L0_gnn_b2': (0.0, 0.1),
     'L1_gnn_b1': (0.0, 0.1),
     'L1_gnn_b2': (0.0, 0.1),
     'L1_gnn_bias': (0.0, 0.1),
     'L1_gnn_gamma': (1.0, 0.2),
     'L1_gnn_beta': (0.0, 0.1),
     'L2_gnn_b1': (0.0, 0.789),
     'L2_gnn_b2': (0.0, 0.722),
     'L3_gnn_b_msg': (0.0, 0.1),
     'L3_gnn_b_attn': (0.0, 0.1)}
    factors = {}
    for name, (base, spread) in spreads.items():
        noise = np.random.default_rng([zlib.crc32(name.encode()), seed]).standard_normal(out[name].shape)
        drawn = base * np.exp(spread * noise) if base else spread * noise
        out[name] = jnp.asarray(drawn.astype(out[name].dtype))
    for name, factor in factors.items():
        out[name] = (out[name] * factor).astype(out[name].dtype)
    return out
```

```python
from contextlib import ExitStack

import concourse.bass as bass
from concourse import mybir
from concourse.alu_op_type import AluOpType as ALU

F32 = mybir.dt.float32
BF16 = mybir.dt.bfloat16
I32 = mybir.dt.int32
ACT = mybir.ActivationFunctionType
AX = mybir.AxisListType

P = 128
N = 6250
C = -(-N // P)
NP = C * P
E = 206250
L = -(-E // P)
D = 16
J = 26
NB = L // J
J3 = 13
NB3 = L // J3
T2 = 18
S3 = 3 * 256
BIG = 1e30
SKIP = 8192
EPS = 1e-5
assert NB * J == L and NB % 2 == 0 and NB3 * J3 == L and NB3 % 2 == 0


class Chain:

    def __init__(self, eng, sem):
        self.eng, self.sem, self.n, self.base = eng, sem, 0, 0

    def do(self, ins):
        ins.then_inc(self.sem, 1)
        self.n += 1
        return self.n

    def wait(self, n):
        self.eng.wait_ge(self.sem, self.base + n)

    def sync(self):
        self.eng.wait_ge(self.sem, self.base + self.n)

    def to(self, ins):
        self.do(ins)
        self.sync()

    def tell(self, sem):
        self.sync()
        self.eng.sem_inc(sem, 1)

    def loop(self, i, per):
        self.start, self.per, self.base = self.n, per, i * per

    def end(self, turns):
        assert self.n - self.start == self.per, (self.n - self.start, self.per)
        self.n, self.base = self.start + turns * self.per, 0


def gnn_kernel(nc, a, out):
    ctx = ExitStack()

    def sb(name, shape, dt=F32, c=ctx):
        return c.enter_context(nc.sbuf_tensor(name, shape, dt))

    def ps(name, shape, c, dt=F32):
        return c.enter_context(nc.psum_tensor(name, shape, dt))

    def sem(name, c=ctx):
        return c.enter_context(nc.semaphore(name))

    def dram(name, shape):
        return nc.dram_tensor(name, shape, F32, kind="Internal").ap()

    tab = [dram(f"tab{k}", (NP, T2 if k == 2 else D)) for k in range(4)]
    runs = [dram(f"runs{k}", (P * L, D)) for k in range(3)]
    corr = [dram(f"corr{k}", (NP, D)) for k in range(3)]
    state3 = dram("state3", (NP, S3))

    with ctx:
        ident = sb("ident", [P, P])
        tri = sb("tri", [P, P])
        ones = sb("ones", [P, P])
        iota_f = sb("iota_f", [P, P])
        x = sb("x", [P, C, D])
        h = sb("h", [P, C, D])
        agg = sb("agg", [P, C, D])
        tmp = sb("tmp", [P, C, D])
        same = sb("same", [P, L])
        apart = sb("apart", [P, L])
        end_to = sb("end_to", [P, L], I32)
        src_lo = sb("src_lo", [P, L])
        src_hi = sb("src_hi", [P, L])
        cnt_d = sb("cnt_d", [P, C])
        full = sb("full", [P, C])
        real = sb("real", [P, C])
        dinv = sb("dinv", [P, C])
        dis = sb("dis", [P, C])
        v1 = sb("v1", [P, C])
        v2 = sb("v2", [P, C])
        last_edge = sb("last_edge", [P, C], I32)
        through = sb("through", [P, P])
        carry_to = sb("carry_to", [P, 1], I32)
        first_node = sb("first_node", [P, 1], I32)
        eps = sb("eps", [P, 1])

        def bc_f(t):
            return t[:, :, None].to_broadcast([P, C, D])

        def flat(t):
            return t.rearrange("p c f -> p (c f)")

        def by_node(t):
            return t.rearrange("(c p) f -> p c f", p=P)

        def stage(name):
            c = ExitStack()
            return (c, lambda n, s, dt=F32: sb(f"{name}_{n}", s, dt, c),
                    lambda n: ps(f"{name}_{n}", [P, 512], c),
                    lambda *names: [used.append(sem(f"{name}_{n}", sems)) or used[-1] for n in names])

        used, sems = [], ExitStack()

        def renew_semaphores():
            with nc.Block() as block:
                @block.gpsimd
                def _(e):
                    for s in used:
                        e.sem_clear(s)
            sems.close()
            used.clear()

        c, sbl, psl, seml = stage("prep")
        with c:
            dstw = sbl("dstw", [P, L + 2], I32)
            dstf = sbl("dstf", [P, L + 2])
            srci = sbl("srci", [P, L], I32)
            ti = sbl("ti", [P, L], I32)
            nxt = sbl("nxt", [P, L])
            dst_lo = sbl("dst_lo", [P, L])
            dst_hi = sbl("dst_hi", [P, L])
            iota_i = sbl("iota_i", [P, P], I32)
            iota_b = sbl("iota_b", [P, P], BF16)
            node_i = sbl("node_i", [P, C], I32)
            node_f = sbl("node_f", [P, C])
            cnt_s = sbl("cnt_s", [P, C])
            zero = sbl("zero", [P, 7 * S3])
            digits = [sbl(f"digits{b}", [P, 2, J, P + C], BF16) for b in range(2)]
            f1, f2, f3, f4 = (sbl(f"f{k}", [P, 1]) for k in range(1, 5))
            diag = sbl("diag", [P, P])
            col_total = sbl("col_total", [P, C])
            onec = sbl("onec", [P, C])
            pcnt = [psl(f"cnt{k}") for k in range(2)]
            pthr, pcum, ptot = (psl(n) for n in ("thr", "cum", "tot"))
            s_in, s_zero, s_zd, s_pool, s_clear, s_v, s_oh, s_mm = seml(
                "in", "zero", "zd", "pool", "clear", "v", "oh", "mm")
            s_diag, s_thr, s_cnt, s_cum, s_deg, s_sqrt = seml("diag", "thr", "cnt", "cum", "deg", "sqrt")
            with nc.Block() as block:
                @block.sync
                def _(e):
                    e.dma_start(dstw[:, :], a["dst"]).then_inc(s_in, 16)
                    e.dma_start(srci[:, :], a["src"]).then_inc(s_in, 16)
                    e.dma_start(x[:, :, :], a["x"]).then_inc(s_in, 16)
                    e.wait_ge(s_zero, 1)
                    for t in corr:
                        e.dma_start(t.rearrange("(p c) f -> p (c f)", p=P), zero[:, 0:C * D]).then_inc(s_zd, 16)
                    st = state3.rearrange("(p c) f -> p (c f)", p=P)
                    for k in range(C // 7):
                        e.dma_start(st[:, k * 7 * S3:(k + 1) * 7 * S3], zero[:, :]).then_inc(s_zd, 16)
                    e.wait_ge(s_zd, 16 * (3 + C // 7))
                    e.wait_ge(s_in, 48)

                @block.gpsimd
                def _(e):
                    ch = Chain(e, s_pool)
                    ch.do(e.iota(iota_i[:, :], pattern=[[1, P]], base=0, channel_multiplier=0))
                    ch.do(e.iota(node_i[:, :], pattern=[[P, C]], base=0, channel_multiplier=1))
                    ch.to(e.memset(ones[:, :], 1.0))
                    ch.do(e.affine_select(out=ident[:, :], in_=ones[:, :], compare_op=ALU.is_equal, fill=0.0,
                                          base=0, pattern=[[-1, P]], channel_multiplier=1))
                    ch.do(e.affine_select(out=tri[:, :], in_=ones[:, :], compare_op=ALU.is_ge, fill=0.0,
                                          base=0, pattern=[[1, P]], channel_multiplier=-1))

                @block.vector
                def _(e):
                    e.memset(zero[:, :], 0.0).then_inc(s_zero, 1)
                    ch = Chain(e, s_v)
                    for t in pcnt:
                        ch.do(e.memset(t[:, 0:C], 0.0))
                    ch.tell(s_clear)
                    ch.do(e.memset(onec[:, :], 1.0))
                    ch.do(e.memset(eps[:, :], EPS))
                    e.wait_ge(s_pool, 5)
                    ch.do(e.tensor_copy(iota_f[:, :], iota_i[:, :]))
                    ch.do(e.tensor_copy(iota_b[:, :], iota_i[:, :]))
                    ch.do(e.tensor_copy(node_f[:, :], node_i[:, :]))
                    e.wait_ge(s_in, 48)
                    ch.do(e.tensor_copy(dstf[:, :], dstw[:, :]))
                    for ids, lo, hi in ((dstw[:, 1:L + 1], dst_lo, dst_hi), (srci[:, :], src_lo, src_hi)):
                        ch.to(e.tensor_scalar(ti[:, :], ids, 127, None, ALU.bitwise_and))
                        ch.to(e.tensor_copy(lo[:, :], ti[:, :]))
                        ch.to(e.tensor_scalar(ti[:, :], ids, 7, None, ALU.arith_shift_right))
                        ch.to(e.tensor_copy(hi[:, :], ti[:, :]))
                    ch.do(e.tensor_tensor(same[:, 1:L], dstf[:, 2:L + 1], dstf[:, 1:L], ALU.is_equal))
                    ch.do(e.memset(same[:, 0:1], 0.0))
                    ch.sync()
                    ch.do(e.tensor_scalar(apart[:, :], same[:, :], BIG, -BIG, ALU.mult, ALU.add))
                    ch.to(e.tensor_tensor(nxt[:, :], dstf[:, 2:L + 2], dstf[:, 1:L + 1], ALU.is_equal))
                    ch.to(e.tensor_scalar(nxt[:, :], nxt[:, :], float(SKIP), None, ALU.mult))
                    ch.to(e.tensor_tensor(nxt[:, :], nxt[:, :], dstf[:, 1:L + 1], ALU.add))
                    ch.do(e.tensor_copy(end_to[:, :], nxt[:, :]))
                    ch.do(e.tensor_scalar(real[:, :], node_f[:, :], float(N), None, ALU.is_lt))
                    ch.do(e.tensor_tensor(f1[:, :], dstf[:, 1:2], dstf[:, L:L + 1], ALU.is_equal))
                    ch.do(e.tensor_tensor(f2[:, :], dstf[:, 0:1], dstf[:, 1:2], ALU.is_equal))
                    ch.do(e.tensor_tensor(f3[:, :], dstf[:, L:L + 1], dstf[:, L + 1:L + 2], ALU.is_equal))
                    ch.sync()
                    ch.to(e.tensor_tensor(f4[:, :], f1[:, :], f2[:, :], ALU.mult))
                    ch.do(e.tensor_scalar(diag[:, :], ident[:, :], f4[:, 0:1], None, ALU.mult))
                    ch.tell(s_diag)
                    ch.to(e.tensor_tensor(f1[:, :], f1[:, :], f3[:, :], ALU.mult))
                    ch.to(e.tensor_scalar(f1[:, :], f1[:, :], -1.0, 1.0, ALU.mult, ALU.add))
                    ch.to(e.tensor_tensor(f2[:, :], f2[:, :], f1[:, :], ALU.mult))
                    ch.to(e.tensor_scalar(f2[:, :], f2[:, :], -float(SKIP), float(SKIP), ALU.mult, ALU.add))
                    ch.to(e.tensor_tensor(f2[:, :], f2[:, :], dstf[:, 1:2], ALU.add))
                    ch.do(e.tensor_copy(carry_to[:, :], f2[:, :]))
                    ch.do(e.tensor_copy(first_node[:, :], dstf[:, 1:2]))
                    with e.Fori(0, NB // 2) as i:
                        for b in range(2):
                            e.wait_ge(s_mm, i * 2 + (b + 1))
                            cols = bass.ds(i * (2 * J) + b * J, J)
                            for k, lohi in enumerate(((dst_lo, dst_hi), (src_lo, src_hi))):
                                for dig, at, w in ((lohi[0], 0, P), (lohi[1], P, C)):
                                    e.tensor_tensor(
                                        digits[b][:, k, :, at:at + w],
                                        iota_b[:, None, 0:w].to_broadcast([P, J, w]),
                                        dig[:, cols][:, :, None].to_broadcast([P, J, w]),
                                        ALU.is_equal).then_inc(s_oh, 1)
                    e.wait_ge(s_cnt, 1)
                    ch.do(e.tensor_copy(cnt_d[:, :], pcnt[0][:, 0:C]))
                    ch.do(e.tensor_copy(cnt_s[:, :], pcnt[1][:, 0:C]))
                    ch.tell(s_deg)
                    ch.do(e.tensor_scalar(v1[:, :], cnt_d[:, :], 1.0, None, ALU.add))
                    ch.to(e.tensor_tensor(v2[:, :], cnt_d[:, :], cnt_s[:, :], ALU.add))
                    ch.do(e.tensor_scalar(v2[:, :], v2[:, :], 1e-5, None, ALU.max))
                    ch.do(e.tensor_scalar(full[:, :], cnt_d[:, :], 0.5, None, ALU.is_ge))
                    ch.tell(s_deg)
                    e.wait_ge(s_thr, 1)
                    ch.do(e.tensor_copy(through[:, :], pthr[:, 0:P]))
                    e.wait_ge(s_sqrt, 2)
                    ch.do(e.reciprocal(dinv[:, :], dinv[:, :]))
                    ch.do(e.reciprocal(dis[:, :], dis[:, :]))
                    e.wait_ge(s_cum, 1)
                    ch.to(e.tensor_copy(col_total[:, :], ptot[:, 0:C]))
                    ch.to(e.tensor_tensor_scan(v1[:, :], onec[:, :], col_total[:, :], 0.0, ALU.mult, ALU.add))
                    ch.to(e.tensor_tensor(v1[:, :], v1[:, :], col_total[:, :], ALU.subtract))
                    ch.to(e.tensor_tensor(v1[:, :], v1[:, :], pcum[:, 0:C], ALU.add))
                    ch.to(e.tensor_scalar(v1[:, :], v1[:, :], -1.0, 0.0, ALU.add, ALU.max))
                    ch.to(e.tensor_copy(last_edge[:, :], v1[:, :]))

                @block.tensor
                def _(e):
                    e.wait_ge(s_pool, 5)
                    e.wait_ge(s_clear, 1)
                    e.sem_inc(s_mm, 2)
                    with e.Fori(0, NB // 2) as i:
                        for b in range(2):
                            e.wait_ge(s_oh, i * 8 + (4 * b + 4))
                            for k in range(2):
                                for j in range(J):
                                    mm = e.matmul(pcnt[k][:, 0:C], digits[b][:, k, j, 0:P],
                                                  digits[b][:, k, j, P:P + C],
                                                  start=False, stop=False, skip_group_check=True)
                            mm.then_inc(s_mm, 1)
                    e.wait_ge(s_mm, NB + 2)
                    e.sem_inc(s_cnt, 1)
                    e.wait_ge(s_diag, 1)
                    e.matmul(pthr[:, 0:P], ones[:, :], diag[:, :], start=True, stop=True).then_inc(s_thr, 1)
                    e.wait_ge(s_deg, 1)
                    e.matmul(pcum[:, 0:C], tri[:, :], cnt_d[:, :], start=True, stop=True)
                    e.matmul(ptot[:, 0:C], ones[:, :], cnt_d[:, :], start=True, stop=True).then_inc(s_cum, 1)

                @block.scalar
                def _(e):
                    e.wait_ge(s_deg, 2)
                    e.activation(dinv[:, :], v1[:, :], ACT.Sqrt).then_inc(s_sqrt, 1)
                    e.activation(dis[:, :], v2[:, :], ACT.Sqrt).then_inc(s_sqrt, 1)

        def norm_and_table(k):
            c, sbl, psl, seml = stage(f"norm{k}")
            with c:
                row = sbl("row", [P, C, T2]) if k == 2 else tmp if k == 0 else h
                s_v, s_var, s_std, s_row, s_tab = seml("v", "var", "std", "row", "tab")
                with nc.Block() as block:
                    @block.vector
                    def _(e):
                        ch = Chain(e, s_v)
                        ch.to(e.tensor_reduce(v1[:, :], x[:, :, :], AX.X, ALU.add))
                        ch.to(e.tensor_scalar(v1[:, :], v1[:, :], 1.0 / D, None, ALU.mult))
                        ch.to(e.tensor_tensor(tmp[:, :, :], x[:, :, :], bc_f(v1), ALU.subtract))
                        ch.to(e.tensor_tensor(h[:, :, :], tmp[:, :, :], tmp[:, :, :], ALU.mult))
                        ch.to(e.tensor_reduce(v2[:, :], h[:, :, :], AX.X, ALU.add))
                        ch.tell(s_var)
                        e.wait_ge(s_std, 1)
                        ch.to(e.reciprocal(v1[:, :], v1[:, :]))
                        ch.to(e.tensor_tensor(tmp[:, :, :], tmp[:, :, :], bc_f(v1), ALU.mult))
                        ch.to(e.tensor_scalar(h[:, :, :], tmp[:, :, :], 0.0, None, ALU.max))
                        if k == 0:
                            ch.do(e.tensor_tensor(row[:, :, :], h[:, :, :], bc_f(dinv), ALU.mult))
                        if k == 2:
                            ch.do(e.tensor_copy(row[:, :, 0:D], h[:, :, :]))
                            ch.do(e.tensor_copy(row[:, :, D:D + 1], dis[:, :, None]))
                            ch.do(e.memset(row[:, :, D + 1:T2], 1.0))
                        ch.tell(s_row)

                    @block.scalar
                    def _(e):
                        e.wait_ge(s_var, 1)
                        e.activation(v1[:, :], v2[:, :], ACT.Sqrt, bias=eps[:, 0:1], scale=1.0 / D).then_inc(s_std, 1)

                    @block.sync
                    def _(e):
                        e.wait_ge(s_row, 1)
                        e.dma_start(by_node(tab[k]), row[:, :, :]).then_inc(s_tab, 16)
                        e.wait_ge(s_tab, 16)

        s_turns = sem("turns")

        def turn_wait(e, s, value):
            e.wait_ge(s, value)
            e.sem_inc(s_turns, 1)

        def indices(idx, b):
            return bass.IndirectOffsetOnAxis(ap=idx[:, b:b + 1], axis=0)

        def scan_block(e, ch, cols, msg, run, before):
            for f in range(D):
                ch.do(e.tensor_tensor_scan(run[:, :, f], same[:, cols], msg[:, :, f], before[:, J - 1, f:f + 1],
                                           ALU.mult, ALU.add))

        def node_sums(k, last):
            c, sbl, psl, seml = stage(f"sums{k}")
            with c:
                stT = sbl("stT", [D, P])
                cT = sbl("cT", [D, P])
                shifted = sbl("shifted", [D, P])
                carry = sbl("carry", [P, D])
                more = sbl("more", [P, C, D])
                pa, pb = psl("a"), psl("b")
                s_v, s_t, s_sh, s_back, s_carry, s_cd, s_g, s_more = seml(
                    "v", "t", "sh", "back", "carry", "cd", "g", "more")
                with nc.Block() as block:
                    @block.tensor
                    def _(e):
                        e.transpose(pa[0:D, 0:P], last, ident[:, :]).then_inc(s_t, 1)
                        e.wait_ge(s_sh, 1)
                        e.transpose(pb[:, 0:D], shifted[:, :], ident[0:D, 0:D]).then_inc(s_back, 1)

                    @block.vector
                    def _(e):
                        ch = Chain(e, s_v)
                        ch.do(e.memset(shifted[:, 0:1], 0.0))
                        e.wait_ge(s_t, 1)
                        ch.to(e.tensor_copy(stT[:, :], pa[0:D, 0:P]))
                        ch.to(e.tensor_tensor_scan(cT[:, :], through[0:D, :], stT[:, :], 0.0, ALU.mult, ALU.add))
                        ch.do(e.tensor_copy(shifted[:, 1:P], cT[:, 0:P - 1]))
                        ch.tell(s_sh)
                        e.wait_ge(s_back, 1)
                        ch.do(e.tensor_copy(carry[:, :], pb[:, 0:D]))
                        ch.tell(s_carry)
                        e.wait_ge(s_g, 16 * C)
                        ch.to(e.tensor_tensor(agg[:, :, :], agg[:, :, :], bc_f(full), ALU.mult))
                        e.wait_ge(s_more, 16)
                        ch.to(e.tensor_tensor(agg[:, :, :], agg[:, :, :], more[:, :, :], ALU.add))

                    @block.gpsimd
                    def _(e):
                        e.wait_ge(s_carry, 1)
                        e.indirect_dma_start(out=corr[k], out_offset=indices(carry_to, 0), in_=carry[:, :],
                                             in_offset=None, bounds_check=NP - 1, oob_is_err=False).then_inc(s_cd, 16)
                        for q in range(C):
                            e.indirect_dma_start(out=agg[:, q, :], out_offset=None, in_=runs[k],
                                                 in_offset=indices(last_edge, q)).then_inc(s_g, 16)

                    @block.sync
                    def _(e):
                        e.wait_ge(s_cd, 16)
                        e.dma_start(more[:, :, :], by_node(corr[k])).then_inc(s_more, 16)

        def block_cols(i, b, size=J):
            return bass.ds(i * (2 * size) + b * size, size)

        norm_and_table(0)
        c, sbl, psl, seml = stage("gcn")
        with c:
            idx = [sbl(f"idx{b}", [P, J], I32) for b in range(2)]
            got = [sbl(f"got{b}", [P, J, D]) for b in range(2)]
            run = [sbl(f"run{b}", [P, J, D]) for b in range(2)]
            s_v, = seml("v")
            s_idx, s_got, s_run, s_st, s_kept = (seml(f"{n}0", f"{n}1") for n in ("idx", "got", "run", "st", "kept"))
            src_blk = a["src"]
            run_rows = runs[0].rearrange("(p l) f -> p l f", p=P)
            with nc.Block() as block:
                @block.sync
                def _(e):
                    for b in range(2):
                        e.dma_start(idx[b][:, :], src_blk[:, b * J:(b + 1) * J]).then_inc(s_idx[b], 16)
                    for b in range(2):
                        e.sem_inc(s_kept[b], 1)
                    with e.Fori(0, NB // 2 - 1) as i:
                        for b in range(2):
                            e.wait_ge(s_run[b], i + 1)
                            e.dma_start(run_rows[:, block_cols(i, b), :], run[b][:, :, :]).then_inc(s_st[b], 16)
                            e.dma_start(idx[b][:, :], src_blk[:, block_cols(i + 1, b)]).then_inc(s_idx[b], 16)
                            e.wait_ge(s_st[b], i * 16 + 16)
                            e.sem_inc(s_kept[b], 1)
                    for b in range(2):
                        e.wait_ge(s_run[b], NB // 2)
                        at = L - (2 - b) * J
                        e.dma_start(run_rows[:, at:at + J, :], run[b][:, :, :]).then_inc(s_st[b], 16)
                    for b in range(2):
                        e.wait_ge(s_st[b], 16 * (NB // 2))

                @block.gpsimd
                def _(e):
                    with e.Fori(0, NB // 2) as i:
                        for b in range(2):
                            turn_wait(e, s_idx[b], i * 16 + 16)
                            for j in range(J):
                                e.indirect_dma_start(out=got[b][:, j, :], out_offset=None, in_=tab[0],
                                                     in_offset=indices(idx[b], j)).then_inc(s_got[b], 16)

                @block.vector
                def _(e):
                    ch = Chain(e, s_v)
                    ch.to(e.memset(run[1][:, J - 1, :], 0.0))
                    with e.Fori(0, NB // 2) as i:
                        ch.loop(i, 2 * D)
                        for b in range(2):
                            e.wait_ge(s_got[b], i * (16 * J) + 16 * J)
                            e.wait_ge(s_kept[b], i + 1)
                            scan_block(e, ch, block_cols(i, b), got[b], run[b], run[1 - b])
                            ch.tell(s_run[b])
                    ch.end(NB // 2)
            node_sums(0, run[1][:, J - 1, :])

        c, sbl, psl, seml = stage("gcn_nodes")
        with c:
            G = 7
            Wg, W1, b1 = sbl("Wg", [D, 48]), sbl("W1", [48, 32]), sbl("b1", [32, 1])
            W2 = sbl("W2", [33, D])
            part = [sbl(f"part{b}", [P, G, D]) for b in range(2)]
            aT, fT, uT = sbl("aT", [D, G * P]), sbl("fT", [48, G * P]), sbl("uT", [33, G * P])
            pt, pf, pu = ([psl(f"{n}{q}") for q in range(2)] for n in "tfu")
            po = psl("o")
            s_w, s_v, s_part, s_t, s_at, s_f, s_ft, s_u, s_ut, s_o, s_free = seml(
                "w", "v", "part", "t", "at", "f", "ft", "u", "ut", "o", "free")
            split = ((0, 4), (4, 7))
            with nc.Block() as block:
                @block.sync
                def _(e):
                    for t, n in ((Wg[:, :], "L0_gnn_W_gcn"), (W1[:, :], "L0_gnn_W1"),
                                 (b1[:, :], "L0_gnn_b1"), (W2[0:32, :], "L0_gnn_W2"), (W2[32:33, :], "L0_gnn_b2")):
                        e.dma_start(t, a[n]).then_inc(s_w, 16)

                @block.vector
                def _(e):
                    ch = Chain(e, s_v)
                    ch.do(e.memset(uT[32:33, :], 1.0))
                    ch.to(e.tensor_tensor(tmp[:, :, :], h[:, :, :], bc_f(dinv), ALU.mult))
                    ch.to(e.tensor_tensor(agg[:, :, :], agg[:, :, :], tmp[:, :, :], ALU.add))
                    ch.do(e.tensor_tensor(agg[:, :, :], agg[:, :, :], bc_f(dinv), ALU.mult))
                    ch.to(e.tensor_tensor(x[:, :, :], x[:, :, :], h[:, :, :], ALU.add))
                    with e.Fori(0, C // G) as i:
                        ch.loop(i, 6)
                        cols = bass.ds(i * G, G)
                        ch.do(e.tensor_copy(part[0][:, :, :], agg[:, cols, :]))
                        ch.tell(s_part)
                        for q, (lo, hi) in enumerate(split):
                            e.wait_ge(s_t, i * 2 + (q + 1))
                            ch.do(e.tensor_copy(aT[:, lo * P:hi * P], pt[q][0:D, 0:(hi - lo) * P]))
                            ch.tell(s_at)
                        for q, (lo, hi) in enumerate(split):
                            e.wait_ge(s_f, i * 2 + (q + 1))
                            ch.do(e.tensor_copy(fT[:, lo * P:hi * P], pf[q][0:48, 0:(hi - lo) * P]))
                            ch.tell(s_ft)
                        e.wait_ge(s_o, i + 1)
                        ch.to(e.tensor_tensor(x[:, cols, :], x[:, cols, :],
                                              po[:, 0:G * D].rearrange("p (g f) -> p g f", f=D), ALU.add))
                    ch.end(C // G)

                @block.tensor
                def _(e):
                    e.wait_ge(s_w, 80)
                    with e.Fori(0, C // G) as i:
                        turn_wait(e, s_part, i + 1)
                        for q, (lo, hi) in enumerate(split):
                            for g in range(lo, hi):
                                mm = e.transpose(pt[q][0:D, (g - lo) * P:(g - lo + 1) * P], part[0][:, g, :], ident[:, :])
                            mm.then_inc(s_t, 1)
                        for q, (lo, hi) in enumerate(split):
                            turn_wait(e, s_at, i * 2 + (q + 1))
                            e.matmul(pf[q][0:48, 0:(hi - lo) * P], Wg[:, :], aT[:, lo * P:hi * P],
                                     start=True, stop=True).then_inc(s_f, 1)
                        for q, (lo, hi) in enumerate(split):
                            turn_wait(e, s_ft, i * 2 + (q + 1))
                            e.matmul(pu[q][0:32, 0:(hi - lo) * P], W1[:, :], fT[:, lo * P:hi * P],
                                     start=True, stop=True).then_inc(s_u, 1)
                        turn_wait(e, s_ut, i * 2 + 2)
                        for g in range(G):
                            mm = e.matmul(po[:, g * D:(g + 1) * D], uT[:, g * P:(g + 1) * P], W2[:, :],
                                          start=True, stop=True)
                        mm.then_inc(s_o, 1)

                @block.scalar
                def _(e):
                    e.wait_ge(s_w, 80)
                    with e.Fori(0, C // G) as i:
                        for q, (lo, hi) in enumerate(split):
                            e.wait_ge(s_u, i * 2 + (q + 1))
                            e.activation(uT[0:32, lo * P:hi * P], pu[q][0:32, 0:(hi - lo) * P], ACT.Relu,
                                         bias=b1[:, 0:1]).then_inc(s_ut, 1)

        renew_semaphores()
        norm_and_table(1)
        c, sbl, psl, seml = stage("nnconv")
        H1 = 64
        QT = 8
        WT = J * P // QT
        with c:
            W1, W2 = sbl("W1", [7, H1]), sbl("W2", [H1 + 1, 256])
            idx = [sbl(f"idx{b}", [P, J], I32) for b in range(2)]
            got = [sbl(f"got{b}", [P, J, D]) for b in range(2)]
            ef = [sbl(f"ef{b}", [7, J, P]) for b in range(2)]
            tT = [sbl(f"tT{b}", [H1 + 1, J * P]) for b in range(2)]
            prod = [sbl(f"prod{q}", [P, 2, D, D]) for q in range(2)]
            msg = [sbl(f"msg{b}", [P, J, D]) for b in range(2)]
            run = [sbl(f"run{b}", [P, J, D]) for b in range(2)]
            pt = [psl(f"t{q}") for q in range(2)]
            pw = [psl(f"w{q}") for q in range(2)]
            s_v, s_w, s_one, s_t, s_relu, s_edge, s_msg = seml("v", "w", "one", "t", "relu", "edge", "msg")
            s_idx, s_ef, s_got, s_run, s_st, s_kept = (seml(f"{n}0", f"{n}1") for n in ("idx", "ef", "got", "run", "st", "kept"))
            run_rows = runs[1].rearrange("(p l) f -> p l f", p=P)
            JJ = J // 2
            with nc.Block() as block:
                @block.sync
                def _(e):
                    for t, n in ((W1[0:6, :], "L1_gnn_W1"), (W1[6:7, :], "L1_gnn_b1"),
                                 (W2[0:H1, :], "L1_gnn_W2"), (W2[H1:H1 + 1, :], "L1_gnn_b2")):
                        e.dma_start(t, a[n]).then_inc(s_w, 16)
                    e.wait_ge(s_one, 1)

                    def load(b, cols):
                        e.dma_start(idx[b][:, :], a["src"][:, cols]).then_inc(s_idx[b], 16)
                        e.dma_start(ef[b][0:6, :, :], a["ef6"][:, cols, :]).then_inc(s_ef[b], 16)

                    for b in range(2):
                        load(b, slice(b * J, (b + 1) * J))
                    for b in range(2):
                        e.sem_inc(s_kept[b], 1)
                    with e.Fori(0, NB // 2 - 1) as i:
                        for b in range(2):
                            e.wait_ge(s_run[b], i + 1)
                            e.dma_start(run_rows[:, block_cols(i, b), :], run[b][:, :, :]).then_inc(s_st[b], 16)
                            load(b, block_cols(i + 1, b))
                            e.wait_ge(s_st[b], i * 16 + 16)
                            e.sem_inc(s_kept[b], 1)
                    for b in range(2):
                        e.wait_ge(s_run[b], NB // 2)
                        at = L - (2 - b) * J
                        e.dma_start(run_rows[:, at:at + J, :], run[b][:, :, :]).then_inc(s_st[b], 16)
                    for b in range(2):
                        e.wait_ge(s_st[b], 16 * (NB // 2))

                @block.gpsimd
                def _(e):
                    with e.Fori(0, NB // 2) as i:
                        for b in range(2):
                            turn_wait(e, s_idx[b], i * 16 + 16)
                            for j in range(J):
                                e.indirect_dma_start(out=got[b][:, j, :], out_offset=None, in_=tab[1],
                                                     in_offset=indices(idx[b], j)).then_inc(s_got[b], 16)

                @block.tensor
                def _(e):
                    e.wait_ge(s_w, 64)
                    with e.Fori(0, NB // 2) as i:
                        for b in range(2):
                            turn_wait(e, s_ef[b], i * 16 + 16)
                            for q in range(QT):
                                turn_wait(e, s_relu, i * (2 * QT) + (b * QT + q + 1))
                                e.matmul(pt[q % 2][0:H1, 0:WT], W1[:, :],
                                         ef[b].rearrange("k j p -> k (j p)")[:, q * WT:(q + 1) * WT],
                                         start=True, stop=True).then_inc(s_t, 1)
                            turn_wait(e, s_relu, i * (2 * QT) + (b * QT + QT + 2))
                            for g in range(JJ):
                                turn_wait(e, s_msg, i * (2 * JJ) + (b * JJ + g + 1))
                                for j in range(2):
                                    at = (2 * g + j) * P
                                    mm = e.matmul(pw[(b * JJ + g) % 2][:, j * 256:(j + 1) * 256], tT[b][:, at:at + P],
                                                  W2[:, :], start=True, stop=True)
                                mm.then_inc(s_edge, 1)

                @block.scalar
                def _(e):
                    e.wait_ge(s_one, 1)
                    e.sem_inc(s_relu, 2)
                    with e.Fori(0, NB // 2) as i:
                        for b in range(2):
                            e.wait_ge(s_kept[b], i + 1)
                            for q in range(QT):
                                e.wait_ge(s_t, i * (2 * QT) + (b * QT + q + 1))
                                e.activation(tT[b][0:H1, q * WT:(q + 1) * WT], pt[q % 2][0:H1, 0:WT],
                                             ACT.Relu).then_inc(s_relu, 1)

                @block.vector
                def _(e):
                    ch = Chain(e, s_v)
                    for b in range(2):
                        ch.do(e.memset(ef[b][:, :, :], 1.0))
                        ch.do(e.memset(tT[b][H1:H1 + 1, :], 1.0))
                    ch.do(e.memset(run[1][:, J - 1, :], 0.0))
                    ch.sync()
                    e.sem_inc(s_one, 1)
                    e.sem_inc(s_msg, 2)
                    with e.Fori(0, NB // 2) as i:
                        ch.loop(i, 2 * (D + JJ))
                        for b in range(2):
                            e.wait_ge(s_got[b], i * (16 * J) + 16 * J)
                            e.wait_ge(s_kept[b], i + 1)
                            for g in range(JJ):
                                e.wait_ge(s_edge, i * (2 * JJ) + (b * JJ + g + 1))
                                q = (b * JJ + g) % 2
                                e.tensor_tensor(prod[q][:, :, :, :],
                                                pw[q][:, :].rearrange("p (j i o) -> p j i o", j=2, i=D),
                                                got[b][:, 2 * g:2 * g + 2, :][:, :, :, None].to_broadcast([P, 2, D, D]),
                                                ALU.mult).then_inc(s_msg, 1)
                                e.wait_ge(s_msg, i * (2 * JJ) + (b * JJ + g + 3))
                                ch.do(e.tensor_reduce(msg[b][:, 2 * g:2 * g + 2, :],
                                                      prod[q][:, :, :, :].rearrange("p j i o -> p j o i"), AX.X, ALU.add))
                            ch.sync()
                            scan_block(e, ch, block_cols(i, b), msg[b], run[b], run[1 - b])
                            ch.tell(s_run[b])
                    ch.end(NB // 2)
            node_sums(1, run[1][:, J - 1, :])

        c, sbl, psl, seml = stage("bn")
        with c:
            bias, gamma, beta = (sbl(n, [P, D]) for n in ("bias", "gamma", "beta"))
            part, mean, std = (sbl(n, [P, D]) for n in ("part", "mean", "std"))
            pm, pv = psl("m"), psl("v")
            s_w, s_v, s_p, s_m, s_std = seml("w", "v", "p", "m", "std")

            def bc_n(t):
                return t[:, None, :].to_broadcast([P, C, D])

            with nc.Block() as block:
                @block.sync
                def _(e):
                    for t, n in ((bias, "bias"), (gamma, "gamma"), (beta, "beta")):
                        e.dma_start(t[:, :], a[f"L1_gnn_{n}"].to_broadcast([P, D])).then_inc(s_w, 16)

                @block.tensor
                def _(e):
                    for k, t in enumerate((pm, pv)):
                        e.wait_ge(s_p, k + 1)
                        e.matmul(t[:, 0:D], ones[:, :], part[:, :], start=True, stop=True).then_inc(s_m, 1)

                @block.scalar
                def _(e):
                    e.wait_ge(s_m, 2)
                    e.activation(std[:, :], pv[:, 0:D], ACT.Sqrt, bias=eps[:, 0:1], scale=1.0 / N).then_inc(s_std, 1)

                @block.vector
                def _(e):
                    ch = Chain(e, s_v)
                    ch.to(e.tensor_scalar(v1[:, :], cnt_d[:, :], 1.0, None, ALU.max))
                    ch.to(e.reciprocal(v1[:, :], v1[:, :]))
                    ch.to(e.tensor_tensor(agg[:, :, :], agg[:, :, :], bc_f(v1), ALU.mult))
                    e.wait_ge(s_w, 48)
                    ch.to(e.tensor_tensor(agg[:, :, :], agg[:, :, :], bc_n(bias), ALU.add))
                    ch.to(e.tensor_scalar(agg[:, :, :], agg[:, :, :], 0.0, None, ALU.max))
                    ch.to(e.tensor_tensor(tmp[:, :, :], agg[:, :, :], bc_f(real), ALU.mult))
                    ch.do(e.tensor_reduce(part[:, :], tmp[:, :, :].rearrange("p c f -> p f c"), AX.X, ALU.add))
                    ch.tell(s_p)
                    e.wait_ge(s_m, 1)
                    ch.to(e.tensor_scalar(mean[:, :], pm[:, 0:D], 1.0 / N, None, ALU.mult))
                    ch.to(e.tensor_tensor(agg[:, :, :], agg[:, :, :], bc_n(mean), ALU.subtract))
                    ch.to(e.tensor_tensor(tmp[:, :, :], agg[:, :, :], bc_f(real), ALU.mult))
                    ch.to(e.tensor_tensor(tmp[:, :, :], tmp[:, :, :], tmp[:, :, :], ALU.mult))
                    ch.do(e.tensor_reduce(part[:, :], tmp[:, :, :].rearrange("p c f -> p f c"), AX.X, ALU.add))
                    ch.tell(s_p)
                    e.wait_ge(s_std, 1)
                    ch.to(e.reciprocal(std[:, :], std[:, :]))
                    ch.to(e.tensor_tensor(std[:, :], std[:, :], gamma[:, :], ALU.mult))
                    ch.to(e.tensor_tensor(agg[:, :, :], agg[:, :, :], bc_n(std), ALU.mult))
                    ch.to(e.tensor_tensor(agg[:, :, :], agg[:, :, :], bc_n(beta), ALU.add))
                    ch.to(e.tensor_tensor(x[:, :, :], x[:, :, :], agg[:, :, :], ALU.add))

        renew_semaphores()
        norm_and_table(2)
        c, sbl, psl, seml = stage("sheaf")
        H2 = 64
        JH = J // 2
        with c:
            Wz, W2 = sbl("Wz", [2 * T2, 2 * H2]), sbl("W2", [2 * H2, 2 * D])
            b2 = sbl("b2", [1, JH, 2, D])
            idx = [sbl(f"idx{b}", [P, 2, J], I32) for b in range(2)]
            got = [sbl(f"got{b}", [P, J, 2, T2]) for b in range(2)]
            gT = [sbl(f"gT{q}", [2 * T2, 2 * P]) for q in range(2)]
            zT = [sbl(f"zT{q}", [2 * H2, 2 * P]) for q in range(2)]
            vec = [sbl(f"vec{q}", [P, JH, 2, D]) for q in range(2)]
            prod = sbl("prod", [P, JH, 7, D])
            dots = sbl("dots", [P, JH, 7])
            cc = sbl("cc", [P, JH, 2])
            first = sbl("first", [P, JH, 2])
            second = sbl("second", [P, JH, 2])
            term = sbl("term", [P, JH, 2, D])
            msg = sbl("msg", [P, J, 2, D])
            hot_lo = [sbl(f"hot_lo{q}", [P, P]) for q in range(2)]
            hot_hi = sbl("hot_hi", [P, JH, C])
            wide = [sbl(f"wide{q}", [P, C, D]) for q in range(2)]
            run = [sbl(f"run{b}", [P, J, D]) for b in range(2)]
            from_src = sbl("from_src", [P, C, D])
            banks = ExitStack()
            pg, pz, pv, pacc = ([ps(f"sheaf_{n}{q}", [P, 512], banks) for q in range(2)] for n in ("g", "z", "v", "acc"))
            PER_HALF = 20
            HC = 25
            halves = ((0, HC), (HC, C))
            s_v, s_w, s_one, s_gT, s_gTc, s_z, s_zc, s_used, s_vc, s_vfree, s_hot, s_acc = seml(
                "v", "w", "one", "gT", "gTc", "z", "zc", "used", "vc", "vfree", "hot", "acc")
            s_idx, s_got, s_run, s_st, s_kept = (seml(f"{n}0", f"{n}1") for n in ("idx", "got", "run", "st", "kept"))
            run_rows = runs[2].rearrange("(p l) f -> p l f", p=P)
            NG = JH
            with nc.Block() as block:
                @block.sync
                def _(e):
                    e.wait_ge(s_one, 1)
                    w1, w2 = a["L2_W1T"], a["L2_W2T"]
                    s, d, one = slice(0, D), slice(T2, T2 + D), slice(D + 1, D + 2)
                    for t, n in ((Wz[s, 0:H2], w1[0:D, :]), (Wz[d, 0:H2], w1[D:2 * D, :]),
                                 (Wz[d, H2:], w1[0:D, :]), (Wz[s, H2:], w1[D:2 * D, :]),
                                 (Wz[one, 0:H2], a["L2_gnn_b1"]), (Wz[one, H2:], a["L2_gnn_b1"]),
                                 (W2[0:H2, 0:D], w2), (W2[H2:, D:], w2),
                                 (b2.rearrange("k j t f -> k (j t) f"),
                                  a["L2_gnn_b2"][:, None, :].to_broadcast([1, 2 * JH, D]))):
                        e.dma_start(t, n).then_inc(s_w, 16)

                    def load(b, cols, cols_d):
                        e.dma_start(idx[b][:, 0, :], a["src"][:, cols]).then_inc(s_idx[b], 16)
                        e.dma_start(idx[b][:, 1, :], a["dst"][:, cols_d]).then_inc(s_idx[b], 16)

                    for b in range(2):
                        load(b, slice(b * J, (b + 1) * J), slice(1 + b * J, 1 + (b + 1) * J))
                    for b in range(2):
                        e.sem_inc(s_kept[b], 1)
                    with e.Fori(0, NB // 2 - 1) as i:
                        for b in range(2):
                            e.wait_ge(s_run[b], i + 1)
                            e.dma_start(run_rows[:, block_cols(i, b), :], run[b][:, :, :]).then_inc(s_st[b], 16)
                            load(b, block_cols(i + 1, b), bass.ds(i * (2 * J) + ((2 + b) * J + 1), J))
                            e.wait_ge(s_st[b], i * 16 + 16)
                            e.sem_inc(s_kept[b], 1)
                    for b in range(2):
                        e.wait_ge(s_run[b], NB // 2)
                        at = L - (2 - b) * J
                        e.dma_start(run_rows[:, at:at + J, :], run[b][:, :, :]).then_inc(s_st[b], 16)
                    for b in range(2):
                        e.wait_ge(s_st[b], 16 * (NB // 2))

                @block.gpsimd
                def _(e):
                    with e.Fori(0, NB // 2) as i:
                        for b in range(2):
                            turn_wait(e, s_idx[b], i * 32 + 32)
                            for j in range(J):
                                for k in range(2):
                                    e.indirect_dma_start(out=got[b][:, j, k, :], out_offset=None, in_=tab[2],
                                                         in_offset=indices(idx[b][:, k, :], j)).then_inc(s_got[b], 16)

                @block.tensor
                def _(e):
                    e.wait_ge(s_w, 16 * 9)
                    e.wait_ge(s_one, 1)
                    e.sem_inc(s_z, 2)
                    e.sem_inc(s_used, 2)
                    e.sem_inc(s_acc, 2)
                    with e.Fori(0, NB // 2) as i:
                        for b in range(2):
                            turn_wait(e, s_got[b], i * (32 * J) + 32 * J)

                            def turned(g):
                                k = b * NG + g
                                turn_wait(e, s_gTc, i * (2 * NG) + (k + 1))
                                for j in range(2):
                                    mm = e.transpose(pg[k % 2][0:2 * T2, j * P:(j + 1) * P],
                                                     got[b][:, 2 * g + j, :, :].rearrange("p t f -> p (t f)"),
                                                     ident[:, :])
                                mm.then_inc(s_gT, 1)

                            def hidden(g):
                                k = b * NG + g
                                turn_wait(e, s_gTc, i * (2 * NG) + (k + 3))
                                turn_wait(e, s_zc, i * (2 * NG) + (k + 1))
                                e.matmul(pz[k % 2][:, 0:2 * P], Wz[:, :], gT[k % 2][:, :],
                                         start=True, stop=True).then_inc(s_z, 1)

                            def vectors(g):
                                k = b * NG + g
                                turn_wait(e, s_zc, i * (2 * NG) + (k + 3))
                                for j in range(2):
                                    half, col = divmod(2 * g + j, JH)
                                    if col == 0:
                                        turn_wait(e, s_vc, i * 4 + (b * 2 + half + 1))
                                        e.matmul(pv[half][:, 0:JH * 2 * D], ones[0:1, :],
                                                 b2.rearrange("k j t f -> k (j t f)"), start=True, stop=False,
                                                 skip_group_check=True)
                                    mm = e.matmul(pv[half][:, col * 2 * D:(col + 1) * 2 * D],
                                                  zT[k % 2][:, j * P:(j + 1) * P], W2[:, :],
                                                  start=False, stop=False, skip_group_check=True)
                                mm.then_inc(s_used, 1)

                            for g in range(NG + 2):
                                if g < NG:
                                    turned(g)
                                if 0 <= g - 1 < NG:
                                    hidden(g - 1)
                                if 0 <= g - 2:
                                    vectors(g - 2)
                            for j in range(J):
                                q = b * J + j
                                turn_wait(e, s_hot, i * (2 * J) + (q + 2))
                                for k, (lo, hi) in enumerate(halves):
                                    mm = e.matmul(pacc[k][:, 0:(hi - lo) * D], hot_lo[q % 2][:, :],
                                                  wide[q % 2][:, lo:hi, :].rearrange("p c f -> p (c f)"),
                                                  start=False, stop=False, skip_group_check=True)
                                mm.then_inc(s_acc, 1)

                @block.scalar
                def _(e):
                    e.wait_ge(s_one, 1)
                    for s in (s_gTc, s_zc, s_vc):
                        e.sem_inc(s, 2)

                    with e.Fori(0, NB // 2) as i:
                        for b in range(2):
                            def copy_vectors(half):
                                m = b * 2 + half
                                e.wait_ge(s_used, i * (2 * NG) + (b * NG + (JH + 1) // 2 + half * (NG // 2) + 2))
                                e.wait_ge(s_vfree, i * 4 + (m + 1))
                                e.copy(vec[half].rearrange("p j t f -> p (j t f)"),
                                       pv[half][:, 0:JH * 2 * D]).then_inc(s_vc, 1)

                            for g in range(NG + 1):
                                k = b * NG + g
                                if g < NG:
                                    e.wait_ge(s_gT, i * (2 * NG) + (k + 1))
                                    e.wait_ge(s_z, i * (2 * NG) + (k + 1))
                                    e.copy(gT[k % 2][:, :], pg[k % 2][0:2 * T2, 0:2 * P]).then_inc(s_gTc, 1)
                                if g >= 1:
                                    e.wait_ge(s_z, i * (2 * NG) + (k + 2))
                                    e.wait_ge(s_used, i * (2 * NG) + k)
                                    e.activation(zT[(k - 1) % 2][:, :], pz[(k - 1) % 2][:, 0:2 * P],
                                                 ACT.Relu).then_inc(s_zc, 1)
                                if g == NG // 2 + 3:
                                    copy_vectors(0)
                            copy_vectors(1)

                @block.vector
                def _(e):
                    ch = Chain(e, s_v)
                    ch.do(e.memset(Wz[:, :], 0.0))
                    ch.do(e.memset(W2[:, :], 0.0))
                    for t in pacc:
                        ch.do(e.memset(t[:, :], 0.0))
                    ch.do(e.memset(run[1][:, J - 1, :], 0.0))
                    ch.sync()
                    e.sem_inc(s_one, 1)
                    e.sem_inc(s_vfree, 2)
                    e.sem_inc(s_hot, 1)
                    dot_w = [P, JH, 2, D]
                    with e.Fori(0, NB // 2) as i:
                        ch.loop(i, 2 * (2 * PER_HALF + D))
                        for b in range(2):
                            e.wait_ge(s_got[b], i * (32 * J) + 32 * J)
                            for half in range(2):
                                m = b * 2 + half
                                cols = slice(half * JH, (half + 1) * JH)
                                g4 = got[b][:, cols, :, :]
                                xs, xd = g4[:, :, 0, 0:D], g4[:, :, 1, 0:D]
                                V = vec[half]
                                u, w = V[:, :, 0, :], V[:, :, 1, :]
                                out_m = msg[:, cols, :, :]

                                def both(t):
                                    return t[:, :, None, :].to_broadcast(dot_w)

                                def each(t):
                                    return t[:, :, :, None].to_broadcast(dot_w)

                                e.wait_ge(s_vc, i * 4 + (m + 3))
                                ch.do(e.tensor_tensor(prod[:, :, 0:2, :], V[:, :, :, :], V[:, :, :, :], ALU.mult))
                                ch.do(e.tensor_tensor(prod[:, :, 2:4, :], V[:, :, :, :], both(xs), ALU.mult))
                                ch.do(e.tensor_tensor(prod[:, :, 4:6, :], V[:, :, :, :], both(xd), ALU.mult))
                                ch.do(e.tensor_tensor(prod[:, :, 6, :], u, w, ALU.mult))
                                ch.sync()
                                ch.to(e.tensor_reduce(dots[:, :, :], prod[:, :, :, :], AX.X, ALU.add))
                                ch.to(e.tensor_scalar(cc[:, :, :], dots[:, :, 0:2], 1e-24, 0.5, ALU.max, ALU.mult))
                                ch.to(e.reciprocal(cc[:, :, :], cc[:, :, :]))
                                uw = dots[:, :, 6]
                                ch.do(e.tensor_tensor(first[:, :, 0], cc[:, :, 0], dots[:, :, 2], ALU.mult))
                                ch.do(e.tensor_tensor(first[:, :, 1], cc[:, :, 1], dots[:, :, 5], ALU.mult))
                                ch.sync()
                                ch.to(e.tensor_tensor(second[:, :, :], first[:, :, :],
                                                      uw[:, :, None].to_broadcast([P, JH, 2]), ALU.mult))
                                ch.to(e.tensor_tensor(second[:, :, :], dots[:, :, 3:5], second[:, :, :], ALU.subtract))
                                ch.do(e.tensor_tensor(second[:, :, 0], second[:, :, 0], cc[:, :, 1], ALU.mult))
                                ch.do(e.tensor_tensor(second[:, :, 1], second[:, :, 1], cc[:, :, 0], ALU.mult))
                                ch.to(e.tensor_tensor(term[:, :, :, :], each(first), V[:, :, :, :], ALU.mult))
                                ch.to(e.tensor_tensor(out_m, g4[:, :, :, 0:D], term[:, :, :, :], ALU.subtract))
                                ch.do(e.tensor_tensor(term[:, :, 0, :], second[:, :, 0][:, :, None].to_broadcast([P, JH, D]), w, ALU.mult))
                                ch.do(e.tensor_tensor(term[:, :, 1, :], second[:, :, 1][:, :, None].to_broadcast([P, JH, D]), u, ALU.mult))
                                ch.sync()
                                ch.to(e.tensor_tensor(out_m, out_m, term[:, :, :, :], ALU.subtract))
                                e.sem_inc(s_vfree, 1)
                                ch.to(e.tensor_tensor(out_m, out_m, g4[:, :, :, D:D + 1].to_broadcast(dot_w), ALU.mult))
                                e.wait_ge(s_hot, i * (2 * J) + (b * J + half * JH + 1))
                                hi = src_hi[:, bass.ds(i * (2 * J) + (b * J + half * JH), JH)]
                                ch.do(e.tensor_tensor(hot_hi[:, :, :], iota_f[:, None, 0:C].to_broadcast([P, JH, C]),
                                                      hi[:, :, None].to_broadcast([P, JH, C]), ALU.is_equal))
                                ch.sync()
                                for j in range(JH):
                                    q = b * J + half * JH + j
                                    e.wait_ge(s_acc, i * (2 * J) + (q + 1))
                                    lo = src_lo[:, bass.ds(i * (2 * J) + q, 1)]
                                    e.tensor_scalar(hot_lo[q % 2][:, :], iota_f[:, :], lo, None, ALU.is_equal)
                                    e.tensor_tensor(wide[q % 2][:, :, :],
                                                    msg[:, half * JH + j, 1, :][:, None, :].to_broadcast([P, C, D]),
                                                    hot_hi[:, j, :][:, :, None].to_broadcast([P, C, D]),
                                                    ALU.mult).then_inc(s_hot, 1)
                            e.wait_ge(s_kept[b], i + 1)
                            scan_block(e, ch, block_cols(i, b), msg[:, :, 0, :], run[b], run[1 - b])
                            ch.tell(s_run[b])
                    ch.end(NB // 2)
                    e.wait_ge(s_acc, NB * J + 2)
                    for k, (lo, hi) in enumerate(halves):
                        ch.do(e.tensor_copy(from_src[:, lo:hi, :], pacc[k][:, 0:(hi - lo) * D].rearrange("p (c f) -> p c f", f=D)))
                    ch.sync()
            banks.close()
            node_sums(2, run[1][:, J - 1, :])
            s_n, = seml("n")
            with nc.Block() as block:
                @block.vector
                def _(e):
                    ch = Chain(e, s_n)
                    ch.to(e.tensor_tensor(agg[:, :, :], agg[:, :, :], from_src[:, :, :], ALU.add))
                    ch.to(e.tensor_tensor(agg[:, :, :], agg[:, :, :], bc_f(dis), ALU.mult))
                    ch.to(e.tensor_tensor(agg[:, :, :], agg[:, :, :], h[:, :, :], ALU.add))
                    ch.to(e.tensor_scalar(agg[:, :, :], agg[:, :, :], 0.0, None, ALU.max))
                    ch.to(e.tensor_tensor(x[:, :, :], x[:, :, :], agg[:, :, :], ALU.add))

        renew_semaphores()
        norm_and_table(3)
        c, sbl, psl, seml = stage("attn")
        CH = D * D
        OFF = 8
        with c:
            banks = ExitStack()
            S = [sbl(f"S{b}", [P, J3, S3]) for b in range(2)]
            Wc = sb("attn_Wc", [D + 1, 2 * CH], c=banks)
            idx = [sb(f"attn_idx{b}", [P, J3], I32, c=banks) for b in range(2)]
            eidx = [sb(f"attn_eidx{b}", [P, J3], I32, c=banks) for b in range(2)]
            got = [sb(f"attn_got{b}", [P, J3, D], c=banks) for b in range(2)]
            ef = [sb(f"attn_ef{b}", [D + 1, J3, P], c=banks) for b in range(2)]
            T = [sb(f"attn_T{b}", [P, J3, 2 * CH], c=banks) for b in range(2)]
            drop = sb("attn_drop", [P, CH], c=banks)
            scale = sb("attn_scale", [P, CH], c=banks)
            carried = sb("attn_carried", [P, 2 * CH], c=banks)
            pw = [ps(f"attn_w{q}", [P, 512], banks) for q in range(OFF)]
            s_w, s_v, s_one, s_col, s_t, s_e, s_x, s_state = seml("w", "v", "one", "col", "t", "e", "x", "state")
            s_idx, s_ef, s_got, s_sc = (seml(f"{n}0", f"{n}1") for n in ("idx", "ef", "got", "sc"))

            class At:

                def __init__(self, k, i=None):
                    self.k, self.i, self.b = k, i, k % 2

                def of(self, per, more):
                    return self.k * per + more if self.i is None else self.i * (2 * per) + (self.k * per + more)

                def half(self, per, more):
                    return self.k // 2 * per + more if self.i is None else self.i * per + (self.k // 2 * per + more)

                def cols(self):
                    return bass.ds(self.of(J3, 0), J3)

                def col(self, j):
                    return bass.ds(self.of(J3, j), 1)

                def plus(self, d):
                    return At(self.k + d, self.i)

            def blocks(e, step):
                step(At(0))
                step(At(1))
                with e.Fori(0, NB3 // 2 - 2) as i:
                    step(At(2, i))
                    step(At(3, i))
                step(At(NB3 - 2))
                step(At(NB3 - 1))

            with nc.Block() as block:
                @block.sync
                def _(e):
                    for t, n in ((Wc[0:D, 0:CH], "L3_gnn_W_attn"), (Wc[0:D, CH:], "L3_gnn_W_msg"),
                                 (Wc[D:D + 1, 0:CH], "L3_gnn_b_attn"), (Wc[D:D + 1, CH:], "L3_gnn_b_msg")):
                        e.dma_start(t, a[n]).then_inc(s_w, 16)
                    e.wait_ge(s_one, 1)

                    def load(at):
                        e.dma_start(idx[at.b][:, :], a["src"][:, at.cols()]).then_inc(s_idx[at.b], 16)
                        e.dma_start(ef[at.b][0:D, :, :], a["ef16"][:, at.cols(), :]).then_inc(s_ef[at.b], 16)

                    load(At(0))
                    load(At(1))
                    with e.Fori(0, NB3 // 2 - 1) as i:
                        for k in range(2):
                            e.wait_ge(s_t, At(k, i).of(J3, J3 + OFF))
                            load(At(k + 2, i))

                @block.gpsimd
                def _(e):
                    def gather(at):
                        turn_wait(e, s_idx[at.b], at.half(16, 16))
                        for j in range(J3):
                            e.indirect_dma_start(out=got[at.b][:, j, :], out_offset=None, in_=tab[3],
                                                 in_offset=indices(idx[at.b], j)).then_inc(s_got[at.b], 16)

                    def scatter(at):
                        turn_wait(e, s_state, at.of(1, 1))
                        for j in range(J3):
                            e.indirect_dma_start(out=state3, out_offset=indices(eidx[at.b], j),
                                                 in_=S[at.b][:, j, :], in_offset=None, bounds_check=NP - 1,
                                                 oob_is_err=False).then_inc(s_sc[at.b], 16)

                    gather(At(0))
                    gather(At(1))
                    gather(At(2))
                    with e.Fori(0, NB3 // 2 - 2) as i:
                        for k in range(2):
                            gather(At(k + 3, i))
                            scatter(At(k, i))
                    gather(At(NB3 - 1))
                    for k in range(NB3 - 4, NB3):
                        scatter(At(k))
                    for b in range(2):
                        e.wait_ge(s_sc[b], 16 * J3 * (NB3 // 2))

                @block.tensor
                def _(e):
                    e.wait_ge(s_w, 64)
                    with e.Fori(0, NB3 // 2) as i:
                        for b in range(2):
                            turn_wait(e, s_ef[b], i * 16 + 16)
                            for j in range(J3):
                                k = b * J3 + j
                                before = k - OFF if k >= OFF else max(q for q in range(2 * J3) if q % OFF == k) - 2 * J3
                                turn_wait(e, s_t, i * (2 * J3) + (before + 1 + OFF))
                                e.matmul(pw[k % OFF][:, :], ef[b][:, j, :], Wc[:, :], start=True, stop=True).then_inc(s_col, 1)

                @block.scalar
                def _(e):
                    def exps(at):
                        e.wait_ge(s_e, at.of(1, 1))
                        e.activation(S[at.b][:, :, CH:2 * CH], T[at.b][:, :, 0:CH], ACT.Exp).then_inc(s_x, 1)
                        e.activation(scale[:, :], drop[:, :], ACT.Exp).then_inc(s_x, 1)

                    blocks(e, exps)

                @block.vector
                def _(e):
                    ch = Chain(e, s_v)
                    for b in range(2):
                        ch.do(e.memset(ef[b][:, :, :], 1.0))
                    ch.do(e.memset(S[1][:, J3 - 1, 0:CH], -BIG))
                    ch.do(e.memset(S[1][:, J3 - 1, CH:], 0.0))
                    ch.tell(s_one)
                    e.sem_inc(s_t, OFF)

                    def edge(at, j):
                        if j == 0:
                            e.wait_ge(s_got[at.b], at.half(16 * J3, 16 * J3))
                        e.wait_ge(s_col, at.of(J3, j + 1))
                        e.tensor_tensor(T[at.b][:, j, :].rearrange("p (m i o) -> p m i o", m=2, i=D),
                                        pw[(at.b * J3 + j) % OFF][:, :].rearrange("p (m i o) -> p m i o", m=2, i=D),
                                        got[at.b][:, j, :][:, None, :, None].to_broadcast([P, 2, D, D]),
                                        ALU.mult).then_inc(s_t, 1)

                    def sums(at, j):
                        Sb = S[at.b]
                        return ch.do(e.scalar_tensor_tensor(
                            out=Sb[:, j, CH:], in0=carried[:, :] if j == 0 else Sb[:, j - 1, CH:],
                            scalar=same[:, at.col(j)], in1=Sb[:, j, CH:], op0=ALU.mult, op1=ALU.add))

                    def a_block(at):
                        Sb, Tb, So = S[at.b], T[at.b], S[1 - at.b]
                        prev, first, last = at.plus(-1), at.k == 0, at.k == NB3 - 1
                        if at.k == NB3 - 2:
                            ch.end(NB3 // 2 - 2)
                        if at.i is not None and at.k == 2:
                            ch.loop(at.i, 2 * (3 * J3 - 1 + 4 + 2))
                        e.wait_ge(s_t, at.of(J3, J3 + OFF))
                        if at.k >= 2:
                            e.wait_ge(s_sc[at.b], at.half(16 * J3, 0))
                        s_prev = None
                        for j in range(J3):
                            m_now = ch.do(e.scalar_tensor_tensor(
                                out=Sb[:, j, 0:CH], in0=So[:, J3 - 1, 0:CH] if j == 0 else Sb[:, j - 1, 0:CH],
                                scalar=apart[:, at.col(j)], in1=Tb[:, j, 0:CH], op0=ALU.add, op1=ALU.max))
                            if not first:
                                if s_prev:
                                    ch.wait(s_prev)
                                s_prev = sums(prev, j)
                            ch.wait(m_now)
                        if not first:
                            ch.tell(s_state)
                        early = 0 if last else J3 // 2
                        for j in range(J3 - 2, -1, -1):
                            m_now = ch.do(e.scalar_tensor_tensor(
                                out=Sb[:, j, 0:CH], in0=Sb[:, j + 1, 0:CH], scalar=apart[:, at.col(j + 1)],
                                in1=Sb[:, j, 0:CH], op0=ALU.add, op1=ALU.max))
                            if J3 - 2 - j < early:
                                edge(at.plus(1), J3 - 2 - j)
                            ch.wait(m_now)
                        ch.do(e.tensor_copy(eidx[at.b][:, :], end_to[:, at.cols()]))
                        ch.do(e.tensor_tensor(Tb[:, :, 0:CH], Tb[:, :, 0:CH], Sb[:, :, 0:CH], ALU.subtract))
                        ch.to(e.tensor_tensor(drop[:, :], So[:, J3 - 1, 0:CH], Sb[:, 0, 0:CH], ALU.subtract))
                        ch.do(e.tensor_scalar(drop[:, :], drop[:, :], 0.0, None, ALU.min))
                        ch.tell(s_e)
                        if not last:
                            for j in range(early, J3):
                                edge(at.plus(1), j)
                        e.wait_ge(s_x, at.of(2, 2))
                        ch.do(e.tensor_tensor(Sb[:, :, 2 * CH:], Tb[:, :, CH:], Sb[:, :, CH:2 * CH], ALU.mult))
                        ch.do(e.tensor_tensor(carried[:, :].rearrange("p (t c) -> p t c", t=2),
                                              So[:, J3 - 1, CH:].rearrange("p (t c) -> p t c", t=2),
                                              scale[:, None, :].to_broadcast([P, 2, CH]), ALU.mult))
                        ch.sync()

                    for j in range(J3):
                        edge(At(0), j)
                    blocks(e, a_block)
                    for j in range(J3):
                        sums(At(NB3 - 1), j)
                        ch.sync()
                    ch.tell(s_state)
            banks.close()

            TT = sbl("TT", [P, 6, P])
            Mx = sbl("Mx", [P, 2, P])
            ea, eb = sbl("ea", [P, 2, P]), sbl("eb", [P, 2, P])
            apT = sbl("apT", [P, P])
            sh = sbl("sh", [P, 6, P])
            cin = sbl("cin", [P, S3])
            own = sbl("own", [P, S3])
            top = sbl("top", [P, CH])
            e1, e2 = sbl("e1", [P, CH]), sbl("e2", [P, CH])
            last_state = S[1][:, J3 - 1, :]
            pT, pB = psl("turn0"), psl("turn1")
            pC, pD = psl("back0"), psl("back1")
            s_u, s_pt, s_d, s_ex, s_sh, s_pb, s_own, s_mrg, s_put = seml("u", "pt", "d", "ex", "sh", "pb", "own", "mrg", "put")
            with nc.Block() as block:
                @block.tensor
                def _(e):
                    for k in range(6):
                        e.transpose((pT, pB)[k // 4][:, k % 4 * P:(k % 4 + 1) * P],
                                    last_state[:, k * P:(k + 1) * P], ident[:, :]).then_inc(s_pt, 1)
                    e.wait_ge(s_sh, 1)
                    for k in range(6):
                        e.transpose((pC, pD)[k // 4][:, k % 4 * P:(k % 4 + 1) * P], sh[:, k, :], ident[:, :]).then_inc(s_pb, 1)

                @block.gpsimd
                def _(e):
                    e.indirect_dma_start(out=own[:, :], out_offset=None, in_=state3,
                                         in_offset=indices(first_node, 0)).then_inc(s_own, 16)
                    e.wait_ge(s_own, 16)
                    e.wait_ge(s_mrg, 1)
                    e.indirect_dma_start(out=state3, out_offset=indices(carry_to, 0), in_=own[:, :],
                                         in_offset=None, bounds_check=NP - 1, oob_is_err=False).then_inc(s_put, 16)
                    e.wait_ge(s_put, 16)

                @block.scalar
                def _(e):
                    e.wait_ge(s_d, 1)
                    e.activation(ea[:, :, :], ea[:, :, :], ACT.Exp).then_inc(s_ex, 1)
                    e.activation(eb[:, :, :], eb[:, :, :], ACT.Exp).then_inc(s_ex, 1)
                    e.wait_ge(s_d, 2)
                    e.activation(e1[:, :], e1[:, :], ACT.Exp).then_inc(s_ex, 1)
                    e.activation(e2[:, :], e2[:, :], ACT.Exp).then_inc(s_ex, 1)

                @block.vector
                def _(e):
                    ch = Chain(e, s_u)
                    ch.do(e.tensor_scalar(apT[:, :], through[:, :], BIG, -BIG, ALU.mult, ALU.add))
                    ch.do(e.memset(sh[:, 0:2, 0:1], -BIG))
                    ch.do(e.memset(sh[:, 2:6, 0:1], 0.0))
                    ch.do(e.memset(ea[:, :, 0:1], 0.0))
                    e.wait_ge(s_pt, 6)
                    ch.do(e.tensor_copy(TT[:, 0:4, :].rearrange("p k n -> p (k n)"), pT[:, :]))
                    ch.to(e.tensor_copy(TT[:, 4:6, :].rearrange("p k n -> p (k n)"), pB[:, 0:2 * P]))
                    for k in range(2):
                        ch.do(e.tensor_tensor_scan(Mx[:, k, :], apT[:, :], TT[:, k, :], -BIG, ALU.add, ALU.max))
                    ch.sync()
                    ch.do(e.tensor_tensor(ea[:, :, 1:P], Mx[:, :, 0:P - 1], Mx[:, :, 1:P], ALU.subtract))
                    ch.do(e.tensor_tensor(eb[:, :, :], TT[:, 0:2, :], Mx[:, :, :], ALU.subtract))
                    ch.sync()
                    ch.do(e.tensor_scalar(ea[:, :, :], ea[:, :, :], 0.0, None, ALU.min))
                    ch.tell(s_d)
                    e.wait_ge(s_ex, 2)
                    ch.do(e.tensor_tensor(ea[:, :, :], ea[:, :, :],
                                          through[:, None, :].to_broadcast([P, 2, P]), ALU.mult))
                    for t in range(2):
                        ch.do(e.tensor_tensor(TT[:, 2 + 2 * t:4 + 2 * t, :], TT[:, 2 + 2 * t:4 + 2 * t, :], eb[:, :, :], ALU.mult))
                    ch.sync()
                    ch.do(e.tensor_copy(sh[:, 0:2, 1:P], Mx[:, :, 0:P - 1]))
                    for k in range(2, 6):
                        ch.do(e.tensor_tensor_scan(sh[:, k, 1:P], ea[:, k % 2, 0:P - 1], TT[:, k, 0:P - 1], 0.0,
                                                   ALU.mult, ALU.add))
                    ch.tell(s_sh)
                    e.wait_ge(s_pb, 6)
                    ch.do(e.tensor_copy(cin[:, 0:4 * P], pC[:, :]))
                    ch.to(e.tensor_copy(cin[:, 4 * P:], pD[:, 0:2 * P]))
                    e.wait_ge(s_own, 16)
                    ch.to(e.tensor_tensor(top[:, :], cin[:, 0:CH], own[:, 0:CH], ALU.max))
                    ch.do(e.tensor_tensor(e1[:, :], own[:, 0:CH], top[:, :], ALU.subtract))
                    ch.do(e.tensor_tensor(e2[:, :], cin[:, 0:CH], top[:, :], ALU.subtract))
                    ch.tell(s_d)
                    e.wait_ge(s_ex, 4)
                    for t in (1, 2):
                        ch.do(e.tensor_tensor(own[:, t * CH:(t + 1) * CH], own[:, t * CH:(t + 1) * CH], e1[:, :], ALU.mult))
                        ch.do(e.tensor_tensor(cin[:, t * CH:(t + 1) * CH], cin[:, t * CH:(t + 1) * CH], e2[:, :], ALU.mult))
                    ch.sync()
                    ch.do(e.tensor_tensor(own[:, CH:], own[:, CH:], cin[:, CH:], ALU.add))
                    ch.do(e.tensor_copy(own[:, 0:CH], top[:, :]))
                    ch.tell(s_mrg)

        c, sbl, psl, seml = stage("attn_nodes")
        with c:
            G = 7
            st = [sbl(f"st{q}", [P, G, 2 * CH]) for q in range(2)]
            s_v, s_ld0, s_ld1, s_done = seml("v", "ld0", "ld1", "done")
            s_ld = (s_ld0, s_ld1)
            rows = by_node(state3)
            with nc.Block() as block:
                @block.sync
                def _(e):
                    for k in range(C // G):
                        if k >= 2:
                            e.wait_ge(s_done, k - 1)
                        e.dma_start(st[k % 2][:, :, :], rows[:, k * G:(k + 1) * G, CH:]).then_inc(s_ld[k % 2], 16)

                @block.vector
                def _(e):
                    ch = Chain(e, s_v)
                    for k in range(C // G):
                        e.wait_ge(s_ld[k % 2], 16 * (k // 2 + 1))
                        den, num = st[k % 2][:, :, 0:CH], st[k % 2][:, :, CH:]
                        ch.to(e.tensor_scalar(den, den, 1e-30, None, ALU.max))
                        ch.to(e.reciprocal(den, den))
                        ch.to(e.tensor_tensor(num, num, den, ALU.mult))
                        ch.to(e.tensor_reduce(agg[:, k * G:(k + 1) * G, :],
                                              num.rearrange("p g (i o) -> p g o i", i=D), AX.X, ALU.add))
                        e.sem_inc(s_done, 1)
                    ch.to(e.tensor_tensor(x[:, :, :], x[:, :, :], agg[:, :, :], ALU.add))

        c, sbl, psl, seml = stage("store")
        s_out, = seml("out")
        with nc.Block() as block:
            @block.sync
            def _(e):
                e.dma_start(out, x[:, :, :]).then_inc(s_out, 16)
                e.wait_ge(s_out, 16)


_WEIGHTS = ["L0_gnn_W_gcn", "L0_gnn_W1", "L0_gnn_W2", "L1_gnn_W1", "L1_gnn_W2", "L3_gnn_W_msg", "L3_gnn_W_attn"]
_COLUMNS = ["L0_gnn_b1"]
_ROWS = ["L0_gnn_b2", "L1_gnn_b1", "L1_gnn_b2", "L1_gnn_bias", "L1_gnn_gamma", "L1_gnn_beta", "L2_gnn_b1",
         "L2_gnn_b2", "L3_gnn_b_msg", "L3_gnn_b_attn"]


def kernel(**inputs):
    import numpy as np
    import concourse.bacc as bacc
    from concourse.bass_utils import run_bass_kernel_spmd

    got = {k: np.asarray(v) for k, v in inputs.items()}
    pad = P * L - E

    def edges(v):
        v = np.concatenate([v, np.zeros((pad, v.shape[1]), v.dtype)])
        return np.ascontiguousarray(v.reshape(P, L, -1).transpose(2, 1, 0))

    src = np.concatenate([got["src"], np.full(pad, NP - 1, np.int32)])
    dst = np.concatenate([[-1], got["dst"], np.full(pad, NP - 1), [-1]]).astype(np.int32)
    nodes = np.concatenate([got["x"], np.zeros((NP - N, D), np.float32)])
    arrays = {
        "x": np.ascontiguousarray(nodes.reshape(C, P, D).transpose(1, 0, 2)),
        "src": src.reshape(P, L),
        "dst": np.stack([dst[p * L:p * L + L + 2] for p in range(P)]),
        "ef16": edges(got["edge_attr_16"]),
        "ef6": edges(got["edge_attr_6"]),
        "L2_W1T": np.ascontiguousarray(got["L2_gnn_W1"].T),
        "L2_W2T": np.ascontiguousarray(got["L2_gnn_W2"].T),
    }
    arrays.update({k: got[k] for k in _WEIGHTS})
    arrays.update({k: got[k].reshape(-1, 1) for k in _COLUMNS})
    arrays.update({k: got[k].reshape(1, -1) for k in _ROWS})
    nc = bacc.Bacc("TRN2", target_bir_lowering=False, num_devices=1)
    a = {k: nc.dram_tensor(f"in_{k}", v.shape, mybir.dt.from_np(v.dtype), kind="ExternalInput").ap()
         for k, v in arrays.items()}
    out = nc.dram_tensor("out_x", (P, C, D), F32, kind="ExternalOutput").ap()
    gnn_kernel(nc, a, out)
    r = run_bass_kernel_spmd(nc, [{f"in_{k}": v for k, v in arrays.items()}], core_ids=[0])
    res = r.results[0]["out_x"]
    return np.ascontiguousarray(res.transpose(1, 0, 2).reshape(NP, D)[:N])
```

```python
from contextlib import ExitStack

import concourse.bass as bass
from concourse import mybir
from concourse.alu_op_type import AluOpType as ALU

F32 = mybir.dt.float32
BF16 = mybir.dt.bfloat16
I32 = mybir.dt.int32
ACT = mybir.ActivationFunctionType
AX = mybir.AxisListType

P = 128
N = 6250
C = -(-N // P)
NP = C * P
E = 206250
L = -(-E // P)
D = 16
J = 26
NB = L // J
J3 = 13
NB3 = L // J3
T2 = 18
S3 = 3 * 256
BIG = 1e30
SKIP = 8192
EPS = 1e-5
assert NB * J == L and NB % 2 == 0 and NB3 * J3 == L and NB3 % 2 == 0


class Chain:

    def __init__(self, eng, sem):
        self.eng, self.sem, self.n, self.base = eng, sem, 0, 0

    def do(self, ins):
        ins.then_inc(self.sem, 1)
        self.n += 1
        return self.n

    def wait(self, n):
        self.eng.wait_ge(self.sem, self.base + n)

    def sync(self):
        self.eng.wait_ge(self.sem, self.base + self.n)

    def to(self, ins):
        self.do(ins)
        self.sync()

    def tell(self, sem):
        self.sync()
        self.eng.sem_inc(sem, 1)

    def loop(self, i, per):
        self.start, self.per, self.base = self.n, per, i * per

    def end(self, turns):
        assert self.n - self.start == self.per, (self.n - self.start, self.per)
        self.n, self.base = self.start + turns * self.per, 0


def gnn_kernel(nc, a, out):
    ctx = ExitStack()

    def sb(name, shape, dt=F32, c=ctx):
        return c.enter_context(nc.sbuf_tensor(name, shape, dt))

    def ps(name, shape, c, dt=F32):
        return c.enter_context(nc.psum_tensor(name, shape, dt))

    def sem(name, c=ctx):
        return c.enter_context(nc.semaphore(name))

    def dram(name, shape):
        return nc.dram_tensor(name, shape, F32, kind="Internal").ap()

    tab = [dram(f"tab{k}", (NP, T2 if k == 2 else D)) for k in range(4)]
    runs = [dram(f"runs{k}", (P * L, D)) for k in range(3)]
    corr = [dram(f"corr{k}", (NP, D)) for k in range(3)]
    state3 = dram("state3", (NP, S3))

    with ctx:
        ident = sb("ident", [P, P])
        tri = sb("tri", [P, P])
        ones = sb("ones", [P, P])
        iota_f = sb("iota_f", [P, P])
        iota_b = sb("iota_b", [P, P], BF16)
        x = sb("x", [P, C, D])
        h = sb("h", [P, C, D])
        agg = sb("agg", [P, C, D])
        tmp = sb("tmp", [P, C, D])
        same = sb("same", [P, L])
        apart = sb("apart", [P, L])
        end_to = sb("end_to", [P, L], I32)
        src_lo = sb("src_lo", [P, L])
        src_hi = sb("src_hi", [P, L])
        cnt_d = sb("cnt_d", [P, C])
        full = sb("full", [P, C])
        real = sb("real", [P, C])
        dinv = sb("dinv", [P, C])
        dis = sb("dis", [P, C])
        v1 = sb("v1", [P, C])
        v2 = sb("v2", [P, C])
        last_edge = sb("last_edge", [P, C], I32)
        through = sb("through", [P, P])
        carry_to = sb("carry_to", [P, 1], I32)
        first_node = sb("first_node", [P, 1], I32)
        eps = sb("eps", [P, 1])

        def bc_f(t):
            return t[:, :, None].to_broadcast([P, C, D])

        def flat(t):
            return t.rearrange("p c f -> p (c f)")

        def by_node(t):
            return t.rearrange("(c p) f -> p c f", p=P)

        def stage(name):
            c = ExitStack()
            return (c, lambda n, s, dt=F32: sb(f"{name}_{n}", s, dt, c),
                    lambda n: ps(f"{name}_{n}", [P, 512], c),
                    lambda *names: [used.append(sem(f"{name}_{n}", sems)) or used[-1] for n in names])

        used, sems = [], ExitStack()

        def renew_semaphores():
            with nc.Block() as block:
                @block.gpsimd
                def _(e):
                    for s in used:
                        e.sem_clear(s)
            sems.close()
            used.clear()

        def block_cols(i, b):
            return bass.ds(i * (2 * J) + b * J, J)

        def one_hot(e, to, digit, cols, w):
            return e.tensor_tensor(to, iota_b[:, None, 0:w].to_broadcast([P, J, w]),
                                   digit[:, cols][:, :, None].to_broadcast([P, J, w]), ALU.is_equal)

        def count(e, to, digits):
            for j in range(J):
                mm = e.matmul(to[:, 0:C], digits[:, j, 0:P], digits[:, j, P:P + C],
                              start=False, stop=False, skip_group_check=True)
            return mm

        class At:

            def __init__(self, k, i=None):
                self.k, self.i, self.b = k, i, k % 2

            def of(self, per, more):
                return self.k * per + more if self.i is None else self.i * (2 * per) + (self.k * per + more)

            def half(self, per, more):
                return self.k // 2 * per + more if self.i is None else self.i * per + (self.k // 2 * per + more)

            def cols(self, size=J, more=0):
                return bass.ds(self.of(size, more), size)

            def plus(self, d):
                return At(self.k + d, self.i)

        def walk(e, n, step, ch=None, per=0, head=0, tail=2):
            for k in range(head):
                step(At(k))
            with e.Fori(0, (n - head - tail) // 2) as i:
                if ch:
                    ch.loop(i, 2 * per)
                step(At(head, i))
                step(At(head + 1, i))
            if ch:
                ch.end((n - head - tail) // 2)
            for k in range(n - tail, n):
                step(At(k))

        def bank_free(k, banks, per):
            last = k - banks if k >= banks else max(q for q in range(per) if q % banks == k) - per
            return last + 1 + banks

        c, sbl, psl, seml = stage("prep")
        with c:
            dstw = sbl("dstw", [P, L + 2], I32)
            dstf = sbl("dstf", [P, L + 2])
            srci = sbl("srci", [P, L], I32)
            ti = sbl("ti", [P, L], I32)
            nxt = sbl("nxt", [P, L])
            dst_lo = sbl("dst_lo", [P, L])
            dst_hi = sbl("dst_hi", [P, L])
            iota_i = sbl("iota_i", [P, P], I32)
            node_i = sbl("node_i", [P, C], I32)
            node_f = sbl("node_f", [P, C])
            zero = sbl("zero", [P, 7 * S3])
            digits = [sbl(f"digits{b}", [P, J, P + C], BF16) for b in range(2)]
            f1, f2, f3, f4 = (sbl(f"f{k}", [P, 1]) for k in range(1, 5))
            diag = sbl("diag", [P, P])
            col_total = sbl("col_total", [P, C])
            onec = sbl("onec", [P, C])
            pcnt = psl("cnt")
            pthr, pcum, ptot = (psl(n) for n in ("thr", "cum", "tot"))
            s_in, s_zero, s_zd, s_pool, s_clear, s_v, s_mm, s_dig = seml(
                "in", "zero", "zd", "pool", "clear", "v", "mm", "dig")
            s_diag, s_thr, s_cnt, s_cum, s_deg, s_sqrt = seml("diag", "thr", "cnt", "cum", "deg", "sqrt")
            with nc.Block() as block:
                @block.sync
                def _(e):
                    e.dma_start(dstw[:, :], a["dst"]).then_inc(s_in, 16)
                    e.dma_start(srci[:, :], a["src"]).then_inc(s_in, 16)
                    e.dma_start(x[:, :, :], a["x"]).then_inc(s_in, 16)
                    e.wait_ge(s_zero, 1)
                    for t in corr:
                        e.dma_start(t.rearrange("(p c) f -> p (c f)", p=P), zero[:, 0:C * D]).then_inc(s_zd, 16)
                    st = state3.rearrange("(p c) f -> p (c f)", p=P)
                    for k in range(C // 7):
                        e.dma_start(st[:, k * 7 * S3:(k + 1) * 7 * S3], zero[:, :]).then_inc(s_zd, 16)
                    e.wait_ge(s_zd, 16 * (3 + C // 7))
                    e.wait_ge(s_in, 48)

                @block.gpsimd
                def _(e):
                    ch = Chain(e, s_pool)
                    ch.do(e.iota(iota_i[:, :], pattern=[[1, P]], base=0, channel_multiplier=0))
                    ch.do(e.iota(node_i[:, :], pattern=[[P, C]], base=0, channel_multiplier=1))
                    ch.to(e.memset(ones[:, :], 1.0))
                    ch.do(e.affine_select(out=ident[:, :], in_=ones[:, :], compare_op=ALU.is_equal, fill=0.0,
                                          base=0, pattern=[[-1, P]], channel_multiplier=1))
                    ch.do(e.affine_select(out=tri[:, :], in_=ones[:, :], compare_op=ALU.is_ge, fill=0.0,
                                          base=0, pattern=[[1, P]], channel_multiplier=-1))

                @block.vector
                def _(e):
                    e.memset(zero[:, :], 0.0).then_inc(s_zero, 1)
                    ch = Chain(e, s_v)
                    ch.do(e.memset(pcnt[:, 0:C], 0.0))
                    ch.tell(s_clear)
                    ch.do(e.memset(onec[:, :], 1.0))
                    ch.do(e.memset(eps[:, :], EPS))
                    e.wait_ge(s_pool, 5)
                    ch.do(e.tensor_copy(iota_f[:, :], iota_i[:, :]))
                    ch.do(e.tensor_copy(iota_b[:, :], iota_i[:, :]))
                    ch.do(e.tensor_copy(node_f[:, :], node_i[:, :]))
                    e.wait_ge(s_in, 48)
                    ch.do(e.tensor_copy(dstf[:, :], dstw[:, :]))
                    for ids, lo, hi in ((dstw[:, 1:L + 1], dst_lo, dst_hi), (srci[:, :], src_lo, src_hi)):
                        ch.to(e.tensor_scalar(ti[:, :], ids, 127, None, ALU.bitwise_and))
                        ch.to(e.tensor_copy(lo[:, :], ti[:, :]))
                        ch.to(e.tensor_scalar(ti[:, :], ids, 7, None, ALU.arith_shift_right))
                        ch.to(e.tensor_copy(hi[:, :], ti[:, :]))
                    ch.do(e.tensor_tensor(same[:, 1:L], dstf[:, 2:L + 1], dstf[:, 1:L], ALU.is_equal))
                    ch.do(e.memset(same[:, 0:1], 0.0))
                    ch.sync()
                    ch.do(e.tensor_scalar(apart[:, :], same[:, :], BIG, -BIG, ALU.mult, ALU.add))
                    ch.to(e.tensor_tensor(nxt[:, :], dstf[:, 2:L + 2], dstf[:, 1:L + 1], ALU.is_equal))
                    ch.to(e.tensor_scalar(nxt[:, :], nxt[:, :], float(SKIP), None, ALU.mult))
                    ch.to(e.tensor_tensor(nxt[:, :], nxt[:, :], dstf[:, 1:L + 1], ALU.add))
                    ch.do(e.tensor_copy(end_to[:, :], nxt[:, :]))
                    ch.do(e.tensor_scalar(real[:, :], node_f[:, :], float(N), None, ALU.is_lt))
                    ch.do(e.tensor_tensor(f1[:, :], dstf[:, 1:2], dstf[:, L:L + 1], ALU.is_equal))
                    ch.do(e.tensor_tensor(f2[:, :], dstf[:, 0:1], dstf[:, 1:2], ALU.is_equal))
                    ch.do(e.tensor_tensor(f3[:, :], dstf[:, L:L + 1], dstf[:, L + 1:L + 2], ALU.is_equal))
                    ch.sync()
                    ch.to(e.tensor_tensor(f4[:, :], f1[:, :], f2[:, :], ALU.mult))
                    ch.do(e.tensor_scalar(diag[:, :], ident[:, :], f4[:, 0:1], None, ALU.mult))
                    ch.tell(s_diag)
                    ch.to(e.tensor_tensor(f1[:, :], f1[:, :], f3[:, :], ALU.mult))
                    ch.to(e.tensor_scalar(f1[:, :], f1[:, :], -1.0, 1.0, ALU.mult, ALU.add))
                    ch.to(e.tensor_tensor(f2[:, :], f2[:, :], f1[:, :], ALU.mult))
                    ch.to(e.tensor_scalar(f2[:, :], f2[:, :], -float(SKIP), float(SKIP), ALU.mult, ALU.add))
                    ch.to(e.tensor_tensor(f2[:, :], f2[:, :], dstf[:, 1:2], ALU.add))
                    ch.do(e.tensor_copy(carry_to[:, :], f2[:, :]))
                    ch.do(e.tensor_copy(first_node[:, :], dstf[:, 1:2]))
                    ch.sync()
                    with e.Fori(0, NB // 2) as i:
                        for b in range(2):
                            e.wait_ge(s_mm, i * 2 + (b + 1))
                            one_hot(e, digits[b][:, :, 0:P], dst_lo, block_cols(i, b), P).then_inc(s_dig, 1)
                            one_hot(e, digits[b][:, :, P:], dst_hi, block_cols(i, b), C).then_inc(s_dig, 1)
                    e.wait_ge(s_cnt, 1)
                    ch.do(e.tensor_copy(cnt_d[:, :], pcnt[:, 0:C]))
                    ch.tell(s_deg)
                    ch.do(e.tensor_scalar(v1[:, :], cnt_d[:, :], 1.0, None, ALU.add))
                    ch.do(e.tensor_scalar(full[:, :], cnt_d[:, :], 0.5, None, ALU.is_ge))
                    ch.tell(s_deg)
                    e.wait_ge(s_thr, 1)
                    ch.do(e.tensor_copy(through[:, :], pthr[:, 0:P]))
                    e.wait_ge(s_sqrt, 1)
                    ch.do(e.reciprocal(dinv[:, :], dinv[:, :]))
                    e.wait_ge(s_cum, 1)
                    ch.to(e.tensor_copy(col_total[:, :], ptot[:, 0:C]))
                    ch.to(e.tensor_tensor_scan(v1[:, :], onec[:, :], col_total[:, :], 0.0, ALU.mult, ALU.add))
                    ch.to(e.tensor_tensor(v1[:, :], v1[:, :], col_total[:, :], ALU.subtract))
                    ch.to(e.tensor_tensor(v1[:, :], v1[:, :], pcum[:, 0:C], ALU.add))
                    ch.to(e.tensor_scalar(v1[:, :], v1[:, :], -1.0, 0.0, ALU.add, ALU.max))
                    ch.to(e.tensor_copy(last_edge[:, :], v1[:, :]))

                @block.tensor
                def _(e):
                    e.wait_ge(s_pool, 5)
                    e.wait_ge(s_clear, 1)
                    e.sem_inc(s_mm, 2)
                    with e.Fori(0, NB // 2) as i:
                        for b in range(2):
                            e.wait_ge(s_dig, i * 4 + (2 * b + 2))
                            count(e, pcnt, digits[b]).then_inc(s_mm, 1)
                    e.wait_ge(s_mm, NB + 2)
                    e.sem_inc(s_cnt, 1)
                    e.wait_ge(s_diag, 1)
                    e.matmul(pthr[:, 0:P], ones[:, :], diag[:, :], start=True, stop=True).then_inc(s_thr, 1)
                    e.wait_ge(s_deg, 1)
                    e.matmul(pcum[:, 0:C], tri[:, :], cnt_d[:, :], start=True, stop=True)
                    e.matmul(ptot[:, 0:C], ones[:, :], cnt_d[:, :], start=True, stop=True).then_inc(s_cum, 1)

                @block.scalar
                def _(e):
                    e.wait_ge(s_deg, 2)
                    e.activation(dinv[:, :], v1[:, :], ACT.Sqrt).then_inc(s_sqrt, 1)

        def norm_and_table(k):
            c, sbl, psl, seml = stage(f"norm{k}")
            with c:
                row = sbl("row", [P, C, T2]) if k == 2 else tmp if k == 0 else h
                s_v, s_var, s_std, s_row, s_tab = seml("v", "var", "std", "row", "tab")
                with nc.Block() as block:
                    @block.vector
                    def _(e):
                        ch = Chain(e, s_v)
                        ch.to(e.tensor_reduce(v1[:, :], x[:, :, :], AX.X, ALU.add))
                        ch.to(e.tensor_scalar(v1[:, :], v1[:, :], 1.0 / D, None, ALU.mult))
                        ch.to(e.tensor_tensor(tmp[:, :, :], x[:, :, :], bc_f(v1), ALU.subtract))
                        ch.to(e.tensor_tensor(h[:, :, :], tmp[:, :, :], tmp[:, :, :], ALU.mult))
                        ch.to(e.tensor_reduce(v2[:, :], h[:, :, :], AX.X, ALU.add))
                        ch.tell(s_var)
                        e.wait_ge(s_std, 1)
                        ch.to(e.reciprocal(v1[:, :], v1[:, :]))
                        ch.to(e.tensor_tensor(tmp[:, :, :], tmp[:, :, :], bc_f(v1), ALU.mult))
                        ch.to(e.tensor_scalar(h[:, :, :], tmp[:, :, :], 0.0, None, ALU.max))
                        if k == 0:
                            ch.do(e.tensor_tensor(row[:, :, :], h[:, :, :], bc_f(dinv), ALU.mult))
                        if k == 2:
                            ch.do(e.tensor_copy(row[:, :, 0:D], h[:, :, :]))
                            ch.do(e.tensor_copy(row[:, :, D:D + 1], dis[:, :, None]))
                            ch.do(e.memset(row[:, :, D + 1:T2], 1.0))
                        ch.tell(s_row)

                    @block.scalar
                    def _(e):
                        e.wait_ge(s_var, 1)
                        e.activation(v1[:, :], v2[:, :], ACT.Sqrt, bias=eps[:, 0:1], scale=1.0 / D).then_inc(s_std, 1)

                    @block.sync
                    def _(e):
                        e.wait_ge(s_row, 1)
                        e.dma_start(by_node(tab[k]), row[:, :, :]).then_inc(s_tab, 16)
                        e.wait_ge(s_tab, 16)

        s_turns = sem("turns")

        def turn_wait(e, s, value):
            e.wait_ge(s, value)
            e.sem_inc(s_turns, 1)

        def indices(idx, b):
            return bass.IndirectOffsetOnAxis(ap=idx[:, b:b + 1], axis=0)

        def scan_block(e, ch, cols, msg, run, before):
            for f in range(D):
                ch.do(e.tensor_tensor_scan(run[:, :, f], same[:, cols], msg[:, :, f], before[:, J - 1, f:f + 1],
                                           ALU.mult, ALU.add))

        def node_sums(k, last):
            c, sbl, psl, seml = stage(f"sums{k}")
            with c:
                stT = sbl("stT", [D, P])
                cT = sbl("cT", [D, P])
                shifted = sbl("shifted", [D, P])
                carry = sbl("carry", [P, D])
                more = sbl("more", [P, C, D])
                pa, pb = psl("a"), psl("b")
                s_v, s_t, s_sh, s_back, s_carry, s_cd, s_g, s_more = seml(
                    "v", "t", "sh", "back", "carry", "cd", "g", "more")
                with nc.Block() as block:
                    @block.tensor
                    def _(e):
                        e.transpose(pa[0:D, 0:P], last, ident[:, :]).then_inc(s_t, 1)
                        e.wait_ge(s_sh, 1)
                        e.transpose(pb[:, 0:D], shifted[:, :], ident[0:D, 0:D]).then_inc(s_back, 1)

                    @block.vector
                    def _(e):
                        ch = Chain(e, s_v)
                        ch.do(e.memset(shifted[:, 0:1], 0.0))
                        e.wait_ge(s_t, 1)
                        ch.to(e.tensor_copy(stT[:, :], pa[0:D, 0:P]))
                        ch.to(e.tensor_tensor_scan(cT[:, :], through[0:D, :], stT[:, :], 0.0, ALU.mult, ALU.add))
                        ch.do(e.tensor_copy(shifted[:, 1:P], cT[:, 0:P - 1]))
                        ch.tell(s_sh)
                        e.wait_ge(s_back, 1)
                        ch.do(e.tensor_copy(carry[:, :], pb[:, 0:D]))
                        ch.tell(s_carry)
                        e.wait_ge(s_g, 16 * C)
                        ch.to(e.tensor_tensor(agg[:, :, :], agg[:, :, :], bc_f(full), ALU.mult))
                        e.wait_ge(s_more, 16)
                        ch.to(e.tensor_tensor(agg[:, :, :], agg[:, :, :], more[:, :, :], ALU.add))

                    @block.gpsimd
                    def _(e):
                        e.wait_ge(s_carry, 1)
                        e.indirect_dma_start(out=corr[k], out_offset=indices(carry_to, 0), in_=carry[:, :],
                                             in_offset=None, bounds_check=NP - 1, oob_is_err=False).then_inc(s_cd, 16)
                        for q in range(C):
                            e.indirect_dma_start(out=agg[:, q, :], out_offset=None, in_=runs[k],
                                                 in_offset=indices(last_edge, q)).then_inc(s_g, 16)

                    @block.sync
                    def _(e):
                        e.wait_ge(s_cd, 16)
                        e.dma_start(more[:, :, :], by_node(corr[k])).then_inc(s_more, 16)

        norm_and_table(0)
        c, sbl, psl, seml = stage("gcn")
        with c:
            idx = [sbl(f"idx{b}", [P, J], I32) for b in range(2)]
            got = [sbl(f"got{b}", [P, J, D]) for b in range(2)]
            run = [sbl(f"run{b}", [P, J, D]) for b in range(2)]
            digits = [sbl(f"digits{b}", [P, J, P + C], BF16) for b in range(2)]
            banks = ExitStack()
            pcnt = ps("gcn_cnt", [P, 512], banks)
            s_v, s_clear, s_dig, s_mm, s_deg, s_sqrt = seml("v", "clear", "dig", "mm", "deg", "sqrt")
            s_idx, s_got, s_run, s_st, s_kept = (seml(f"{n}0", f"{n}1") for n in ("idx", "got", "run", "st", "kept"))
            src_blk = a["src"]
            run_rows = runs[0].rearrange("(p l) f -> p l f", p=P)
            with nc.Block() as block:
                @block.sync
                def _(e):
                    for b in range(2):
                        e.dma_start(idx[b][:, :], src_blk[:, b * J:(b + 1) * J]).then_inc(s_idx[b], 16)
                    for b in range(2):
                        e.sem_inc(s_kept[b], 1)
                    with e.Fori(0, NB // 2 - 1) as i:
                        for b in range(2):
                            e.wait_ge(s_run[b], i + 1)
                            e.dma_start(run_rows[:, block_cols(i, b), :], run[b][:, :, :]).then_inc(s_st[b], 16)
                            e.dma_start(idx[b][:, :], src_blk[:, block_cols(i + 1, b)]).then_inc(s_idx[b], 16)
                            e.wait_ge(s_st[b], i * 16 + 16)
                            e.sem_inc(s_kept[b], 1)
                    for b in range(2):
                        e.wait_ge(s_run[b], NB // 2)
                        at = L - (2 - b) * J
                        e.dma_start(run_rows[:, at:at + J, :], run[b][:, :, :]).then_inc(s_st[b], 16)
                    for b in range(2):
                        e.wait_ge(s_st[b], 16 * (NB // 2))

                @block.gpsimd
                def _(e):
                    with e.Fori(0, NB // 2) as i:
                        for b in range(2):
                            turn_wait(e, s_idx[b], i * 16 + 16)
                            for j in range(J):
                                e.indirect_dma_start(out=got[b][:, j, :], out_offset=None, in_=tab[0],
                                                     in_offset=indices(idx[b], j)).then_inc(s_got[b], 16)

                @block.vector
                def _(e):
                    ch = Chain(e, s_v)
                    ch.do(e.memset(run[1][:, J - 1, :], 0.0))
                    ch.do(e.memset(pcnt[:, 0:C], 0.0))
                    ch.tell(s_clear)
                    with e.Fori(0, NB // 2) as i:
                        ch.loop(i, 2 * D)
                        for b in range(2):
                            e.wait_ge(s_mm, i * 2 + (b + 1))
                            one_hot(e, digits[b][:, :, 0:P], src_lo, block_cols(i, b), P).then_inc(s_dig, 1)
                            one_hot(e, digits[b][:, :, P:], src_hi, block_cols(i, b), C).then_inc(s_dig, 1)
                            e.wait_ge(s_got[b], i * (16 * J) + 16 * J)
                            e.wait_ge(s_kept[b], i + 1)
                            scan_block(e, ch, block_cols(i, b), got[b], run[b], run[1 - b])
                            ch.tell(s_run[b])
                    ch.end(NB // 2)
                    e.wait_ge(s_mm, NB + 2)
                    ch.to(e.tensor_tensor(v2[:, :], cnt_d[:, :], pcnt[:, 0:C], ALU.add))
                    ch.do(e.tensor_scalar(v2[:, :], v2[:, :], 1e-5, None, ALU.max))
                    ch.tell(s_deg)
                    e.wait_ge(s_sqrt, 1)
                    ch.to(e.reciprocal(dis[:, :], dis[:, :]))

                @block.tensor
                def _(e):
                    e.wait_ge(s_clear, 1)
                    e.sem_inc(s_mm, 2)
                    with e.Fori(0, NB // 2) as i:
                        for b in range(2):
                            e.wait_ge(s_dig, i * 4 + (2 * b + 2))
                            count(e, pcnt, digits[b]).then_inc(s_mm, 1)

                @block.scalar
                def _(e):
                    e.wait_ge(s_deg, 1)
                    e.activation(dis[:, :], v2[:, :], ACT.Sqrt).then_inc(s_sqrt, 1)
            banks.close()
            node_sums(0, run[1][:, J - 1, :])

        c, sbl, psl, seml = stage("gcn_nodes")
        with c:
            G = 7
            Wg, W1, b1 = sbl("Wg", [D, 48]), sbl("W1", [48, 32]), sbl("b1", [32, 1])
            W2 = sbl("W2", [33, D])
            part = [sbl(f"part{b}", [P, G, D]) for b in range(2)]
            aT, fT, uT = sbl("aT", [D, G * P]), sbl("fT", [48, G * P]), sbl("uT", [33, G * P])
            pt, pf, pu = ([psl(f"{n}{q}") for q in range(2)] for n in "tfu")
            po = psl("o")
            s_w, s_v, s_part, s_t, s_at, s_f, s_ft, s_u, s_ut, s_o, s_free = seml(
                "w", "v", "part", "t", "at", "f", "ft", "u", "ut", "o", "free")
            split = ((0, 4), (4, 7))
            with nc.Block() as block:
                @block.sync
                def _(e):
                    for t, n in ((Wg[:, :], "L0_gnn_W_gcn"), (W1[:, :], "L0_gnn_W1"),
                                 (b1[:, :], "L0_gnn_b1"), (W2[0:32, :], "L0_gnn_W2"), (W2[32:33, :], "L0_gnn_b2")):
                        e.dma_start(t, a[n]).then_inc(s_w, 16)

                @block.vector
                def _(e):
                    ch = Chain(e, s_v)
                    ch.do(e.memset(uT[32:33, :], 1.0))
                    ch.to(e.tensor_tensor(tmp[:, :, :], h[:, :, :], bc_f(dinv), ALU.mult))
                    ch.to(e.tensor_tensor(agg[:, :, :], agg[:, :, :], tmp[:, :, :], ALU.add))
                    ch.do(e.tensor_tensor(agg[:, :, :], agg[:, :, :], bc_f(dinv), ALU.mult))
                    ch.to(e.tensor_tensor(x[:, :, :], x[:, :, :], h[:, :, :], ALU.add))
                    with e.Fori(0, C // G) as i:
                        ch.loop(i, 6)
                        cols = bass.ds(i * G, G)
                        ch.do(e.tensor_copy(part[0][:, :, :], agg[:, cols, :]))
                        ch.tell(s_part)
                        for q, (lo, hi) in enumerate(split):
                            e.wait_ge(s_t, i * 2 + (q + 1))
                            ch.do(e.tensor_copy(aT[:, lo * P:hi * P], pt[q][0:D, 0:(hi - lo) * P]))
                            ch.tell(s_at)
                        for q, (lo, hi) in enumerate(split):
                            e.wait_ge(s_f, i * 2 + (q + 1))
                            ch.do(e.tensor_copy(fT[:, lo * P:hi * P], pf[q][0:48, 0:(hi - lo) * P]))
                            ch.tell(s_ft)
                        e.wait_ge(s_o, i + 1)
                        ch.to(e.tensor_tensor(x[:, cols, :], x[:, cols, :],
                                              po[:, 0:G * D].rearrange("p (g f) -> p g f", f=D), ALU.add))
                    ch.end(C // G)

                @block.tensor
                def _(e):
                    e.wait_ge(s_w, 80)
                    with e.Fori(0, C // G) as i:
                        turn_wait(e, s_part, i + 1)
                        for q, (lo, hi) in enumerate(split):
                            for g in range(lo, hi):
                                mm = e.transpose(pt[q][0:D, (g - lo) * P:(g - lo + 1) * P], part[0][:, g, :], ident[:, :])
                            mm.then_inc(s_t, 1)
                        for q, (lo, hi) in enumerate(split):
                            turn_wait(e, s_at, i * 2 + (q + 1))
                            e.matmul(pf[q][0:48, 0:(hi - lo) * P], Wg[:, :], aT[:, lo * P:hi * P],
                                     start=True, stop=True).then_inc(s_f, 1)
                        for q, (lo, hi) in enumerate(split):
                            turn_wait(e, s_ft, i * 2 + (q + 1))
                            e.matmul(pu[q][0:32, 0:(hi - lo) * P], W1[:, :], fT[:, lo * P:hi * P],
                                     start=True, stop=True).then_inc(s_u, 1)
                        turn_wait(e, s_ut, i * 2 + 2)
                        for g in range(G):
                            mm = e.matmul(po[:, g * D:(g + 1) * D], uT[:, g * P:(g + 1) * P], W2[:, :],
                                          start=True, stop=True)
                        mm.then_inc(s_o, 1)

                @block.scalar
                def _(e):
                    e.wait_ge(s_w, 80)
                    with e.Fori(0, C // G) as i:
                        for q, (lo, hi) in enumerate(split):
                            e.wait_ge(s_u, i * 2 + (q + 1))
                            e.activation(uT[0:32, lo * P:hi * P], pu[q][0:32, 0:(hi - lo) * P], ACT.Relu,
                                         bias=b1[:, 0:1]).then_inc(s_ut, 1)

        renew_semaphores()
        norm_and_table(1)
        c, sbl, psl, seml = stage("nnconv")
        H1 = 64
        QT = 8
        WT = J * P // QT
        with c:
            W1, W2 = sbl("W1", [7, H1]), sbl("W2", [P, 256])
            idx = [sbl(f"idx{b}", [P, J], I32) for b in range(2)]
            got = [sbl(f"got{b}", [P, J, D]) for b in range(2)]
            ef = [sbl(f"ef{b}", [7, J, P]) for b in range(2)]
            tT = [sbl(f"tT{b}", [P, J * P]) for b in range(2)]
            prod = [sbl(f"prod{q}", [P, 2, D, D]) for q in range(3)]
            msg = [sbl(f"msg{b}", [P, J, D]) for b in range(2)]
            run = [sbl(f"run{b}", [P, J, D]) for b in range(2)]
            pt = [psl(f"t{q}") for q in range(2)]
            BK = 4
            banks = ExitStack()
            pw = [ps(f"nnconv_w{q}", [P, 512], banks) for q in range(BK)]
            s_v, s_w, s_one, s_t, s_relu, s_edge, s_msg = seml("v", "w", "one", "t", "relu", "edge", "msg")
            s_idx, s_ef, s_got, s_run, s_st, s_kept = (seml(f"{n}0", f"{n}1") for n in ("idx", "ef", "got", "run", "st", "kept"))
            run_rows = runs[1].rearrange("(p l) f -> p l f", p=P)
            JJ = J // 2
            with nc.Block() as block:
                @block.sync
                def _(e):
                    e.wait_ge(s_one, 1)
                    for t, n in ((W1[0:6, :], "L1_gnn_W1"), (W1[6:7, :], "L1_gnn_b1"),
                                 (W2[0:H1, :], "L1_gnn_W2"), (W2[H1:H1 + 1, :], "L1_gnn_b2")):
                        e.dma_start(t, a[n]).then_inc(s_w, 16)

                    def load(b, cols):
                        e.dma_start(idx[b][:, :], a["src"][:, cols]).then_inc(s_idx[b], 16)
                        e.dma_start(ef[b][0:6, :, :], a["ef6"][:, cols, :]).then_inc(s_ef[b], 16)

                    for b in range(2):
                        load(b, slice(b * J, (b + 1) * J))
                    for b in range(2):
                        e.sem_inc(s_kept[b], 1)
                    with e.Fori(0, NB // 2 - 1) as i:
                        for b in range(2):
                            e.wait_ge(s_run[b], i + 1)
                            e.dma_start(run_rows[:, block_cols(i, b), :], run[b][:, :, :]).then_inc(s_st[b], 16)
                            load(b, block_cols(i + 1, b))
                            e.wait_ge(s_st[b], i * 16 + 16)
                            e.sem_inc(s_kept[b], 1)
                    for b in range(2):
                        e.wait_ge(s_run[b], NB // 2)
                        at = L - (2 - b) * J
                        e.dma_start(run_rows[:, at:at + J, :], run[b][:, :, :]).then_inc(s_st[b], 16)
                    for b in range(2):
                        e.wait_ge(s_st[b], 16 * (NB // 2))

                @block.gpsimd
                def _(e):
                    with e.Fori(0, NB // 2) as i:
                        for b in range(2):
                            turn_wait(e, s_idx[b], i * 16 + 16)
                            for j in range(J):
                                e.indirect_dma_start(out=got[b][:, j, :], out_offset=None, in_=tab[1],
                                                     in_offset=indices(idx[b], j)).then_inc(s_got[b], 16)

                @block.tensor
                def _(e):
                    e.wait_ge(s_w, 64)

                    def hidden(at):
                        turn_wait(e, s_ef[at.b], at.half(16, 16))
                        for q in range(QT):
                            turn_wait(e, s_relu, at.of(QT, q + 1))
                            e.matmul(pt[q % 2][0:H1, 0:WT], W1[:, :],
                                     ef[at.b].rearrange("k j p -> k (j p)")[:, q * WT:(q + 1) * WT],
                                     start=True, stop=True).then_inc(s_t, 1)

                    def matrices(at):
                        turn_wait(e, s_relu, at.of(QT, QT + 2))
                        for g in range(JJ):
                            k = at.b * JJ + g
                            turn_wait(e, s_msg, at.plus(-at.b).of(JJ, bank_free(k, BK, 2 * JJ)))
                            for j in range(2):
                                mm = e.matmul(pw[k % BK][:, j * 256:(j + 1) * 256],
                                              tT[at.b][:, (2 * g + j) * P:(2 * g + j + 1) * P], W2[:, :],
                                              start=True, stop=True)
                            mm.then_inc(s_edge, 1)

                    def step(at):
                        if at.k < NB - 1:
                            hidden(at.plus(1))
                        matrices(at)

                    hidden(At(0))
                    walk(e, NB, step)

                @block.scalar
                def _(e):
                    e.wait_ge(s_one, 1)
                    e.sem_inc(s_relu, 2)
                    with e.Fori(0, NB // 2) as i:
                        for b in range(2):
                            for q in range(QT):
                                e.wait_ge(s_t, i * (2 * QT) + (b * QT + q + 1))
                                e.activation(tT[b][0:H1, q * WT:(q + 1) * WT], pt[q % 2][0:H1, 0:WT],
                                             ACT.Relu).then_inc(s_relu, 1)

                @block.vector
                def _(e):
                    ch = Chain(e, s_v)
                    ch.do(e.memset(W2[:, :], 0.0))
                    for b in range(2):
                        ch.do(e.memset(ef[b][:, :, :], 1.0))
                        ch.do(e.memset(tT[b][H1:, :], 0.0))
                    ch.sync()
                    for b in range(2):
                        ch.do(e.memset(tT[b][H1:H1 + 1, :], 1.0))
                    ch.do(e.memset(run[1][:, J - 1, :], 0.0))
                    ch.sync()
                    e.sem_inc(s_one, 1)
                    e.sem_inc(s_msg, BK)
                    with e.Fori(0, NB // 2) as i:
                        ch.loop(i, 2 * (D + JJ))
                        for b in range(2):
                            e.wait_ge(s_got[b], i * (16 * J) + 16 * J)
                            e.wait_ge(s_kept[b], i + 1)
                            added = []
                            for g in range(JJ + 1):
                                if g < JJ:
                                    e.wait_ge(s_edge, i * (2 * JJ) + (b * JJ + g + 1))
                                    if g >= 3:
                                        ch.wait(added[g - 3])
                                    e.tensor_tensor(prod[g % 3][:, :, :, :],
                                                    pw[(b * JJ + g) % BK][:, :].rearrange("p (j i o) -> p j i o", j=2, i=D),
                                                    got[b][:, 2 * g:2 * g + 2, :][:, :, :, None].to_broadcast([P, 2, D, D]),
                                                    ALU.mult).then_inc(s_msg, 1)
                                if g >= 1:
                                    e.wait_ge(s_msg, i * (2 * JJ) + (b * JJ + g + BK))
                                    added.append(ch.do(e.tensor_reduce(
                                        msg[b][:, 2 * g - 2:2 * g, :],
                                        prod[(g - 1) % 3][:, :, :, :].rearrange("p j i o -> p j o i"), AX.X, ALU.add)))
                            ch.sync()
                            scan_block(e, ch, block_cols(i, b), msg[b], run[b], run[1 - b])
                            ch.tell(s_run[b])
                    ch.end(NB // 2)
            banks.close()
            node_sums(1, run[1][:, J - 1, :])

        c, sbl, psl, seml = stage("bn")
        with c:
            bias, gamma, beta = (sbl(n, [P, D]) for n in ("bias", "gamma", "beta"))
            part, mean, std = (sbl(n, [P, D]) for n in ("part", "mean", "std"))
            pm, pv = psl("m"), psl("v")
            s_w, s_v, s_p, s_m, s_std = seml("w", "v", "p", "m", "std")

            def bc_n(t):
                return t[:, None, :].to_broadcast([P, C, D])

            with nc.Block() as block:
                @block.sync
                def _(e):
                    for t, n in ((bias, "bias"), (gamma, "gamma"), (beta, "beta")):
                        e.dma_start(t[:, :], a[f"L1_gnn_{n}"].to_broadcast([P, D])).then_inc(s_w, 16)

                @block.tensor
                def _(e):
                    for k, t in enumerate((pm, pv)):
                        e.wait_ge(s_p, k + 1)
                        e.matmul(t[:, 0:D], ones[:, :], part[:, :], start=True, stop=True).then_inc(s_m, 1)

                @block.scalar
                def _(e):
                    e.wait_ge(s_m, 2)
                    e.activation(std[:, :], pv[:, 0:D], ACT.Sqrt, bias=eps[:, 0:1], scale=1.0 / N).then_inc(s_std, 1)

                @block.vector
                def _(e):
                    ch = Chain(e, s_v)
                    ch.to(e.tensor_scalar(v1[:, :], cnt_d[:, :], 1.0, None, ALU.max))
                    ch.to(e.reciprocal(v1[:, :], v1[:, :]))
                    ch.to(e.tensor_tensor(agg[:, :, :], agg[:, :, :], bc_f(v1), ALU.mult))
                    e.wait_ge(s_w, 48)
                    ch.to(e.tensor_tensor(agg[:, :, :], agg[:, :, :], bc_n(bias), ALU.add))
                    ch.to(e.tensor_scalar(agg[:, :, :], agg[:, :, :], 0.0, None, ALU.max))
                    ch.to(e.tensor_tensor(tmp[:, :, :], agg[:, :, :], bc_f(real), ALU.mult))
                    ch.do(e.tensor_reduce(part[:, :], tmp[:, :, :].rearrange("p c f -> p f c"), AX.X, ALU.add))
                    ch.tell(s_p)
                    e.wait_ge(s_m, 1)
                    ch.to(e.tensor_scalar(mean[:, :], pm[:, 0:D], 1.0 / N, None, ALU.mult))
                    ch.to(e.tensor_tensor(agg[:, :, :], agg[:, :, :], bc_n(mean), ALU.subtract))
                    ch.to(e.tensor_tensor(tmp[:, :, :], agg[:, :, :], bc_f(real), ALU.mult))
                    ch.to(e.tensor_tensor(tmp[:, :, :], tmp[:, :, :], tmp[:, :, :], ALU.mult))
                    ch.do(e.tensor_reduce(part[:, :], tmp[:, :, :].rearrange("p c f -> p f c"), AX.X, ALU.add))
                    ch.tell(s_p)
                    e.wait_ge(s_std, 1)
                    ch.to(e.reciprocal(std[:, :], std[:, :]))
                    ch.to(e.tensor_tensor(std[:, :], std[:, :], gamma[:, :], ALU.mult))
                    ch.to(e.tensor_tensor(agg[:, :, :], agg[:, :, :], bc_n(std), ALU.mult))
                    ch.to(e.tensor_tensor(agg[:, :, :], agg[:, :, :], bc_n(beta), ALU.add))
                    ch.to(e.tensor_tensor(x[:, :, :], x[:, :, :], agg[:, :, :], ALU.add))

        renew_semaphores()
        norm_and_table(2)
        c, sbl, psl, seml = stage("sheaf")
        H2 = 64
        JH = J // 2
        with c:
            Wz, W2 = sbl("Wz", [P, 2 * H2]), sbl("W2", [2 * H2, 2 * D])
            b2 = sbl("b2", [1, JH, 2, D])
            idx = [sbl(f"idx{b}", [P, 2, J], I32) for b in range(2)]
            got = [sbl(f"got{b}", [P, J, 2, T2]) for b in range(2)]
            gT = [sbl(f"gT{q}", [P, 2 * P]) for q in range(2)]
            zT = [sbl(f"zT{q}", [2 * H2, 2 * P]) for q in range(2)]
            vec = [sbl(f"vec{q}", [P, JH, 2, D]) for q in range(2)]
            prod = sbl("prod", [P, JH, 7, D])
            dots = sbl("dots", [P, JH, 7])
            cc = sbl("cc", [P, JH, 2])
            first = sbl("first", [P, JH, 2])
            second = sbl("second", [P, JH, 2])
            term = sbl("term", [P, JH, 2, D])
            msg = [sbl(f"msg{b}", [P, J, 2, D]) for b in range(2)]
            hot_lo = [sbl(f"hot_lo{q}", [P, JH, P]) for q in range(2)]
            hot_hi = [sbl(f"hot_hi{q}", [P, JH, C]) for q in range(2)]
            wide = [sbl(f"wide{q}", [P, C, D]) for q in range(2)]
            run = [sbl(f"run{b}", [P, J, D]) for b in range(2)]
            from_src = sbl("from_src", [P, C, D])
            banks = ExitStack()
            pg, pz, pv, pacc = ([ps(f"sheaf_{n}{q}", [P, 512], banks) for q in range(2)] for n in ("g", "z", "v", "acc"))
            HC = 25
            halves = ((0, HC), (HC, C))
            s_v, s_w, s_one, s_gT, s_gTc, s_z, s_zc, s_used, s_vc, s_vfree, s_wide, s_acc, s_sq, s_lo, s_msg = seml(
                "v", "w", "one", "gT", "gTc", "z", "zc", "used", "vc", "vfree", "wide", "acc", "sq", "lo", "msg")
            s_idx, s_got, s_run, s_st, s_kept = (seml(f"{n}0", f"{n}1") for n in ("idx", "got", "run", "st", "kept"))
            run_rows = runs[2].rearrange("(p l) f -> p l f", p=P)
            NG = JH
            with nc.Block() as block:
                @block.sync
                def _(e):
                    e.wait_ge(s_one, 1)
                    w1, w2 = a["L2_W1T"], a["L2_W2T"]
                    s, d, one = slice(0, D), slice(T2, T2 + D), slice(D + 1, D + 2)
                    for t, n in ((Wz[s, 0:H2], w1[0:D, :]), (Wz[d, 0:H2], w1[D:2 * D, :]),
                                 (Wz[d, H2:], w1[0:D, :]), (Wz[s, H2:], w1[D:2 * D, :]),
                                 (Wz[one, 0:H2], a["L2_gnn_b1"]), (Wz[one, H2:], a["L2_gnn_b1"]),
                                 (W2[0:H2, 0:D], w2), (W2[H2:, D:], w2),
                                 (b2.rearrange("k j t f -> k (j t) f"),
                                  a["L2_gnn_b2"][:, None, :].to_broadcast([1, 2 * JH, D]))):
                        e.dma_start(t, n).then_inc(s_w, 16)

                    def load(at):
                        e.dma_start(idx[at.b][:, 0, :], a["src"][:, at.cols()]).then_inc(s_idx[at.b], 16)
                        e.dma_start(idx[at.b][:, 1, :], a["dst"][:, at.cols(more=1)]).then_inc(s_idx[at.b], 16)

                    def step(at):
                        if at.k < NB - 2:
                            e.wait_ge(s_msg, at.of(1, 1))
                            load(at.plus(2))
                        e.wait_ge(s_run[at.b], at.half(1, 1))
                        e.dma_start(run_rows[:, at.cols(), :], run[at.b][:, :, :]).then_inc(s_st[at.b], 16)
                        e.wait_ge(s_st[at.b], at.half(16, 16))
                        e.sem_inc(s_kept[at.b], 1)

                    for b in range(2):
                        e.sem_inc(s_kept[b], 1)
                        load(At(b))
                    walk(e, NB, step, head=2)

                @block.gpsimd
                def _(e):
                    with e.Fori(0, NB // 2) as i:
                        for b in range(2):
                            turn_wait(e, s_idx[b], i * 32 + 32)
                            for j in range(J):
                                for k in range(2):
                                    e.indirect_dma_start(out=got[b][:, j, k, :], out_offset=None, in_=tab[2],
                                                         in_offset=indices(idx[b][:, k, :], j)).then_inc(s_got[b], 16)

                @block.tensor
                def _(e):
                    e.wait_ge(s_w, 16 * 9)
                    e.wait_ge(s_one, 1)
                    e.sem_inc(s_z, 2)
                    e.sem_inc(s_used, 2)
                    e.sem_inc(s_acc, 2)

                    def turned(at, g):
                        q = (at.b * NG + g) % 2
                        turn_wait(e, s_gTc, at.of(NG, g + 1))
                        for j in range(2):
                            mm = e.transpose(pg[q][0:2 * T2, j * P:(j + 1) * P],
                                             got[at.b][:, 2 * g + j, :, :].rearrange("p t f -> p (t f)"), ident[:, :])
                        mm.then_inc(s_gT, 1)

                    def hidden(at, g):
                        q = (at.b * NG + g) % 2
                        turn_wait(e, s_gTc, at.of(NG, g + 3))
                        turn_wait(e, s_zc, at.of(NG, g + 1))
                        e.matmul(pz[q][:, 0:2 * P], Wz[:, :], gT[q][:, :], start=True, stop=True).then_inc(s_z, 1)

                    def vectors(at, g):
                        q = (at.b * NG + g) % 2
                        turn_wait(e, s_zc, at.of(NG, g + 3))
                        for j in range(2):
                            half, col = divmod(2 * g + j, JH)
                            if col == 0:
                                turn_wait(e, s_vc, at.of(2, half + 1))
                                e.matmul(pv[half][:, 0:JH * 2 * D], ones[0:1, :],
                                         b2.rearrange("k j t f -> k (j t f)"), start=True, stop=False,
                                         skip_group_check=True)
                            mm = e.matmul(pv[half][:, col * 2 * D:(col + 1) * 2 * D],
                                          zT[q][:, j * P:(j + 1) * P], W2[:, :],
                                          start=False, stop=False, skip_group_check=True)
                        mm.then_inc(s_used, 1)

                    def all_vectors(at):
                        turn_wait(e, s_got[at.b], at.half(32 * J, 32 * J))
                        for g in range(NG + 2):
                            if g < NG:
                                turned(at, g)
                            if 0 <= g - 1 < NG:
                                hidden(at, g - 1)
                            if 0 <= g - 2:
                                vectors(at, g - 2)

                    def step(at):
                        if at.k < NB - 1:
                            all_vectors(at.plus(1))
                        for j in range(J):
                            half, col = divmod(j, JH)
                            if col == 0:
                                turn_wait(e, s_lo, at.of(2, half + 1))
                            turn_wait(e, s_wide, at.of(J, j + 2))
                            for k, (lo, hi) in enumerate(halves):
                                mm = e.matmul(pacc[k][:, 0:(hi - lo) * D], hot_lo[half][:, col, :],
                                              wide[j % 2][:, lo:hi, :].rearrange("p c f -> p (c f)"),
                                              start=False, stop=False, skip_group_check=True)
                            mm.then_inc(s_acc, 1)

                    all_vectors(At(0))
                    walk(e, NB, step, head=2)

                @block.scalar
                def _(e):
                    e.wait_ge(s_one, 1)
                    for s in (s_gTc, s_zc, s_vc):
                        e.sem_inc(s, 2)

                    def low_digits(at, half):
                        if at.k > 0:
                            e.wait_ge(s_acc, at.of(J, (half + 1) * JH - J + 2))
                        for j in range(JH):
                            e.activation(hot_lo[half][:, j, :], iota_f[:, :], ACT.Square, scale=-1.0,
                                         bias=src_lo[:, bass.ds(at.of(J, half * JH + j), 1)]).then_inc(s_sq, 1)
                        e.wait_ge(s_sq, at.of(J, (half + 1) * JH))
                        e.activation(hot_lo[half][:, :, :], hot_lo[half][:, :, :], ACT.Relu, scale=-1.0,
                                     bias=ones[:, 0:1]).then_inc(s_lo, 1)

                    def copy_vectors(at, half):
                        e.wait_ge(s_used, at.of(NG, (NG // 2 + 1, NG)[half] + 2))
                        e.wait_ge(s_vfree, at.of(2, half + 1))
                        e.copy(vec[half].rearrange("p j t f -> p (j t f)"), pv[half][:, 0:JH * 2 * D]).then_inc(s_vc, 1)

                    def all_vectors(at):
                        for g in range(NG + 1):
                            if g < NG:
                                q = (at.b * NG + g) % 2
                                e.wait_ge(s_gT, at.of(NG, g + 1))
                                e.wait_ge(s_z, at.of(NG, g + 1))
                                e.copy(gT[q][0:2 * T2, :], pg[q][0:2 * T2, 0:2 * P]).then_inc(s_gTc, 1)
                            if g >= 1:
                                q = (at.b * NG + g - 1) % 2
                                e.wait_ge(s_z, at.of(NG, g + 2))
                                e.wait_ge(s_used, at.of(NG, g))
                                e.activation(zT[q][:, :], pz[q][:, 0:2 * P], ACT.Relu).then_inc(s_zc, 1)
                            if g == NG // 2 + 3:
                                copy_vectors(at, 0)
                        copy_vectors(at, 1)

                    def step(at):
                        low_digits(at, 0)
                        if at.k < NB - 1:
                            all_vectors(at.plus(1))
                        low_digits(at, 1)

                    all_vectors(At(0))
                    walk(e, NB, step, head=2)

                @block.vector
                def _(e):
                    ch = Chain(e, s_v)
                    ch.do(e.memset(Wz[:, :], 0.0))
                    ch.do(e.memset(W2[:, :], 0.0))
                    for t in gT + pacc:
                        ch.do(e.memset(t[:, :], 0.0))
                    ch.do(e.memset(run[1][:, J - 1, :], 0.0))
                    ch.sync()
                    e.sem_inc(s_one, 1)
                    e.sem_inc(s_vfree, 2)
                    e.sem_inc(s_wide, 1)
                    two = [P, JH, 2, D]

                    def high_digits(at, half):
                        hi = src_hi[:, bass.ds(at.of(J, half * JH), JH)]
                        ch.do(e.tensor_tensor(hot_hi[half][:, :, :], iota_f[:, None, 0:C].to_broadcast([P, JH, C]),
                                              hi[:, :, None].to_broadcast([P, JH, C]), ALU.is_equal))

                    def widen(at, j):
                        half, col = divmod(j, JH)
                        e.wait_ge(s_acc, at.of(J, j + 1))
                        e.tensor_tensor(wide[j % 2][:, :, :],
                                        msg[at.b][:, j, 1, :][:, None, :].to_broadcast([P, C, D]),
                                        hot_hi[half][:, col, :][:, :, None].to_broadcast([P, C, D]),
                                        ALU.mult).then_inc(s_wide, 1)

                    def messages(at, half):
                        g4 = got[at.b][:, half * JH:(half + 1) * JH, :, :]
                        xs, xd = g4[:, :, 0, 0:D], g4[:, :, 1, 0:D]
                        V = vec[half]
                        u, w = V[:, :, 0, :], V[:, :, 1, :]
                        m = msg[at.b][:, half * JH:(half + 1) * JH, :, :]

                        def both(t):
                            return t[:, :, None, :].to_broadcast(two)

                        def tt(out, in0, in1, op=ALU.mult):
                            return lambda: e.tensor_tensor(out, in0, in1, op)

                        uw = dots[:, :, 6]
                        return [
                            [tt(prod[:, :, 0:2, :], V[:, :, :, :], V[:, :, :, :]),
                             tt(prod[:, :, 2:4, :], V[:, :, :, :], both(xs)),
                             tt(prod[:, :, 4:6, :], V[:, :, :, :], both(xd)),
                             tt(prod[:, :, 6, :], u, w)],
                            [lambda: e.tensor_reduce(dots[:, :, :], prod[:, :, :, :], AX.X, ALU.add)],
                            [lambda: e.tensor_scalar(cc[:, :, :], dots[:, :, 0:2], 1e-24, 0.5, ALU.max, ALU.mult)],
                            [lambda: e.reciprocal(cc[:, :, :], cc[:, :, :])],
                            [tt(first[:, :, 0], cc[:, :, 0], dots[:, :, 2]), tt(first[:, :, 1], cc[:, :, 1], dots[:, :, 5])],
                            [tt(second[:, :, :], first[:, :, :], uw[:, :, None].to_broadcast([P, JH, 2]))],
                            [tt(second[:, :, :], dots[:, :, 3:5], second[:, :, :], ALU.subtract)],
                            [tt(second[:, :, 0], second[:, :, 0], cc[:, :, 1]), tt(second[:, :, 1], second[:, :, 1], cc[:, :, 0]),
                             tt(term[:, :, :, :], first[:, :, :, None].to_broadcast(two), V[:, :, :, :])],
                            [tt(m, g4[:, :, :, 0:D], term[:, :, :, :], ALU.subtract)],
                            [tt(term[:, :, 0, :], second[:, :, 0][:, :, None].to_broadcast([P, JH, D]), w),
                             tt(term[:, :, 1, :], second[:, :, 1][:, :, None].to_broadcast([P, JH, D]), u)],
                            [tt(m, m, term[:, :, :, :], ALU.subtract)],
                            [tt(m, m, g4[:, :, :, D:D + 1].to_broadcast(two))],
                        ]

                    def half_step(at, half, widened=True):
                        nxt = at.plus(1)
                        cols = list(range(half * JH, (half + 1) * JH)) if widened else []
                        if at.k < NB - 1:
                            if half == 0:
                                e.wait_ge(s_got[nxt.b], nxt.half(16 * 2 * J, 16 * 2 * J))
                            if cols:
                                widen(at, cols.pop(0))
                            e.wait_ge(s_vc, nxt.of(2, half + 3))
                            for level in messages(nxt, half):
                                for make in level:
                                    n = ch.do(make())
                                if cols:
                                    widen(at, cols.pop(0))
                                ch.wait(n)
                            e.sem_inc(s_vfree, 1)
                            if half == 1:
                                e.sem_inc(s_msg, 1)
                        for j in cols:
                            widen(at, j)

                    def step(at):
                        if at.k > 0:
                            e.wait_ge(s_wide, at.of(J, 1))
                        high_digits(at, 1)
                        half_step(at, 0)
                        if at.k < NB - 1:
                            e.wait_ge(s_wide, at.of(J, JH + 1))
                            high_digits(at.plus(1), 0)
                        half_step(at, 1)
                        e.wait_ge(s_kept[at.b], at.half(1, 1))
                        scan_block(e, ch, at.cols(), msg[at.b][:, :, 0, :], run[at.b], run[1 - at.b])
                        ch.tell(s_run[at.b])

                    high_digits(At(0), 0)
                    for half in range(2):
                        half_step(At(-1), half, widened=False)
                    walk(e, NB, step, ch, 2 * 19 + 2 + D, head=2)
                    e.wait_ge(s_acc, NB * J + 2)
                    for k, (lo, hi) in enumerate(halves):
                        ch.do(e.tensor_copy(from_src[:, lo:hi, :],
                                            pacc[k][:, 0:(hi - lo) * D].rearrange("p (c f) -> p c f", f=D)))
                    ch.sync()
            banks.close()
            node_sums(2, run[1][:, J - 1, :])
            s_n, = seml("n")
            with nc.Block() as block:
                @block.vector
                def _(e):
                    ch = Chain(e, s_n)
                    ch.to(e.tensor_tensor(agg[:, :, :], agg[:, :, :], from_src[:, :, :], ALU.add))
                    ch.to(e.tensor_tensor(agg[:, :, :], agg[:, :, :], bc_f(dis), ALU.mult))
                    ch.to(e.tensor_tensor(agg[:, :, :], agg[:, :, :], h[:, :, :], ALU.add))
                    ch.to(e.tensor_scalar(agg[:, :, :], agg[:, :, :], 0.0, None, ALU.max))
                    ch.to(e.tensor_tensor(x[:, :, :], x[:, :, :], agg[:, :, :], ALU.add))

        renew_semaphores()
        norm_and_table(3)
        c, sbl, psl, seml = stage("attn")
        CH = D * D
        OFF = 8
        with c:
            banks = ExitStack()
            S = [sbl(f"S{b}", [P, J3, S3]) for b in range(2)]
            Wc = sb("attn_Wc", [D + 1, 2 * CH], c=banks)
            idx = [sb(f"attn_idx{b}", [P, J3], I32, c=banks) for b in range(2)]
            eidx = [sb(f"attn_eidx{b}", [P, J3], I32, c=banks) for b in range(2)]
            got = [sb(f"attn_got{b}", [P, J3, D], c=banks) for b in range(2)]
            ef = [sb(f"attn_ef{b}", [D + 1, J3, P], c=banks) for b in range(2)]
            T = [sb(f"attn_T{b}", [P, J3, 2 * CH], c=banks) for b in range(2)]
            drop = sb("attn_drop", [P, CH], c=banks)
            scale = sb("attn_scale", [P, CH], c=banks)
            carried = sb("attn_carried", [P, 2 * CH], c=banks)
            pw = [ps(f"attn_w{q}", [P, 512], banks) for q in range(OFF)]
            s_w, s_v, s_one, s_col, s_t, s_e, s_x, s_state = seml("w", "v", "one", "col", "t", "e", "x", "state")
            s_idx, s_ef, s_got, s_sc = (seml(f"{n}0", f"{n}1") for n in ("idx", "ef", "got", "sc"))

            with nc.Block() as block:
                @block.sync
                def _(e):
                    for t, n in ((Wc[0:D, 0:CH], "L3_gnn_W_attn"), (Wc[0:D, CH:], "L3_gnn_W_msg"),
                                 (Wc[D:D + 1, 0:CH], "L3_gnn_b_attn"), (Wc[D:D + 1, CH:], "L3_gnn_b_msg")):
                        e.dma_start(t, a[n]).then_inc(s_w, 16)
                    e.wait_ge(s_one, 1)

                    def load(at):
                        e.dma_start(idx[at.b][:, :], a["src"][:, at.cols(J3)]).then_inc(s_idx[at.b], 16)
                        e.dma_start(ef[at.b][0:D, :, :], a["ef16"][:, at.cols(J3), :]).then_inc(s_ef[at.b], 16)

                    load(At(0))
                    load(At(1))
                    with e.Fori(0, NB3 // 2 - 1) as i:
                        for k in range(2):
                            e.wait_ge(s_t, At(k, i).of(J3, J3 + OFF))
                            load(At(k + 2, i))

                @block.gpsimd
                def _(e):
                    def gather(at):
                        turn_wait(e, s_idx[at.b], at.half(16, 16))
                        for j in range(J3):
                            e.indirect_dma_start(out=got[at.b][:, j, :], out_offset=None, in_=tab[3],
                                                 in_offset=indices(idx[at.b], j)).then_inc(s_got[at.b], 16)

                    def scatter(at):
                        turn_wait(e, s_state, at.of(1, 1))
                        for j in range(J3):
                            e.indirect_dma_start(out=state3, out_offset=indices(eidx[at.b], j),
                                                 in_=S[at.b][:, j, :], in_offset=None, bounds_check=NP - 1,
                                                 oob_is_err=False).then_inc(s_sc[at.b], 16)

                    gather(At(0))
                    gather(At(1))
                    gather(At(2))
                    with e.Fori(0, NB3 // 2 - 2) as i:
                        for k in range(2):
                            gather(At(k + 3, i))
                            scatter(At(k, i))
                    gather(At(NB3 - 1))
                    for k in range(NB3 - 4, NB3):
                        scatter(At(k))
                    for b in range(2):
                        e.wait_ge(s_sc[b], 16 * J3 * (NB3 // 2))

                @block.tensor
                def _(e):
                    e.wait_ge(s_w, 64)
                    with e.Fori(0, NB3 // 2) as i:
                        for b in range(2):
                            turn_wait(e, s_ef[b], i * 16 + 16)
                            for j in range(J3):
                                k = b * J3 + j
                                turn_wait(e, s_t, i * (2 * J3) + bank_free(k, OFF, 2 * J3))
                                e.matmul(pw[k % OFF][:, :], ef[b][:, j, :], Wc[:, :], start=True, stop=True).then_inc(s_col, 1)

                @block.scalar
                def _(e):
                    def exps(at):
                        e.wait_ge(s_e, at.of(1, 1))
                        e.activation(S[at.b][:, :, CH:2 * CH], T[at.b][:, :, 0:CH], ACT.Exp).then_inc(s_x, 1)
                        e.activation(scale[:, :], drop[:, :], ACT.Exp).then_inc(s_x, 1)

                    walk(e, NB3, exps, head=2)

                @block.vector
                def _(e):
                    ch = Chain(e, s_v)
                    for b in range(2):
                        ch.do(e.memset(ef[b][:, :, :], 1.0))
                    ch.do(e.memset(S[1][:, J3 - 1, 0:CH], -BIG))
                    ch.do(e.memset(S[1][:, J3 - 1, CH:], 0.0))
                    ch.tell(s_one)
                    e.sem_inc(s_t, OFF)

                    def edge(at, j):
                        if j == 0:
                            e.wait_ge(s_got[at.b], at.half(16 * J3, 16 * J3))
                        e.wait_ge(s_col, at.of(J3, j + 1))
                        e.tensor_tensor(T[at.b][:, j, :].rearrange("p (m i o) -> p m i o", m=2, i=D),
                                        pw[(at.b * J3 + j) % OFF][:, :].rearrange("p (m i o) -> p m i o", m=2, i=D),
                                        got[at.b][:, j, :][:, None, :, None].to_broadcast([P, 2, D, D]),
                                        ALU.mult).then_inc(s_t, 1)

                    def sums(at, j):
                        Sb = S[at.b]
                        return ch.do(e.scalar_tensor_tensor(
                            out=Sb[:, j, CH:], in0=carried[:, :] if j == 0 else Sb[:, j - 1, CH:],
                            scalar=same[:, bass.ds(at.of(J3, j), 1)], in1=Sb[:, j, CH:], op0=ALU.mult, op1=ALU.add))

                    def a_block(at):
                        Sb, Tb, So = S[at.b], T[at.b], S[1 - at.b]
                        prev, first, last = at.plus(-1), at.k == 0, at.k == NB3 - 1
                        e.wait_ge(s_t, at.of(J3, J3 + OFF))
                        if at.k >= 2:
                            e.wait_ge(s_sc[at.b], at.half(16 * J3, 0))
                        s_prev = None
                        for j in range(J3):
                            m_now = ch.do(e.scalar_tensor_tensor(
                                out=Sb[:, j, 0:CH], in0=So[:, J3 - 1, 0:CH] if j == 0 else Sb[:, j - 1, 0:CH],
                                scalar=apart[:, bass.ds(at.of(J3, j), 1)], in1=Tb[:, j, 0:CH], op0=ALU.add, op1=ALU.max))
                            if not first:
                                if s_prev:
                                    ch.wait(s_prev)
                                s_prev = sums(prev, j)
                            ch.wait(m_now)
                        if not first:
                            ch.tell(s_state)
                        early = 0 if last else J3 // 2
                        for j in range(J3 - 2, -1, -1):
                            m_now = ch.do(e.scalar_tensor_tensor(
                                out=Sb[:, j, 0:CH], in0=Sb[:, j + 1, 0:CH], scalar=apart[:, bass.ds(at.of(J3, j + 1), 1)],
                                in1=Sb[:, j, 0:CH], op0=ALU.add, op1=ALU.max))
                            if J3 - 2 - j < early:
                                edge(at.plus(1), J3 - 2 - j)
                            ch.wait(m_now)
                        ch.do(e.tensor_copy(eidx[at.b][:, :], end_to[:, at.cols(J3)]))
                        ch.do(e.tensor_tensor(Tb[:, :, 0:CH], Tb[:, :, 0:CH], Sb[:, :, 0:CH], ALU.subtract))
                        ch.to(e.tensor_tensor(drop[:, :], So[:, J3 - 1, 0:CH], Sb[:, 0, 0:CH], ALU.subtract))
                        ch.do(e.tensor_scalar(drop[:, :], drop[:, :], 0.0, None, ALU.min))
                        ch.tell(s_e)
                        if not last:
                            for j in range(early, J3):
                                edge(at.plus(1), j)
                        e.wait_ge(s_x, at.of(2, 2))
                        ch.do(e.tensor_tensor(Sb[:, :, 2 * CH:], Tb[:, :, CH:], Sb[:, :, CH:2 * CH], ALU.mult))
                        ch.do(e.tensor_tensor(carried[:, :].rearrange("p (t c) -> p t c", t=2),
                                              So[:, J3 - 1, CH:].rearrange("p (t c) -> p t c", t=2),
                                              scale[:, None, :].to_broadcast([P, 2, CH]), ALU.mult))
                        ch.sync()

                    for j in range(J3):
                        edge(At(0), j)
                    walk(e, NB3, a_block, ch, 3 * J3 - 1 + 4 + 2, head=2)
                    for j in range(J3):
                        sums(At(NB3 - 1), j)
                        ch.sync()
                    ch.tell(s_state)
            banks.close()

            TT = sbl("TT", [P, 6, P])
            Mx = sbl("Mx", [P, 2, P])
            ea, eb = sbl("ea", [P, 2, P]), sbl("eb", [P, 2, P])
            apT = sbl("apT", [P, P])
            sh = sbl("sh", [P, 6, P])
            cin = sbl("cin", [P, S3])
            own = sbl("own", [P, S3])
            top = sbl("top", [P, CH])
            e1, e2 = sbl("e1", [P, CH]), sbl("e2", [P, CH])
            last_state = S[1][:, J3 - 1, :]
            pT, pB = psl("turn0"), psl("turn1")
            pC, pD = psl("back0"), psl("back1")
            s_u, s_pt, s_d, s_ex, s_sh, s_pb, s_own, s_mrg, s_put = seml("u", "pt", "d", "ex", "sh", "pb", "own", "mrg", "put")
            with nc.Block() as block:
                @block.tensor
                def _(e):
                    for k in range(6):
                        e.transpose((pT, pB)[k // 4][:, k % 4 * P:(k % 4 + 1) * P],
                                    last_state[:, k * P:(k + 1) * P], ident[:, :]).then_inc(s_pt, 1)
                    e.wait_ge(s_sh, 1)
                    for k in range(6):
                        e.transpose((pC, pD)[k // 4][:, k % 4 * P:(k % 4 + 1) * P], sh[:, k, :], ident[:, :]).then_inc(s_pb, 1)

                @block.gpsimd
                def _(e):
                    e.indirect_dma_start(out=own[:, :], out_offset=None, in_=state3,
                                         in_offset=indices(first_node, 0)).then_inc(s_own, 16)
                    e.wait_ge(s_own, 16)
                    e.wait_ge(s_mrg, 1)
                    e.indirect_dma_start(out=state3, out_offset=indices(carry_to, 0), in_=own[:, :],
                                         in_offset=None, bounds_check=NP - 1, oob_is_err=False).then_inc(s_put, 16)
                    e.wait_ge(s_put, 16)

                @block.scalar
                def _(e):
                    e.wait_ge(s_d, 1)
                    e.activation(ea[:, :, :], ea[:, :, :], ACT.Exp).then_inc(s_ex, 1)
                    e.activation(eb[:, :, :], eb[:, :, :], ACT.Exp).then_inc(s_ex, 1)
                    e.wait_ge(s_d, 2)
                    e.activation(e1[:, :], e1[:, :], ACT.Exp).then_inc(s_ex, 1)
                    e.activation(e2[:, :], e2[:, :], ACT.Exp).then_inc(s_ex, 1)

                @block.vector
                def _(e):
                    ch = Chain(e, s_u)
                    ch.do(e.tensor_scalar(apT[:, :], through[:, :], BIG, -BIG, ALU.mult, ALU.add))
                    ch.do(e.memset(sh[:, 0:2, 0:1], -BIG))
                    ch.do(e.memset(sh[:, 2:6, 0:1], 0.0))
                    ch.do(e.memset(ea[:, :, 0:1], 0.0))
                    e.wait_ge(s_pt, 6)
                    ch.do(e.tensor_copy(TT[:, 0:4, :].rearrange("p k n -> p (k n)"), pT[:, :]))
                    ch.to(e.tensor_copy(TT[:, 4:6, :].rearrange("p k n -> p (k n)"), pB[:, 0:2 * P]))
                    for k in range(2):
                        ch.do(e.tensor_tensor_scan(Mx[:, k, :], apT[:, :], TT[:, k, :], -BIG, ALU.add, ALU.max))
                    ch.sync()
                    ch.do(e.tensor_tensor(ea[:, :, 1:P], Mx[:, :, 0:P - 1], Mx[:, :, 1:P], ALU.subtract))
                    ch.do(e.tensor_tensor(eb[:, :, :], TT[:, 0:2, :], Mx[:, :, :], ALU.subtract))
                    ch.sync()
                    ch.do(e.tensor_scalar(ea[:, :, :], ea[:, :, :], 0.0, None, ALU.min))
                    ch.tell(s_d)
                    e.wait_ge(s_ex, 2)
                    ch.do(e.tensor_tensor(ea[:, :, :], ea[:, :, :],
                                          through[:, None, :].to_broadcast([P, 2, P]), ALU.mult))
                    for t in range(2):
                        ch.do(e.tensor_tensor(TT[:, 2 + 2 * t:4 + 2 * t, :], TT[:, 2 + 2 * t:4 + 2 * t, :], eb[:, :, :], ALU.mult))
                    ch.sync()
                    ch.do(e.tensor_copy(sh[:, 0:2, 1:P], Mx[:, :, 0:P - 1]))
                    for k in range(2, 6):
                        ch.do(e.tensor_tensor_scan(sh[:, k, 1:P], ea[:, k % 2, 0:P - 1], TT[:, k, 0:P - 1], 0.0,
                                                   ALU.mult, ALU.add))
                    ch.tell(s_sh)
                    e.wait_ge(s_pb, 6)
                    ch.do(e.tensor_copy(cin[:, 0:4 * P], pC[:, :]))
                    ch.to(e.tensor_copy(cin[:, 4 * P:], pD[:, 0:2 * P]))
                    e.wait_ge(s_own, 16)
                    ch.to(e.tensor_tensor(top[:, :], cin[:, 0:CH], own[:, 0:CH], ALU.max))
                    ch.do(e.tensor_tensor(e1[:, :], own[:, 0:CH], top[:, :], ALU.subtract))
                    ch.do(e.tensor_tensor(e2[:, :], cin[:, 0:CH], top[:, :], ALU.subtract))
                    ch.tell(s_d)
                    e.wait_ge(s_ex, 4)
                    for t in (1, 2):
                        ch.do(e.tensor_tensor(own[:, t * CH:(t + 1) * CH], own[:, t * CH:(t + 1) * CH], e1[:, :], ALU.mult))
                        ch.do(e.tensor_tensor(cin[:, t * CH:(t + 1) * CH], cin[:, t * CH:(t + 1) * CH], e2[:, :], ALU.mult))
                    ch.sync()
                    ch.do(e.tensor_tensor(own[:, CH:], own[:, CH:], cin[:, CH:], ALU.add))
                    ch.do(e.tensor_copy(own[:, 0:CH], top[:, :]))
                    ch.tell(s_mrg)

        c, sbl, psl, seml = stage("attn_nodes")
        with c:
            G = 7
            st = [sbl(f"st{q}", [P, G, 2 * CH]) for q in range(2)]
            s_v, s_ld0, s_ld1, s_done = seml("v", "ld0", "ld1", "done")
            s_ld = (s_ld0, s_ld1)
            rows = by_node(state3)
            with nc.Block() as block:
                @block.sync
                def _(e):
                    for k in range(C // G):
                        if k >= 2:
                            e.wait_ge(s_done, k - 1)
                        e.dma_start(st[k % 2][:, :, :], rows[:, k * G:(k + 1) * G, CH:]).then_inc(s_ld[k % 2], 16)

                @block.vector
                def _(e):
                    ch = Chain(e, s_v)
                    for k in range(C // G):
                        e.wait_ge(s_ld[k % 2], 16 * (k // 2 + 1))
                        den, num = st[k % 2][:, :, 0:CH], st[k % 2][:, :, CH:]
                        ch.to(e.tensor_scalar(den, den, 1e-30, None, ALU.max))
                        ch.to(e.reciprocal(den, den))
                        ch.to(e.tensor_tensor(num, num, den, ALU.mult))
                        ch.to(e.tensor_reduce(agg[:, k * G:(k + 1) * G, :],
                                              num.rearrange("p g (i o) -> p g o i", i=D), AX.X, ALU.add))
                        e.sem_inc(s_done, 1)
                    ch.to(e.tensor_tensor(x[:, :, :], x[:, :, :], agg[:, :, :], ALU.add))

        c, sbl, psl, seml = stage("store")
        s_out, = seml("out")
        with nc.Block() as block:
            @block.sync
            def _(e):
                e.dma_start(out, x[:, :, :]).then_inc(s_out, 16)
                e.wait_ge(s_out, 16)


_WEIGHTS = ["L0_gnn_W_gcn", "L0_gnn_W1", "L0_gnn_W2", "L1_gnn_W1", "L1_gnn_W2", "L3_gnn_W_msg", "L3_gnn_W_attn"]
_COLUMNS = ["L0_gnn_b1"]
_ROWS = ["L0_gnn_b2", "L1_gnn_b1", "L1_gnn_b2", "L1_gnn_bias", "L1_gnn_gamma", "L1_gnn_beta", "L2_gnn_b1",
         "L2_gnn_b2", "L3_gnn_b_msg", "L3_gnn_b_attn"]


def kernel(**inputs):
    import numpy as np
    import concourse.bacc as bacc
    from concourse.bass_utils import run_bass_kernel_spmd

    got = {k: np.asarray(v) for k, v in inputs.items()}
    pad = P * L - E

    def edges(v):
        v = np.concatenate([v, np.zeros((pad, v.shape[1]), v.dtype)])
        return np.ascontiguousarray(v.reshape(P, L, -1).transpose(2, 1, 0))

    src = np.concatenate([got["src"], np.full(pad, NP - 1, np.int32)])
    dst = np.concatenate([[-1], got["dst"], np.full(pad, NP - 1), [-1]]).astype(np.int32)
    nodes = np.concatenate([got["x"], np.zeros((NP - N, D), np.float32)])
    arrays = {
        "x": np.ascontiguousarray(nodes.reshape(C, P, D).transpose(1, 0, 2)),
        "src": src.reshape(P, L),
        "dst": np.stack([dst[p * L:p * L + L + 2] for p in range(P)]),
        "ef16": edges(got["edge_attr_16"]),
        "ef6": edges(got["edge_attr_6"]),
        "L2_W1T": np.ascontiguousarray(got["L2_gnn_W1"].T),
        "L2_W2T": np.ascontiguousarray(got["L2_gnn_W2"].T),
    }
    arrays.update({k: got[k] for k in _WEIGHTS})
    arrays.update({k: got[k].reshape(-1, 1) for k in _COLUMNS})
    arrays.update({k: got[k].reshape(1, -1) for k in _ROWS})
    nc = bacc.Bacc("TRN2", target_bir_lowering=False, num_devices=1)
    a = {k: nc.dram_tensor(f"in_{k}", v.shape, mybir.dt.from_np(v.dtype), kind="ExternalInput").ap()
         for k, v in arrays.items()}
    out = nc.dram_tensor("out_x", (P, C, D), F32, kind="ExternalOutput").ap()
    gnn_kernel(nc, a, out)
    r = run_bass_kernel_spmd(nc, [{f"in_{k}": v for k, v in arrays.items()}], core_ids=[0])
    res = r.results[0]["out_x"]
    return np.ascontiguousarray(res.transpose(1, 0, 2).reshape(NP, D)[:N])
```

```python
from contextlib import ExitStack

import concourse.bass as bass
from concourse import mybir
from concourse.alu_op_type import AluOpType as ALU

F32 = mybir.dt.float32
BF16 = mybir.dt.bfloat16
I32 = mybir.dt.int32
ACT = mybir.ActivationFunctionType
AX = mybir.AxisListType

P = 128
N = 6250
C = -(-N // P)
NP = C * P
E = 206250
L = -(-E // P)
D = 16
J = 26
NB = L // J
J3 = 13
NB3 = L // J3
T2 = 18
S3 = 3 * 256
BIG = 1e30
SKIP = 8192
SKIP_EDGE = 1 << 18
EPS = 1e-5
assert NB * J == L and NB % 2 == 0 and NB3 * J3 == L and NB3 % 2 == 0


class Chain:

    def __init__(self, eng, sem):
        self.eng, self.sem, self.n, self.base = eng, sem, 0, 0

    def do(self, ins):
        ins.then_inc(self.sem, 1)
        self.n += 1
        return self.n

    def wait(self, n):
        self.eng.wait_ge(self.sem, self.base + n)

    def sync(self):
        self.eng.wait_ge(self.sem, self.base + self.n)

    def to(self, ins):
        self.do(ins)
        self.sync()

    def tell(self, sem):
        self.sync()
        self.eng.sem_inc(sem, 1)

    def loop(self, i, per):
        self.start, self.per, self.base = self.n, per, i * per

    def end(self, turns):
        assert self.n - self.start == self.per, (self.n - self.start, self.per)
        self.n, self.base = self.start + turns * self.per, 0


def gnn_kernel(nc, a, out):
    ctx = ExitStack()

    def sb(name, shape, dt=F32, c=ctx):
        return c.enter_context(nc.sbuf_tensor(name, shape, dt))

    def ps(name, shape, c, dt=F32):
        return c.enter_context(nc.psum_tensor(name, shape, dt))

    def sem(name, c=ctx):
        return c.enter_context(nc.semaphore(name))

    def dram(name, shape):
        return nc.dram_tensor(name, shape, F32, kind="Internal").ap()

    tab = [dram(f"tab{k}", (NP, T2 if k == 2 else D)) for k in range(4)]
    runs = [dram(f"runs{k}", (P * L, D)) for k in range(3)]
    corr = [dram(f"corr{k}", (NP, D)) for k in range(3)]
    starts = dram("starts", (P * L, T2))
    state3 = dram("state3", (NP, S3))

    with ctx:
        ident = sb("ident", [P, P])
        tri = sb("tri", [P, P])
        ones = sb("ones", [P, P])
        iota_f = sb("iota_f", [P, P])
        iota_b = sb("iota_b", [P, P], BF16)
        x = sb("x", [P, C, D])
        h = sb("h", [P, C, D])
        agg = sb("agg", [P, C, D])
        tmp = sb("tmp", [P, C, D])
        same = sb("same", [P, L])
        apart = sb("apart", [P, L])
        end_to = sb("end_to", [P, L], I32)
        src_lo = sb("src_lo", [P, L])
        src_hi = sb("src_hi", [P, L])
        cnt_d = sb("cnt_d", [P, C])
        full = sb("full", [P, C])
        real = sb("real", [P, C])
        dinv = sb("dinv", [P, C])
        dis = sb("dis", [P, C])
        v1 = sb("v1", [P, C])
        v2 = sb("v2", [P, C])
        last_edge = sb("last_edge", [P, C], I32)
        first_edge = sb("first_edge", [P, C], I32)
        run_start = sb("run_start", [P, 1], I32)
        through = sb("through", [P, P])
        carry_to = sb("carry_to", [P, 1], I32)
        first_node = sb("first_node", [P, 1], I32)
        eps = sb("eps", [P, 1])

        def bc_f(t):
            return t[:, :, None].to_broadcast([P, C, D])

        def flat(t):
            return t.rearrange("p c f -> p (c f)")

        def by_node(t):
            return t.rearrange("(c p) f -> p c f", p=P)

        def stage(name):
            c = ExitStack()
            return (c, lambda n, s, dt=F32: sb(f"{name}_{n}", s, dt, c),
                    lambda n: ps(f"{name}_{n}", [P, 512], c),
                    lambda *names: [semaphore(name, n) for n in names])

        by_indirect = {"got0", "got1", "got_a0", "got_a1", "got_b0", "got_b1", "sc0", "sc1", "cd", "g", "begin", "at",
                       "own", "put"}

        def semaphore(name, n):
            if n in by_indirect:
                return sem(f"{name}_{n}")
            used.append(sem(f"{name}_{n}", sems))
            return used[-1]

        used, sems = [], ExitStack()

        def renew_semaphores():
            with nc.Block() as block:
                @block.gpsimd
                def _(e):
                    for s in used:
                        e.sem_clear(s)
            sems.close()
            used.clear()

        def block_cols(i, b):
            return bass.ds(i * (2 * J) + b * J, J)

        def one_hot(e, to, digit, cols, w):
            return e.tensor_tensor(to, iota_b[:, None, 0:w].to_broadcast([P, J, w]),
                                   digit[:, cols][:, :, None].to_broadcast([P, J, w]), ALU.is_equal)

        def count(e, to, digits):
            for j in range(J):
                mm = e.matmul(to[:, 0:C], digits[:, j, 0:P], digits[:, j, P:P + C],
                              start=False, stop=False, skip_group_check=True)
            return mm

        class At:

            def __init__(self, k, i=None):
                self.k, self.i, self.b = k, i, k % 2

            def of(self, per, more):
                return self.k * per + more if self.i is None else self.i * (2 * per) + (self.k * per + more)

            def half(self, per, more):
                return self.k // 2 * per + more if self.i is None else self.i * per + (self.k // 2 * per + more)

            def cols(self, size=J, more=0):
                return bass.ds(self.of(size, more), size)

            def plus(self, d):
                return At(self.k + d, self.i)

        def walk(e, n, step, ch=None, per=0, head=0, tail=2):
            for k in range(head):
                step(At(k))
            with e.Fori(0, (n - head - tail) // 2) as i:
                if ch:
                    ch.loop(i, 2 * per)
                step(At(head, i))
                step(At(head + 1, i))
            if ch:
                ch.end((n - head - tail) // 2)
            for k in range(n - tail, n):
                step(At(k))

        def bank_free(k, banks, per):
            last = k - banks if k >= banks else max(q for q in range(per) if q % banks == k) - per
            return last + 1 + banks

        c, sbl, psl, seml = stage("prep")
        with c:
            dstw = sbl("dstw", [P, L + 2], I32)
            dstf = sbl("dstf", [P, L + 2])
            srci = sbl("srci", [P, L], I32)
            ti = sbl("ti", [P, L], I32)
            nxt = sbl("nxt", [P, L])
            dst_lo = sbl("dst_lo", [P, L])
            dst_hi = sbl("dst_hi", [P, L])
            iota_i = sbl("iota_i", [P, P], I32)
            node_i = sbl("node_i", [P, C], I32)
            node_f = sbl("node_f", [P, C])
            zero = sbl("zero", [P, 7 * S3])
            digits = [sbl(f"digits{b}", [P, J, P + C], BF16) for b in range(2)]
            f1, f2, f3, f4 = (sbl(f"f{k}", [P, 1]) for k in range(1, 5))
            diag = sbl("diag", [P, P])
            col_total = sbl("col_total", [P, C])
            onec = sbl("onec", [P, C])
            pcnt = psl("cnt")
            pthr, pcum, ptot = (psl(n) for n in ("thr", "cum", "tot"))
            s_in, s_zero, s_zd, s_pool, s_clear, s_v, s_mm, s_dig = seml(
                "in", "zero", "zd", "pool", "clear", "v", "mm", "dig")
            s_diag, s_thr, s_cnt, s_cum, s_deg, s_sqrt = seml("diag", "thr", "cnt", "cum", "deg", "sqrt")
            with nc.Block() as block:
                @block.sync
                def _(e):
                    e.dma_start(dstw[:, :], a["dst"]).then_inc(s_in, 16)
                    e.dma_start(srci[:, :], a["src"]).then_inc(s_in, 16)
                    e.dma_start(x[:, :, :], a["x"]).then_inc(s_in, 16)
                    e.wait_ge(s_zero, 1)
                    for t in corr:
                        e.dma_start(t.rearrange("(p c) f -> p (c f)", p=P), zero[:, 0:C * D]).then_inc(s_zd, 16)
                    st = state3.rearrange("(p c) f -> p (c f)", p=P)
                    for k in range(C // 7):
                        e.dma_start(st[:, k * 7 * S3:(k + 1) * 7 * S3], zero[:, :]).then_inc(s_zd, 16)
                    part = L * T2 // 6
                    sr = starts.rearrange("(p l) f -> p (l f)", p=P)
                    for k in range(6):
                        e.dma_start(sr[:, k * part:(k + 1) * part], zero[:, 0:part]).then_inc(s_zd, 16)
                    e.wait_ge(s_zd, 16 * (3 + C // 7 + 6))
                    e.wait_ge(s_in, 48)

                @block.gpsimd
                def _(e):
                    ch = Chain(e, s_pool)
                    ch.do(e.iota(iota_i[:, :], pattern=[[1, P]], base=0, channel_multiplier=0))
                    ch.do(e.iota(node_i[:, :], pattern=[[P, C]], base=0, channel_multiplier=1))
                    ch.do(e.iota(run_start[:, :], pattern=[[0, 1]], base=0, channel_multiplier=L))
                    ch.to(e.memset(ones[:, :], 1.0))
                    ch.do(e.affine_select(out=ident[:, :], in_=ones[:, :], compare_op=ALU.is_equal, fill=0.0,
                                          base=0, pattern=[[-1, P]], channel_multiplier=1))
                    ch.do(e.affine_select(out=tri[:, :], in_=ones[:, :], compare_op=ALU.is_ge, fill=0.0,
                                          base=0, pattern=[[1, P]], channel_multiplier=-1))

                @block.vector
                def _(e):
                    e.memset(zero[:, :], 0.0).then_inc(s_zero, 1)
                    ch = Chain(e, s_v)
                    ch.do(e.memset(pcnt[:, 0:C], 0.0))
                    ch.tell(s_clear)
                    ch.do(e.memset(onec[:, :], 1.0))
                    ch.do(e.memset(eps[:, :], EPS))
                    e.wait_ge(s_pool, 6)
                    ch.do(e.tensor_copy(iota_f[:, :], iota_i[:, :]))
                    ch.do(e.tensor_copy(iota_b[:, :], iota_i[:, :]))
                    ch.do(e.tensor_copy(node_f[:, :], node_i[:, :]))
                    e.wait_ge(s_in, 48)
                    ch.do(e.tensor_copy(dstf[:, :], dstw[:, :]))
                    for ids, lo, hi in ((dstw[:, 1:L + 1], dst_lo, dst_hi), (srci[:, :], src_lo, src_hi)):
                        ch.to(e.tensor_scalar(ti[:, :], ids, 127, None, ALU.bitwise_and))
                        ch.to(e.tensor_copy(lo[:, :], ti[:, :]))
                        ch.to(e.tensor_scalar(ti[:, :], ids, 7, None, ALU.arith_shift_right))
                        ch.to(e.tensor_copy(hi[:, :], ti[:, :]))
                    ch.do(e.tensor_tensor(same[:, 1:L], dstf[:, 2:L + 1], dstf[:, 1:L], ALU.is_equal))
                    ch.do(e.memset(same[:, 0:1], 0.0))
                    ch.sync()
                    ch.do(e.tensor_scalar(apart[:, :], same[:, :], BIG, -BIG, ALU.mult, ALU.add))
                    ch.to(e.tensor_tensor(nxt[:, :], dstf[:, 2:L + 2], dstf[:, 1:L + 1], ALU.is_equal))
                    ch.to(e.tensor_scalar(nxt[:, :], nxt[:, :], float(SKIP), None, ALU.mult))
                    ch.to(e.tensor_tensor(nxt[:, :], nxt[:, :], dstf[:, 1:L + 1], ALU.add))
                    ch.do(e.tensor_copy(end_to[:, :], nxt[:, :]))
                    ch.do(e.tensor_scalar(real[:, :], node_f[:, :], float(N), None, ALU.is_lt))
                    ch.do(e.tensor_tensor(f1[:, :], dstf[:, 1:2], dstf[:, L:L + 1], ALU.is_equal))
                    ch.do(e.tensor_tensor(f2[:, :], dstf[:, 0:1], dstf[:, 1:2], ALU.is_equal))
                    ch.do(e.tensor_tensor(f3[:, :], dstf[:, L:L + 1], dstf[:, L + 1:L + 2], ALU.is_equal))
                    ch.sync()
                    ch.to(e.tensor_tensor(f4[:, :], f1[:, :], f2[:, :], ALU.mult))
                    ch.do(e.tensor_scalar(diag[:, :], ident[:, :], f4[:, 0:1], None, ALU.mult))
                    ch.tell(s_diag)
                    ch.to(e.tensor_tensor(f1[:, :], f1[:, :], f3[:, :], ALU.mult))
                    ch.to(e.tensor_scalar(f1[:, :], f1[:, :], -1.0, 1.0, ALU.mult, ALU.add))
                    ch.to(e.tensor_tensor(f2[:, :], f2[:, :], f1[:, :], ALU.mult))
                    ch.to(e.tensor_scalar(f2[:, :], f2[:, :], -float(SKIP), float(SKIP), ALU.mult, ALU.add))
                    ch.to(e.tensor_tensor(f2[:, :], f2[:, :], dstf[:, 1:2], ALU.add))
                    ch.do(e.tensor_copy(carry_to[:, :], f2[:, :]))
                    ch.do(e.tensor_copy(first_node[:, :], dstf[:, 1:2]))
                    ch.sync()
                    with e.Fori(0, NB // 2) as i:
                        for b in range(2):
                            e.wait_ge(s_mm, i * 2 + (b + 1))
                            one_hot(e, digits[b][:, :, 0:P], dst_lo, block_cols(i, b), P).then_inc(s_dig, 1)
                            one_hot(e, digits[b][:, :, P:], dst_hi, block_cols(i, b), C).then_inc(s_dig, 1)
                    e.wait_ge(s_cnt, 1)
                    ch.do(e.tensor_copy(cnt_d[:, :], pcnt[:, 0:C]))
                    ch.tell(s_deg)
                    ch.do(e.tensor_scalar(v1[:, :], cnt_d[:, :], 1.0, None, ALU.add))
                    ch.do(e.tensor_scalar(full[:, :], cnt_d[:, :], 0.5, None, ALU.is_ge))
                    ch.tell(s_deg)
                    e.wait_ge(s_thr, 1)
                    ch.do(e.tensor_copy(through[:, :], pthr[:, 0:P]))
                    e.wait_ge(s_sqrt, 1)
                    ch.do(e.reciprocal(dinv[:, :], dinv[:, :]))
                    e.wait_ge(s_cum, 1)
                    ch.to(e.tensor_copy(col_total[:, :], ptot[:, 0:C]))
                    ch.to(e.tensor_tensor_scan(v1[:, :], onec[:, :], col_total[:, :], 0.0, ALU.mult, ALU.add))
                    ch.to(e.tensor_tensor(v1[:, :], v1[:, :], col_total[:, :], ALU.subtract))
                    ch.to(e.tensor_tensor(v1[:, :], v1[:, :], pcum[:, 0:C], ALU.add))
                    ch.do(e.tensor_tensor(v2[:, :], v1[:, :], cnt_d[:, :], ALU.subtract))
                    ch.to(e.tensor_scalar(onec[:, :], full[:, :], -float(SKIP_EDGE), float(SKIP_EDGE), ALU.mult, ALU.add))
                    ch.to(e.tensor_tensor(v2[:, :], v2[:, :], onec[:, :], ALU.add))
                    ch.do(e.tensor_copy(first_edge[:, :], v2[:, :]))
                    ch.to(e.tensor_scalar(v1[:, :], v1[:, :], -1.0, 0.0, ALU.add, ALU.max))
                    ch.to(e.tensor_copy(last_edge[:, :], v1[:, :]))

                @block.tensor
                def _(e):
                    e.wait_ge(s_pool, 6)
                    e.wait_ge(s_clear, 1)
                    e.sem_inc(s_mm, 2)
                    with e.Fori(0, NB // 2) as i:
                        for b in range(2):
                            e.wait_ge(s_dig, i * 4 + (2 * b + 2))
                            count(e, pcnt, digits[b]).then_inc(s_mm, 1)
                    e.wait_ge(s_mm, NB + 2)
                    e.sem_inc(s_cnt, 1)
                    e.wait_ge(s_diag, 1)
                    e.matmul(pthr[:, 0:P], ones[:, :], diag[:, :], start=True, stop=True).then_inc(s_thr, 1)
                    e.wait_ge(s_deg, 1)
                    e.matmul(pcum[:, 0:C], tri[:, :], cnt_d[:, :], start=True, stop=True)
                    e.matmul(ptot[:, 0:C], ones[:, :], cnt_d[:, :], start=True, stop=True).then_inc(s_cum, 1)

                @block.scalar
                def _(e):
                    e.wait_ge(s_deg, 2)
                    e.activation(dinv[:, :], v1[:, :], ACT.Sqrt).then_inc(s_sqrt, 1)

        def norm_and_table(k):
            c, sbl, psl, seml = stage(f"norm{k}")
            with c:
                row = sbl("row", [P, C, T2]) if k == 2 else tmp if k == 0 else h
                s_v, s_var, s_std, s_row, s_tab, s_begin, s_at = seml("v", "var", "std", "row", "tab", "begin", "at")
                at_run = sbl("at_run", [P, T2])
                with nc.Block() as block:
                    @block.vector
                    def _(e):
                        ch = Chain(e, s_v)
                        ch.to(e.tensor_reduce(v1[:, :], x[:, :, :], AX.X, ALU.add))
                        ch.to(e.tensor_scalar(v1[:, :], v1[:, :], 1.0 / D, None, ALU.mult))
                        ch.to(e.tensor_tensor(tmp[:, :, :], x[:, :, :], bc_f(v1), ALU.subtract))
                        ch.to(e.tensor_tensor(h[:, :, :], tmp[:, :, :], tmp[:, :, :], ALU.mult))
                        ch.to(e.tensor_reduce(v2[:, :], h[:, :, :], AX.X, ALU.add))
                        ch.tell(s_var)
                        e.wait_ge(s_std, 1)
                        ch.to(e.reciprocal(v1[:, :], v1[:, :]))
                        ch.to(e.tensor_tensor(tmp[:, :, :], tmp[:, :, :], bc_f(v1), ALU.mult))
                        ch.to(e.tensor_scalar(h[:, :, :], tmp[:, :, :], 0.0, None, ALU.max))
                        if k == 0:
                            ch.do(e.tensor_tensor(row[:, :, :], h[:, :, :], bc_f(dinv), ALU.mult))
                        if k == 2:
                            ch.do(e.tensor_copy(row[:, :, 0:D], h[:, :, :]))
                            ch.do(e.tensor_copy(row[:, :, D:D + 1], dis[:, :, None]))
                            ch.do(e.memset(row[:, :, D + 1:T2], 1.0))
                        ch.tell(s_row)

                    @block.scalar
                    def _(e):
                        e.wait_ge(s_var, 1)
                        e.activation(v1[:, :], v2[:, :], ACT.Sqrt, bias=eps[:, 0:1], scale=1.0 / D).then_inc(s_std, 1)

                    if k == 2:
                        @block.gpsimd
                        def _(e):
                            e.wait_ge(s_row, 1)
                            for q in range(C):
                                e.indirect_dma_start(out=starts, out_offset=indices(first_edge, q), in_=row[:, q, :],
                                                     in_offset=None, bounds_check=P * L - 1,
                                                     oob_is_err=False).then_inc(s_begin, 16)
                            e.wait_ge(s_tab, 16)
                            e.indirect_dma_start(out=at_run[:, :], out_offset=None, in_=tab[2],
                                                 in_offset=indices(first_node, 0)).then_inc(s_at, 16)
                            e.wait_ge(s_begin, 16 * C)
                            e.wait_ge(s_at, 16)
                            e.indirect_dma_start(out=starts, out_offset=indices(run_start, 0), in_=at_run[:, :],
                                                 in_offset=None, bounds_check=P * L - 1,
                                                 oob_is_err=False).then_inc(s_at, 16)
                            e.wait_ge(s_at, 32)

                    @block.sync
                    def _(e):
                        e.wait_ge(s_row, 1)
                        e.dma_start(by_node(tab[k]), row[:, :, :]).then_inc(s_tab, 16)
                        e.wait_ge(s_tab, 16)

        s_turns = sem("turns")

        def turn_wait(e, s, value):
            e.wait_ge(s, value)
            e.sem_inc(s_turns, 1)

        def indices(idx, b):
            return bass.IndirectOffsetOnAxis(ap=idx[:, b:b + 1], axis=0)

        def scan_block(e, ch, cols, msg, run, before):
            for f in range(D):
                ch.do(e.tensor_tensor_scan(run[:, :, f], same[:, cols], msg[:, :, f], before[:, J - 1, f:f + 1],
                                           ALU.mult, ALU.add))

        def node_sums(k, last):
            c, sbl, psl, seml = stage(f"sums{k}")
            with c:
                stT = sbl("stT", [D, P])
                cT = sbl("cT", [D, P])
                shifted = sbl("shifted", [D, P])
                carry = sbl("carry", [P, D])
                more = sbl("more", [P, C, D])
                pa, pb = psl("a"), psl("b")
                s_v, s_t, s_sh, s_back, s_carry, s_cd, s_g, s_more = seml(
                    "v", "t", "sh", "back", "carry", "cd", "g", "more")
                with nc.Block() as block:
                    @block.tensor
                    def _(e):
                        e.transpose(pa[0:D, 0:P], last, ident[:, :]).then_inc(s_t, 1)
                        e.wait_ge(s_sh, 1)
                        e.transpose(pb[:, 0:D], shifted[:, :], ident[0:D, 0:D]).then_inc(s_back, 1)

                    @block.vector
                    def _(e):
                        ch = Chain(e, s_v)
                        ch.do(e.memset(shifted[:, 0:1], 0.0))
                        e.wait_ge(s_t, 1)
                        ch.to(e.tensor_copy(stT[:, :], pa[0:D, 0:P]))
                        ch.to(e.tensor_tensor_scan(cT[:, :], through[0:D, :], stT[:, :], 0.0, ALU.mult, ALU.add))
                        ch.do(e.tensor_copy(shifted[:, 1:P], cT[:, 0:P - 1]))
                        ch.tell(s_sh)
                        e.wait_ge(s_back, 1)
                        ch.do(e.tensor_copy(carry[:, :], pb[:, 0:D]))
                        ch.tell(s_carry)
                        e.wait_ge(s_g, 16 * C)
                        ch.to(e.tensor_tensor(agg[:, :, :], agg[:, :, :], bc_f(full), ALU.mult))
                        e.wait_ge(s_more, 16)
                        ch.to(e.tensor_tensor(agg[:, :, :], agg[:, :, :], more[:, :, :], ALU.add))

                    @block.gpsimd
                    def _(e):
                        e.wait_ge(s_carry, 1)
                        e.indirect_dma_start(out=corr[k], out_offset=indices(carry_to, 0), in_=carry[:, :],
                                             in_offset=None, bounds_check=NP - 1, oob_is_err=False).then_inc(s_cd, 16)
                        for q in range(C):
                            e.indirect_dma_start(out=agg[:, q, :], out_offset=None, in_=runs[k],
                                                 in_offset=indices(last_edge, q)).then_inc(s_g, 16)

                    @block.sync
                    def _(e):
                        e.wait_ge(s_cd, 16)
                        e.dma_start(more[:, :, :], by_node(corr[k])).then_inc(s_more, 16)

        norm_and_table(0)
        c, sbl, psl, seml = stage("gcn")
        with c:
            idx = [sbl(f"idx{b}", [P, J], I32) for b in range(2)]
            got = [sbl(f"got{b}", [P, J, D]) for b in range(2)]
            run = [sbl(f"run{b}", [P, J, D]) for b in range(2)]
            digits = [sbl(f"digits{b}", [P, J, P + C], BF16) for b in range(2)]
            banks = ExitStack()
            pcnt = ps("gcn_cnt", [P, 512], banks)
            s_v, s_clear, s_dig, s_mm, s_deg, s_sqrt = seml("v", "clear", "dig", "mm", "deg", "sqrt")
            s_idx, s_got, s_run, s_st, s_kept = (seml(f"{n}0", f"{n}1") for n in ("idx", "got", "run", "st", "kept"))
            src_blk = a["src"]
            run_rows = runs[0].rearrange("(p l) f -> p l f", p=P)
            with nc.Block() as block:
                @block.sync
                def _(e):
                    for b in range(2):
                        e.dma_start(idx[b][:, :], src_blk[:, b * J:(b + 1) * J]).then_inc(s_idx[b], 16)
                    for b in range(2):
                        e.sem_inc(s_kept[b], 1)
                    with e.Fori(0, NB // 2 - 1) as i:
                        for b in range(2):
                            e.wait_ge(s_run[b], i + 1)
                            e.dma_start(run_rows[:, block_cols(i, b), :], run[b][:, :, :]).then_inc(s_st[b], 16)
                            e.dma_start(idx[b][:, :], src_blk[:, block_cols(i + 1, b)]).then_inc(s_idx[b], 16)
                            e.wait_ge(s_st[b], i * 16 + 16)
                            e.sem_inc(s_kept[b], 1)
                    for b in range(2):
                        e.wait_ge(s_run[b], NB // 2)
                        at = L - (2 - b) * J
                        e.dma_start(run_rows[:, at:at + J, :], run[b][:, :, :]).then_inc(s_st[b], 16)
                    for b in range(2):
                        e.wait_ge(s_st[b], 16 * (NB // 2))

                @block.gpsimd
                def _(e):
                    with e.Fori(0, NB // 2) as i:
                        for b in range(2):
                            turn_wait(e, s_idx[b], i * 16 + 16)
                            for j in range(J):
                                e.indirect_dma_start(out=got[b][:, j, :], out_offset=None, in_=tab[0],
                                                     in_offset=indices(idx[b], j)).then_inc(s_got[b], 16)

                @block.vector
                def _(e):
                    ch = Chain(e, s_v)
                    ch.do(e.memset(run[1][:, J - 1, :], 0.0))
                    ch.do(e.memset(pcnt[:, 0:C], 0.0))
                    ch.tell(s_clear)
                    with e.Fori(0, NB // 2) as i:
                        ch.loop(i, 2 * D)
                        for b in range(2):
                            e.wait_ge(s_mm, i * 2 + (b + 1))
                            one_hot(e, digits[b][:, :, 0:P], src_lo, block_cols(i, b), P).then_inc(s_dig, 1)
                            one_hot(e, digits[b][:, :, P:], src_hi, block_cols(i, b), C).then_inc(s_dig, 1)
                            e.wait_ge(s_got[b], i * (16 * J) + 16 * J)
                            e.wait_ge(s_kept[b], i + 1)
                            scan_block(e, ch, block_cols(i, b), got[b], run[b], run[1 - b])
                            ch.tell(s_run[b])
                    ch.end(NB // 2)
                    e.wait_ge(s_mm, NB + 2)
                    ch.to(e.tensor_tensor(v2[:, :], cnt_d[:, :], pcnt[:, 0:C], ALU.add))
                    ch.do(e.tensor_scalar(v2[:, :], v2[:, :], 1e-5, None, ALU.max))
                    ch.tell(s_deg)
                    e.wait_ge(s_sqrt, 1)
                    ch.to(e.reciprocal(dis[:, :], dis[:, :]))

                @block.tensor
                def _(e):
                    e.wait_ge(s_clear, 1)
                    e.sem_inc(s_mm, 2)
                    with e.Fori(0, NB // 2) as i:
                        for b in range(2):
                            e.wait_ge(s_dig, i * 4 + (2 * b + 2))
                            count(e, pcnt, digits[b]).then_inc(s_mm, 1)

                @block.scalar
                def _(e):
                    e.wait_ge(s_deg, 1)
                    e.activation(dis[:, :], v2[:, :], ACT.Sqrt).then_inc(s_sqrt, 1)
            banks.close()
            node_sums(0, run[1][:, J - 1, :])

        c, sbl, psl, seml = stage("gcn_nodes")
        with c:
            G = 7
            Wg, W1, b1 = sbl("Wg", [D, 48]), sbl("W1", [48, 32]), sbl("b1", [32, 1])
            W2 = sbl("W2", [33, D])
            part = [sbl(f"part{b}", [P, G, D]) for b in range(2)]
            aT, fT, uT = sbl("aT", [D, G * P]), sbl("fT", [48, G * P]), sbl("uT", [33, G * P])
            pt, pf, pu = ([psl(f"{n}{q}") for q in range(2)] for n in "tfu")
            po = psl("o")
            s_w, s_v, s_part, s_t, s_at, s_f, s_ft, s_u, s_ut, s_o, s_free = seml(
                "w", "v", "part", "t", "at", "f", "ft", "u", "ut", "o", "free")
            split = ((0, 4), (4, 7))
            with nc.Block() as block:
                @block.sync
                def _(e):
                    for t, n in ((Wg[:, :], "L0_gnn_W_gcn"), (W1[:, :], "L0_gnn_W1"),
                                 (b1[:, :], "L0_gnn_b1"), (W2[0:32, :], "L0_gnn_W2"), (W2[32:33, :], "L0_gnn_b2")):
                        e.dma_start(t, a[n]).then_inc(s_w, 16)

                @block.vector
                def _(e):
                    ch = Chain(e, s_v)
                    ch.do(e.memset(uT[32:33, :], 1.0))
                    ch.to(e.tensor_tensor(tmp[:, :, :], h[:, :, :], bc_f(dinv), ALU.mult))
                    ch.to(e.tensor_tensor(agg[:, :, :], agg[:, :, :], tmp[:, :, :], ALU.add))
                    ch.do(e.tensor_tensor(agg[:, :, :], agg[:, :, :], bc_f(dinv), ALU.mult))
                    ch.to(e.tensor_tensor(x[:, :, :], x[:, :, :], h[:, :, :], ALU.add))
                    with e.Fori(0, C // G) as i:
                        ch.loop(i, 6)
                        cols = bass.ds(i * G, G)
                        ch.do(e.tensor_copy(part[0][:, :, :], agg[:, cols, :]))
                        ch.tell(s_part)
                        for q, (lo, hi) in enumerate(split):
                            e.wait_ge(s_t, i * 2 + (q + 1))
                            ch.do(e.tensor_copy(aT[:, lo * P:hi * P], pt[q][0:D, 0:(hi - lo) * P]))
                            ch.tell(s_at)
                        for q, (lo, hi) in enumerate(split):
                            e.wait_ge(s_f, i * 2 + (q + 1))
                            ch.do(e.tensor_copy(fT[:, lo * P:hi * P], pf[q][0:48, 0:(hi - lo) * P]))
                            ch.tell(s_ft)
                        e.wait_ge(s_o, i + 1)
                        ch.to(e.tensor_tensor(x[:, cols, :], x[:, cols, :],
                                              po[:, 0:G * D].rearrange("p (g f) -> p g f", f=D), ALU.add))
                    ch.end(C // G)

                @block.tensor
                def _(e):
                    e.wait_ge(s_w, 80)
                    with e.Fori(0, C // G) as i:
                        turn_wait(e, s_part, i + 1)
                        for q, (lo, hi) in enumerate(split):
                            for g in range(lo, hi):
                                mm = e.transpose(pt[q][0:D, (g - lo) * P:(g - lo + 1) * P], part[0][:, g, :], ident[:, :])
                            mm.then_inc(s_t, 1)
                        for q, (lo, hi) in enumerate(split):
                            turn_wait(e, s_at, i * 2 + (q + 1))
                            e.matmul(pf[q][0:48, 0:(hi - lo) * P], Wg[:, :], aT[:, lo * P:hi * P],
                                     start=True, stop=True).then_inc(s_f, 1)
                        for q, (lo, hi) in enumerate(split):
                            turn_wait(e, s_ft, i * 2 + (q + 1))
                            e.matmul(pu[q][0:32, 0:(hi - lo) * P], W1[:, :], fT[:, lo * P:hi * P],
                                     start=True, stop=True).then_inc(s_u, 1)
                        turn_wait(e, s_ut, i * 2 + 2)
                        for g in range(G):
                            mm = e.matmul(po[:, g * D:(g + 1) * D], uT[:, g * P:(g + 1) * P], W2[:, :],
                                          start=True, stop=True)
                        mm.then_inc(s_o, 1)

                @block.scalar
                def _(e):
                    e.wait_ge(s_w, 80)
                    with e.Fori(0, C // G) as i:
                        for q, (lo, hi) in enumerate(split):
                            e.wait_ge(s_u, i * 2 + (q + 1))
                            e.activation(uT[0:32, lo * P:hi * P], pu[q][0:32, 0:(hi - lo) * P], ACT.Relu,
                                         bias=b1[:, 0:1]).then_inc(s_ut, 1)

        renew_semaphores()
        norm_and_table(1)
        c, sbl, psl, seml = stage("nnconv")
        H1 = 64
        QT = 8
        WT = J * P // QT
        with c:
            W1, W2 = sbl("W1", [7, H1]), sbl("W2", [P, 256])
            idx = [sbl(f"idx{b}", [P, J], I32) for b in range(2)]
            got = [sbl(f"got{b}", [P, J, D]) for b in range(2)]
            ef = [sbl(f"ef{b}", [7, J, P]) for b in range(2)]
            tT = [sbl(f"tT{b}", [P, J * P]) for b in range(2)]
            prod = [sbl(f"prod{q}", [P, 2, D, D]) for q in range(3)]
            msg = [sbl(f"msg{b}", [P, J, D]) for b in range(2)]
            run = [sbl(f"run{b}", [P, J, D]) for b in range(2)]
            pt = [psl(f"t{q}") for q in range(2)]
            BK = 4
            banks = ExitStack()
            pw = [ps(f"nnconv_w{q}", [P, 512], banks) for q in range(BK)]
            s_v, s_w, s_one, s_t, s_relu, s_edge, s_msg = seml("v", "w", "one", "t", "relu", "edge", "msg")
            s_idx, s_ef, s_got, s_run, s_st, s_kept = (seml(f"{n}0", f"{n}1") for n in ("idx", "ef", "got", "run", "st", "kept"))
            run_rows = runs[1].rearrange("(p l) f -> p l f", p=P)
            JJ = J // 2
            with nc.Block() as block:
                @block.sync
                def _(e):
                    e.wait_ge(s_one, 1)
                    for t, n in ((W1[0:6, :], "L1_gnn_W1"), (W1[6:7, :], "L1_gnn_b1"),
                                 (W2[0:H1, :], "L1_gnn_W2"), (W2[H1:H1 + 1, :], "L1_gnn_b2")):
                        e.dma_start(t, a[n]).then_inc(s_w, 16)

                    def load_idx(at):
                        e.dma_start(idx[at.b][:, :], a["src"][:, at.cols()]).then_inc(s_idx[at.b], 16)

                    def load_ef(at):
                        e.dma_start(ef[at.b][0:6, :, :], a["ef6"][:, at.cols(), :]).then_inc(s_ef[at.b], 16)

                    def step(at):
                        if at.k < NB - 3:
                            turn_wait(e, s_t, at.of(QT, 2 * QT))
                            load_ef(at.plus(3))
                        e.wait_ge(s_run[at.b], at.half(1, 1))
                        e.dma_start(run_rows[:, at.cols(), :], run[at.b][:, :, :]).then_inc(s_st[at.b], 16)
                        if at.k < NB - 2:
                            load_idx(at.plus(2))
                        e.wait_ge(s_st[at.b], at.half(16, 16))
                        e.sem_inc(s_kept[at.b], 1)

                    for b in range(2):
                        load_idx(At(b))
                        load_ef(At(b))
                        e.sem_inc(s_kept[b], 1)
                    e.wait_ge(s_t, QT)
                    load_ef(At(2))
                    walk(e, NB, step, head=2, tail=4)

                @block.gpsimd
                def _(e):
                    with e.Fori(0, NB // 2) as i:
                        for b in range(2):
                            turn_wait(e, s_idx[b], i * 16 + 16)
                            for j in range(J):
                                e.indirect_dma_start(out=got[b][:, j, :], out_offset=None, in_=tab[1],
                                                     in_offset=indices(idx[b], j)).then_inc(s_got[b], 16)

                @block.tensor
                def _(e):
                    e.wait_ge(s_w, 64)

                    def hidden(at, q):
                        if q == 0:
                            turn_wait(e, s_ef[at.b], at.half(16, 16))
                        turn_wait(e, s_relu, at.of(QT, q + 1))
                        e.matmul(pt[q % 2][0:H1, 0:WT], W1[:, :],
                                 ef[at.b].rearrange("k j p -> k (j p)")[:, q * WT:(q + 1) * WT],
                                 start=True, stop=True).then_inc(s_t, 1)

                    def matrices(at, g):
                        k = at.b * JJ + g
                        if g == 0:
                            turn_wait(e, s_relu, at.of(QT, QT + 2))
                        turn_wait(e, s_msg, at.plus(-at.b).of(JJ, bank_free(k, BK, 2 * JJ)))
                        for j in range(2):
                            mm = e.matmul(pw[k % BK][:, j * 256:(j + 1) * 256],
                                          tT[at.b][:, (2 * g + j) * P:(2 * g + j + 1) * P], W2[:, :],
                                          start=True, stop=True)
                        mm.then_inc(s_edge, 1)

                    def step(at):
                        for g in range(JJ):
                            matrices(at, g)
                            if at.k < NB - 1 and g < QT:
                                hidden(at.plus(1), g)

                    for q in range(QT):
                        hidden(At(0), q)
                    walk(e, NB, step)

                @block.scalar
                def _(e):
                    e.wait_ge(s_one, 1)
                    e.sem_inc(s_relu, 2)
                    with e.Fori(0, NB // 2) as i:
                        for b in range(2):
                            for q in range(QT):
                                e.wait_ge(s_t, i * (2 * QT) + (b * QT + q + 1))
                                e.activation(tT[b][0:H1, q * WT:(q + 1) * WT], pt[q % 2][0:H1, 0:WT],
                                             ACT.Relu).then_inc(s_relu, 1)

                @block.vector
                def _(e):
                    ch = Chain(e, s_v)
                    ch.do(e.memset(W2[:, :], 0.0))
                    for b in range(2):
                        ch.do(e.memset(ef[b][:, :, :], 1.0))
                        ch.do(e.memset(tT[b][H1:, :], 0.0))
                    ch.sync()
                    for b in range(2):
                        ch.do(e.memset(tT[b][H1:H1 + 1, :], 1.0))
                    ch.do(e.memset(run[1][:, J - 1, :], 0.0))
                    ch.sync()
                    e.sem_inc(s_one, 1)
                    e.sem_inc(s_msg, BK)
                    with e.Fori(0, NB // 2) as i:
                        ch.loop(i, 2 * (D + JJ))
                        for b in range(2):
                            e.wait_ge(s_got[b], i * (16 * J) + 16 * J)
                            e.wait_ge(s_kept[b], i + 1)
                            added = []
                            for g in range(JJ + 1):
                                if g < JJ:
                                    e.wait_ge(s_edge, i * (2 * JJ) + (b * JJ + g + 1))
                                    if g >= 3:
                                        ch.wait(added[g - 3])
                                    e.tensor_tensor(prod[g % 3][:, :, :, :],
                                                    pw[(b * JJ + g) % BK][:, :].rearrange("p (j i o) -> p j i o", j=2, i=D),
                                                    got[b][:, 2 * g:2 * g + 2, :][:, :, :, None].to_broadcast([P, 2, D, D]),
                                                    ALU.mult).then_inc(s_msg, 1)
                                if g >= 1:
                                    e.wait_ge(s_msg, i * (2 * JJ) + (b * JJ + g + BK))
                                    added.append(ch.do(e.tensor_reduce(
                                        msg[b][:, 2 * g - 2:2 * g, :],
                                        prod[(g - 1) % 3][:, :, :, :].rearrange("p j i o -> p j o i"), AX.X, ALU.add)))
                            ch.sync()
                            scan_block(e, ch, block_cols(i, b), msg[b], run[b], run[1 - b])
                            ch.tell(s_run[b])
                    ch.end(NB // 2)
            banks.close()
            node_sums(1, run[1][:, J - 1, :])

        c, sbl, psl, seml = stage("bn")
        with c:
            bias, gamma, beta = (sbl(n, [P, D]) for n in ("bias", "gamma", "beta"))
            part, mean, std = (sbl(n, [P, D]) for n in ("part", "mean", "std"))
            pm, pv = psl("m"), psl("v")
            s_w, s_v, s_p, s_m, s_std = seml("w", "v", "p", "m", "std")

            def bc_n(t):
                return t[:, None, :].to_broadcast([P, C, D])

            with nc.Block() as block:
                @block.sync
                def _(e):
                    for t, n in ((bias, "bias"), (gamma, "gamma"), (beta, "beta")):
                        e.dma_start(t[:, :], a[f"L1_gnn_{n}"].to_broadcast([P, D])).then_inc(s_w, 16)

                @block.tensor
                def _(e):
                    for k, t in enumerate((pm, pv)):
                        e.wait_ge(s_p, k + 1)
                        e.matmul(t[:, 0:D], ones[:, :], part[:, :], start=True, stop=True).then_inc(s_m, 1)

                @block.scalar
                def _(e):
                    e.wait_ge(s_m, 2)
                    e.activation(std[:, :], pv[:, 0:D], ACT.Sqrt, bias=eps[:, 0:1], scale=1.0 / N).then_inc(s_std, 1)

                @block.vector
                def _(e):
                    ch = Chain(e, s_v)
                    ch.to(e.tensor_scalar(v1[:, :], cnt_d[:, :], 1.0, None, ALU.max))
                    ch.to(e.reciprocal(v1[:, :], v1[:, :]))
                    ch.to(e.tensor_tensor(agg[:, :, :], agg[:, :, :], bc_f(v1), ALU.mult))
                    e.wait_ge(s_w, 48)
                    ch.to(e.tensor_tensor(agg[:, :, :], agg[:, :, :], bc_n(bias), ALU.add))
                    ch.to(e.tensor_scalar(agg[:, :, :], agg[:, :, :], 0.0, None, ALU.max))
                    ch.to(e.tensor_tensor(tmp[:, :, :], agg[:, :, :], bc_f(real), ALU.mult))
                    ch.do(e.tensor_reduce(part[:, :], tmp[:, :, :].rearrange("p c f -> p f c"), AX.X, ALU.add))
                    ch.tell(s_p)
                    e.wait_ge(s_m, 1)
                    ch.to(e.tensor_scalar(mean[:, :], pm[:, 0:D], 1.0 / N, None, ALU.mult))
                    ch.to(e.tensor_tensor(agg[:, :, :], agg[:, :, :], bc_n(mean), ALU.subtract))
                    ch.to(e.tensor_tensor(tmp[:, :, :], agg[:, :, :], bc_f(real), ALU.mult))
                    ch.to(e.tensor_tensor(tmp[:, :, :], tmp[:, :, :], tmp[:, :, :], ALU.mult))
                    ch.do(e.tensor_reduce(part[:, :], tmp[:, :, :].rearrange("p c f -> p f c"), AX.X, ALU.add))
                    ch.tell(s_p)
                    e.wait_ge(s_std, 1)
                    ch.to(e.reciprocal(std[:, :], std[:, :]))
                    ch.to(e.tensor_tensor(std[:, :], std[:, :], gamma[:, :], ALU.mult))
                    ch.to(e.tensor_tensor(agg[:, :, :], agg[:, :, :], bc_n(std), ALU.mult))
                    ch.to(e.tensor_tensor(agg[:, :, :], agg[:, :, :], bc_n(beta), ALU.add))
                    ch.to(e.tensor_tensor(x[:, :, :], x[:, :, :], agg[:, :, :], ALU.add))

        renew_semaphores()
        norm_and_table(2)
        c, sbl, psl, seml = stage("sheaf")
        H2 = 64
        JH = J // 2
        NW = 4
        with c:
            Wz, W2 = sbl("Wz", [P, 2 * H2]), sbl("W2", [2 * H2, 2 * D])
            b2 = sbl("b2", [1, JH, 2, D])
            idx = [sbl(f"idx{b}", [P, J], I32) for b in range(2)]
            begun = [sbl(f"begun{b}", [P, J, T2]) for b in range(2)]
            got = [sbl(f"got{b}", [P, J, 2, T2]) for b in range(2)]
            gT = [sbl(f"gT{q}", [P, 2 * P]) for q in range(2)]
            zT = [sbl(f"zT{q}", [2 * H2, 2 * P]) for q in range(2)]
            vec = [sbl(f"vec{q}", [P, JH, 2, D]) for q in range(2)]
            prod = sbl("prod", [P, JH, 7, D])
            dots = sbl("dots", [P, JH, 7])
            cc = sbl("cc", [P, JH, 2])
            first = sbl("first", [P, JH, 2])
            second = sbl("second", [P, JH, 2])
            term = sbl("term", [P, JH, 2, D])
            msg = [sbl(f"msg{b}", [P, J, 2, D]) for b in range(2)]
            hot_lo = [sbl(f"hot_lo{q}", [P, JH, P]) for q in range(2)]
            hot_hi = [sbl(f"hot_hi{q}", [P, JH, C]) for q in range(2)]
            wide = [sbl(f"wide{q}", [P, C, D]) for q in range(NW)]
            run = [sbl(f"run{b}", [P, J, D]) for b in range(2)]
            from_src = sbl("from_src", [P, C, D])
            banks = ExitStack()
            pg, pz, pv, pacc = ([ps(f"sheaf_{n}{q}", [P, 512], banks) for q in range(2)] for n in ("g", "z", "v", "acc"))
            HC = 25
            halves = ((0, HC), (HC, C))
            s_v, s_w, s_one, s_gT, s_gTc, s_z, s_zc, s_used, s_vc, s_vfree, s_wide, s_acc, s_sq, s_lo, s_msg, s_held = seml(
                "v", "w", "one", "gT", "gTc", "z", "zc", "used", "vc", "vfree", "wide", "acc", "sq", "lo", "msg", "held")
            s_idx, s_begun, s_got_a, s_got_b, s_run, s_st, s_kept = (
                seml(f"{n}0", f"{n}1") for n in ("idx", "begun", "got_a", "got_b", "run", "st", "kept"))
            s_got = (s_got_a, s_got_b)
            start_rows = starts.rearrange("(p l) f -> p l f", p=P)
            run_rows = runs[2].rearrange("(p l) f -> p l f", p=P)
            NG = JH
            parts = ((0, NG // 2 + 1), (NG // 2 + 1, NG))
            JA = 2 * parts[0][1]
            with nc.Block() as block:
                @block.sync
                def _(e):
                    e.wait_ge(s_one, 1)
                    w1, w2 = a["L2_W1T"], a["L2_W2T"]
                    s, d, one = slice(0, D), slice(T2, T2 + D), slice(D + 1, D + 2)
                    for t, n in ((Wz[s, 0:H2], w1[0:D, :]), (Wz[d, 0:H2], w1[D:2 * D, :]),
                                 (Wz[d, H2:], w1[0:D, :]), (Wz[s, H2:], w1[D:2 * D, :]),
                                 (Wz[one, 0:H2], a["L2_gnn_b1"]), (Wz[one, H2:], a["L2_gnn_b1"]),
                                 (W2[0:H2, 0:D], w2), (W2[H2:, D:], w2),
                                 (b2.rearrange("k j t f -> k (j t) f"),
                                  a["L2_gnn_b2"][:, None, :].to_broadcast([1, 2 * JH, D]))):
                        e.dma_start(t, n).then_inc(s_w, 16)

                    def load(at):
                        e.dma_start(idx[at.b][:, :], a["src"][:, at.cols()]).then_inc(s_idx[at.b], 16)

                    def load_begun(at):
                        e.dma_start(begun[at.b][:, :, :], start_rows[:, at.cols(), :]).then_inc(s_begun[at.b], 16)

                    def step(at):
                        e.wait_ge(s_run[at.b], at.half(1, 1))
                        e.dma_start(run_rows[:, at.cols(), :], run[at.b][:, :, :]).then_inc(s_st[at.b], 16)
                        if at.k < NB - 3:
                            turn_wait(e, s_msg, at.of(1, 2))
                            load(at.plus(3))
                        if at.k < NB - 5:
                            turn_wait(e, s_held, at.of(1, 4))
                            load_begun(at.plus(5))
                        e.wait_ge(s_st[at.b], at.half(16, 16))
                        e.sem_inc(s_kept[at.b], 1)

                    for b in range(2):
                        e.sem_inc(s_kept[b], 1)
                        load(At(b))
                        load_begun(At(b))
                    for b in range(2):
                        e.wait_ge(s_held, b + 1)
                        load_begun(At(b + 2))
                    e.wait_ge(s_msg, 1)
                    load(At(2))
                    e.wait_ge(s_held, 3)
                    load_begun(At(4))
                    walk(e, NB, step, head=2, tail=6)

                @block.gpsimd
                def _(e):
                    with e.Fori(0, NB // 2) as i:
                        for b in range(2):
                            turn_wait(e, s_idx[b], i * 16 + 16)
                            for j in range(J):
                                e.indirect_dma_start(out=got[b][:, j, 0, :], out_offset=None, in_=tab[2],
                                                     in_offset=indices(idx[b], j)).then_inc(s_got[int(j >= JA)][b], 16)

                @block.tensor
                def _(e):
                    e.wait_ge(s_w, 16 * 9)
                    e.wait_ge(s_one, 1)
                    e.sem_inc(s_z, 2)
                    e.sem_inc(s_used, 2)
                    e.sem_inc(s_acc, NW)

                    def turned(at, g):
                        q = (at.b * NG + g) % 2
                        turn_wait(e, s_gTc, at.of(NG, g + 1))
                        for j in range(2):
                            mm = e.transpose(pg[q][0:2 * T2, j * P:(j + 1) * P],
                                             got[at.b][:, 2 * g + j, :, :].rearrange("p t f -> p (t f)"), ident[:, :])
                        mm.then_inc(s_gT, 1)

                    def hidden(at, g):
                        q = (at.b * NG + g) % 2
                        turn_wait(e, s_gTc, at.of(NG, g + 3))
                        turn_wait(e, s_zc, at.of(NG, g + 1))
                        e.matmul(pz[q][:, 0:2 * P], Wz[:, :], gT[q][:, :], start=True, stop=True).then_inc(s_z, 1)

                    def vectors(at, g):
                        q = (at.b * NG + g) % 2
                        turn_wait(e, s_zc, at.of(NG, g + 3))
                        for j in range(2):
                            half, col = divmod(2 * g + j, JH)
                            if col == 0:
                                turn_wait(e, s_vc, at.of(2, half + 1))
                                e.matmul(pv[half][:, 0:JH * 2 * D], ones[0:1, :],
                                         b2.rearrange("k j t f -> k (j t f)"), start=True, stop=False,
                                         skip_group_check=True)
                            mm = e.matmul(pv[half][:, col * 2 * D:(col + 1) * 2 * D],
                                          zT[q][:, j * P:(j + 1) * P], W2[:, :],
                                          start=False, stop=False, skip_group_check=True)
                        mm.then_inc(s_used, 1)

                    def phase(at, part, sums=()):
                        groups = range(*parts[part])
                        steps, sums = len(groups) + 2, list(sums)
                        if part == 0:
                            turn_wait(e, s_held, at.of(1, 1))
                        n = 16 * (JA, J - JA)[part]
                        turn_wait(e, s_got[part][at.b], at.half(n, n))
                        for t in range(steps):
                            for make, g in ((turned, t), (hidden, t - 1), (vectors, t - 2)):
                                if 0 <= g < len(groups):
                                    make(at, groups[g])
                            while sums and len(sums) * steps > JH * (steps - 1 - t):
                                add(*sums.pop(0))

                    def add(at, j):
                        half, col = divmod(j, JH)
                        if col == 0:
                            turn_wait(e, s_lo, at.of(2, half + 1))
                        turn_wait(e, s_wide, at.of(J, j + 2))
                        for k, (lo, hi) in enumerate(halves):
                            mm = e.matmul(pacc[k][:, 0:(hi - lo) * D], hot_lo[half][:, col, :],
                                          wide[(at.b * J + j) % NW][:, lo:hi, :].rearrange("p c f -> p (c f)"),
                                          start=False, stop=False, skip_group_check=True)
                        mm.then_inc(s_acc, 1)

                    def step(at):
                        first, second = ([(at, half * JH + j) for j in range(JH)] for half in range(2))
                        if at.k < NB - 1:
                            phase(at.plus(1), 1, first)
                        else:
                            second = first + second
                        if at.k < NB - 2:
                            phase(at.plus(2), 0, second)
                        else:
                            for q in second:
                                add(*q)

                    phase(At(0), 0)
                    phase(At(0), 1)
                    phase(At(1), 0)
                    walk(e, NB, step, head=2)

                @block.scalar
                def _(e):
                    e.wait_ge(s_one, 1)
                    for s in (s_gTc, s_zc, s_vc):
                        e.sem_inc(s, 2)

                    def low_digits(at, half):
                        def square(j):
                            if j == 0 and at.k > 0:
                                e.wait_ge(s_acc, at.of(J, (half + 1) * JH - J + NW))
                            e.activation(hot_lo[half][:, j, :], iota_f[:, :], ACT.Square, scale=-1.0,
                                         bias=src_lo[:, bass.ds(at.of(J, half * JH + j), 1)]).then_inc(s_sq, 1)

                        def hot():
                            e.wait_ge(s_sq, at.of(J, (half + 1) * JH))
                            e.activation(hot_lo[half][:, :, :], hot_lo[half][:, :, :], ACT.Relu, scale=-1.0,
                                         bias=ones[:, 0:1]).then_inc(s_lo, 1)

                        return [lambda j=j: square(j) for j in range(JH)] + [hot]

                    def copy_vectors(at, half):
                        e.wait_ge(s_used, at.of(NG, parts[half][1] + 2))
                        e.wait_ge(s_vfree, at.of(2, half + 1))
                        e.copy(vec[half].rearrange("p j t f -> p (j t f)"), pv[half][:, 0:JH * 2 * D]).then_inc(s_vc, 1)

                    def phase(at, part, digits=()):
                        digits = list(digits)
                        g0, g1 = parts[part]
                        for g in range(g0, g1 + 1):
                            if g < g1:
                                q = (at.b * NG + g) % 2
                                e.wait_ge(s_gT, at.of(NG, g + 1))
                                e.wait_ge(s_z, at.of(NG, g + 1))
                                e.copy(gT[q][0:2 * T2, :], pg[q][0:2 * T2, 0:2 * P]).then_inc(s_gTc, 1)
                            if g > g0:
                                q = (at.b * NG + g - 1) % 2
                                e.wait_ge(s_z, at.of(NG, g + 2))
                                e.wait_ge(s_used, at.of(NG, g))
                                e.activation(zT[q][:, :], pz[q][:, 0:2 * P], ACT.Relu).then_inc(s_zc, 1)
                            for make in digits[:2]:
                                make()
                            del digits[:2]
                        copy_vectors(at, part)
                        for make in digits:
                            make()

                    def step(at):
                        if at.k < NB - 1:
                            phase(at.plus(1), 1, low_digits(at, 1))
                            if at.k < NB - 2:
                                phase(at.plus(2), 0, low_digits(at.plus(1), 0))
                            else:
                                for make in low_digits(at.plus(1), 0):
                                    make()
                        else:
                            for make in low_digits(at, 1):
                                make()

                    phase(At(0), 0)
                    phase(At(0), 1)
                    phase(At(1), 0, low_digits(At(0), 0))
                    walk(e, NB, step, head=2)

                @block.vector
                def _(e):
                    ch = Chain(e, s_v)
                    ch.do(e.memset(Wz[:, :], 0.0))
                    ch.do(e.memset(W2[:, :], 0.0))
                    for t in gT + pacc:
                        ch.do(e.memset(t[:, :], 0.0))
                    ch.do(e.memset(run[1][:, J - 1, :], 0.0))
                    ch.do(e.memset(got[1][:, J - 1, 1, :], 0.0))
                    ch.sync()
                    e.sem_inc(s_one, 1)
                    e.sem_inc(s_vfree, 2)
                    e.sem_inc(s_wide, 1)
                    two = [P, JH, 2, D]

                    def hold(at):
                        e.wait_ge(s_begun[at.b], at.half(16, 16))
                        for f in range(T2):
                            ch.do(e.tensor_tensor_scan(got[at.b][:, :, 1, f], same[:, at.cols()], begun[at.b][:, :, f],
                                                       got[1 - at.b][:, J - 1, 1, f:f + 1], ALU.mult, ALU.add))
                        ch.tell(s_held)

                    def high_digits(at, half):
                        hi = src_hi[:, bass.ds(at.of(J, half * JH), JH)]
                        ch.do(e.tensor_tensor(hot_hi[half][:, :, :], iota_f[:, None, 0:C].to_broadcast([P, JH, C]),
                                              hi[:, :, None].to_broadcast([P, JH, C]), ALU.is_equal))

                    def widen(at, j):
                        half, col = divmod(j, JH)
                        e.wait_ge(s_acc, at.of(J, j + 1))
                        e.tensor_tensor(wide[(at.b * J + j) % NW][:, :, :],
                                        msg[at.b][:, j, 1, :][:, None, :].to_broadcast([P, C, D]),
                                        hot_hi[half][:, col, :][:, :, None].to_broadcast([P, C, D]),
                                        ALU.mult).then_inc(s_wide, 1)

                    def messages(at, half):
                        g4 = got[at.b][:, half * JH:(half + 1) * JH, :, :]
                        xs, xd = g4[:, :, 0, 0:D], g4[:, :, 1, 0:D]
                        V = vec[half]
                        u, w = V[:, :, 0, :], V[:, :, 1, :]
                        m = msg[at.b][:, half * JH:(half + 1) * JH, :, :]

                        def both(t):
                            return t[:, :, None, :].to_broadcast(two)

                        def tt(out, in0, in1, op=ALU.mult):
                            return lambda: e.tensor_tensor(out, in0, in1, op)

                        uw = dots[:, :, 6]
                        return [
                            [tt(prod[:, :, 0:2, :], V[:, :, :, :], V[:, :, :, :]),
                             tt(prod[:, :, 2:4, :], V[:, :, :, :], both(xs)),
                             tt(prod[:, :, 4:6, :], V[:, :, :, :], both(xd)),
                             tt(prod[:, :, 6, :], u, w)],
                            [lambda: e.tensor_reduce(dots[:, :, :], prod[:, :, :, :], AX.X, ALU.add)],
                            [lambda: e.tensor_scalar(cc[:, :, :], dots[:, :, 0:2], 1e-24, 0.5, ALU.max, ALU.mult)],
                            [lambda: e.reciprocal(cc[:, :, :], cc[:, :, :])],
                            [tt(first[:, :, 0], cc[:, :, 0], dots[:, :, 2]), tt(first[:, :, 1], cc[:, :, 1], dots[:, :, 5])],
                            [tt(second[:, :, :], first[:, :, :], uw[:, :, None].to_broadcast([P, JH, 2]))],
                            [tt(second[:, :, :], dots[:, :, 3:5], second[:, :, :], ALU.subtract)],
                            [tt(second[:, :, 0], second[:, :, 0], cc[:, :, 1]), tt(second[:, :, 1], second[:, :, 1], cc[:, :, 0]),
                             tt(term[:, :, :, :], first[:, :, :, None].to_broadcast(two), V[:, :, :, :])],
                            [tt(m, g4[:, :, :, 0:D], term[:, :, :, :], ALU.subtract)],
                            [tt(term[:, :, 0, :], second[:, :, 0][:, :, None].to_broadcast([P, JH, D]), w),
                             tt(term[:, :, 1, :], second[:, :, 1][:, :, None].to_broadcast([P, JH, D]), u)],
                            [tt(m, m, term[:, :, :, :], ALU.subtract)],
                            [tt(m, m, g4[:, :, :, D:D + 1].to_broadcast(two))],
                        ]

                    def half_step(at, half, widened=True):
                        nxt = at.plus(1)
                        cols = list(range(half * JH, (half + 1) * JH)) if widened else []
                        if at.k < NB - 1:
                            n = 16 * (JA, J - JA)[half]
                            e.wait_ge(s_got[half][nxt.b], nxt.half(n, n))
                            if cols:
                                widen(at, cols.pop(0))
                            e.wait_ge(s_vc, nxt.of(2, half + 3))
                            for level in messages(nxt, half):
                                for make in level:
                                    n = ch.do(make())
                                if cols:
                                    widen(at, cols.pop(0))
                                ch.wait(n)
                            e.sem_inc(s_vfree, 1)
                            if half == 1:
                                e.sem_inc(s_msg, 1)
                        for j in cols:
                            widen(at, j)

                    def step(at):
                        if at.k > 0:
                            e.wait_ge(s_wide, at.of(J, 1))
                        high_digits(at, 1)
                        half_step(at, 0)
                        e.wait_ge(s_kept[at.b], at.half(1, 1))
                        scan_block(e, ch, at.cols(), msg[at.b][:, :, 0, :], run[at.b], run[1 - at.b])
                        ch.tell(s_run[at.b])
                        if at.k < NB - 1:
                            e.wait_ge(s_wide, at.of(J, JH + 1))
                            high_digits(at.plus(1), 0)
                        half_step(at, 1)
                        if at.k < NB - 3:
                            hold(at.plus(3))

                    for b in range(2):
                        hold(At(b))
                    high_digits(At(0), 0)
                    for half in range(2):
                        half_step(At(-1), half, widened=False)
                    hold(At(2))
                    walk(e, NB, step, ch, 2 * 19 + 2 + D + T2, head=2, tail=4)
                    e.wait_ge(s_acc, NB * J + NW)
                    for k, (lo, hi) in enumerate(halves):
                        ch.do(e.tensor_copy(from_src[:, lo:hi, :],
                                            pacc[k][:, 0:(hi - lo) * D].rearrange("p (c f) -> p c f", f=D)))
                    ch.sync()
            banks.close()
            node_sums(2, run[1][:, J - 1, :])
            s_n, = seml("n")
            with nc.Block() as block:
                @block.vector
                def _(e):
                    ch = Chain(e, s_n)
                    ch.to(e.tensor_tensor(agg[:, :, :], agg[:, :, :], from_src[:, :, :], ALU.add))
                    ch.to(e.tensor_tensor(agg[:, :, :], agg[:, :, :], bc_f(dis), ALU.mult))
                    ch.to(e.tensor_tensor(agg[:, :, :], agg[:, :, :], h[:, :, :], ALU.add))
                    ch.to(e.tensor_scalar(agg[:, :, :], agg[:, :, :], 0.0, None, ALU.max))
                    ch.to(e.tensor_tensor(x[:, :, :], x[:, :, :], agg[:, :, :], ALU.add))

        renew_semaphores()
        norm_and_table(3)
        c, sbl, psl, seml = stage("attn")
        CH = D * D
        TAKES = {"act": (1, 3, 5), "dve": (0, 2, 4, 6, 7, 8, 9, 10, 11, 12)}
        BANKS = {"act": 1, "dve": 3}
        PAIRS = [J3 - 2, J3 - 4, J3 - 6, J3 - 8]
        J0 = PAIRS[-1]
        NX = len(PAIRS) + 2
        with c:
            banks = ExitStack()
            S = [sbl(f"S{b}", [P, J3, S3]) for b in range(2)]
            Wc = sb("attn_Wc", [P, 2 * CH], c=banks)
            minus = sb("attn_minus", [P, P], c=banks)
            idx = [sb(f"attn_idx{b}", [P, J3], I32, c=banks) for b in range(2)]
            eidx = [sb(f"attn_eidx{b}", [P, J3], I32, c=banks) for b in range(2)]
            got = [sb(f"attn_got{b}", [P, J3, D], c=banks) for b in range(2)]
            ef = [sb(f"attn_ef{b}", [P, J3, P], c=banks) for b in range(2)]
            T = [sb(f"attn_T{b}", [P, J3, 2 * CH], c=banks) for b in range(2)]
            drop = sb("attn_drop", [P, CH], c=banks)
            scale = sb("attn_scale", [P, CH], c=banks)
            carried = sb("attn_carried", [P, 2 * CH], c=banks)
            pw = {by: [ps(f"attn_{by}{q}", [P, 512], banks) for q in range(n)] for by, n in BANKS.items()}
            px = [ps(f"attn_x{q}", [P, 512], banks) for q in range(len(PAIRS))]
            s_w, s_v, s_one, s_max, s_sub, s_e, s_x, s_state, s_step = seml(
                "w", "v", "one", "max", "sub", "e", "x", "state", "step")
            s_col, s_t = ({by: seml(f"{n}_{by}")[0] for by in BANKS} for n in ("col", "t"))
            s_idx, s_ef, s_got, s_sc = (seml(f"{n}0", f"{n}1") for n in ("idx", "ef", "got", "sc"))

            def products(e, at):
                for by, cols in TAKES.items():
                    turn_wait(e, s_t[by], at.of(len(cols), len(cols) + BANKS[by]))

            def bank(by, at, n):
                return pw[by][(at.b * len(TAKES[by]) + n) % BANKS[by]]

            def per_matrix(t):
                return t.rearrange("p (m i o) -> p m i o", m=2, i=D)

            with nc.Block() as block:
                @block.sync
                def _(e):
                    e.wait_ge(s_one, 1)
                    for t, n in ((Wc[0:D, 0:CH], "L3_gnn_W_attn"), (Wc[0:D, CH:], "L3_gnn_W_msg"),
                                 (Wc[D:D + 1, 0:CH], "L3_gnn_b_attn"), (Wc[D:D + 1, CH:], "L3_gnn_b_msg")):
                        e.dma_start(t, a[n]).then_inc(s_w, 16)

                    def load(at):
                        e.dma_start(idx[at.b][:, :], a["src"][:, at.cols(J3)]).then_inc(s_idx[at.b], 16)
                        e.dma_start(ef[at.b][0:D, :, :], a["ef16"][:, at.cols(J3), :]).then_inc(s_ef[at.b], 16)

                    load(At(0))
                    load(At(1))
                    with e.Fori(0, NB3 // 2 - 1) as i:
                        for k in range(2):
                            products(e, At(k, i))
                            load(At(k + 2, i))

                @block.gpsimd
                def _(e):
                    def gather(at):
                        turn_wait(e, s_idx[at.b], at.half(16, 16))
                        for j in range(J3):
                            e.indirect_dma_start(out=got[at.b][:, j, :], out_offset=None, in_=tab[3],
                                                 in_offset=indices(idx[at.b], j)).then_inc(s_got[at.b], 16)

                    def scatter(at):
                        turn_wait(e, s_state, at.of(1, 1))
                        for j in range(J3):
                            e.indirect_dma_start(out=state3, out_offset=indices(eidx[at.b], j),
                                                 in_=S[at.b][:, j, :], in_offset=None, bounds_check=NP - 1,
                                                 oob_is_err=False).then_inc(s_sc[at.b], 16)

                    gather(At(0))
                    gather(At(1))
                    gather(At(2))
                    with e.Fori(0, NB3 // 2 - 2) as i:
                        for k in range(2):
                            gather(At(k + 3, i))
                            scatter(At(k, i))
                    gather(At(NB3 - 1))
                    for k in range(NB3 - 4, NB3):
                        scatter(At(k))
                    for b in range(2):
                        e.wait_ge(s_sc[b], 16 * J3 * (NB3 // 2))

                @block.tensor
                def _(e):
                    e.wait_ge(s_w, 64)

                    def matrices(at, *which):
                        for by, n in which:
                            cols, nb = len(TAKES[by]), BANKS[by]
                            if n == 0:
                                turn_wait(e, s_ef[at.b], at.half(16, 16))
                            turn_wait(e, s_t[by], at.plus(-at.b).of(cols, bank_free(at.b * cols + n, nb, 2 * cols)))
                            e.matmul(bank(by, at, n)[:, :], ef[at.b][:, TAKES[by][n], :], Wc[:, :],
                                     start=True, stop=True).then_inc(s_col[by], 1)

                    head = (("dve", 0), ("act", 0), ("dve", 1), ("dve", 2))
                    middle = (("act", 1), ("dve", 3), ("dve", 4), ("act", 2), ("dve", 5), ("dve", 6))
                    end = (("dve", 7), ("dve", 8), ("dve", 9))

                    def exponents(at, n):
                        j = PAIRS[n]
                        turn_wait(e, s_max, at.of(len(PAIRS), n + 1))
                        turn_wait(e, s_x, at.of(NX, n + 1))
                        e.matmul(px[n][:, :], ident[:, :], T[at.b][:, j:j + 2, 0:CH], start=True, stop=False)
                        e.matmul(px[n][:, :], minus[:, :], S[at.b][:, j:j + 2, 0:CH], start=False, stop=True).then_inc(s_sub, 1)

                    def step(at):
                        more = at.k < NB3 - 1
                        if more:
                            matrices(at.plus(1), *middle)
                        for n in range(len(PAIRS)):
                            exponents(at, n)
                            if more:
                                matrices(at.plus(1), *end[n:n + 1])
                        if at.k < NB3 - 2:
                            matrices(at.plus(2), *head)

                    matrices(At(0), *head, *middle, *end)
                    matrices(At(1), *head)
                    walk(e, NB3, step, head=2)

                @block.scalar
                def _(e):
                    def edges(at):
                        e.wait_ge(s_got[at.b], at.half(16 * J3, 16 * J3))
                        if at.k >= 2:
                            e.wait_ge(s_step, at.of(1, -1))
                        for n, j in enumerate(TAKES["act"]):
                            e.wait_ge(s_col["act"], at.of(len(TAKES["act"]), n + 1))
                            for i in range(D):
                                to = e.activation(per_matrix(T[at.b][:, j, :])[:, :, i, :],
                                                  per_matrix(bank("act", at, n)[:, :])[:, :, i, :],
                                                  ACT.Copy, scale=got[at.b][:, j, i:i + 1])
                            to.then_inc(s_t["act"], 1)

                    def exps(at):
                        if at.k < NB3 - 1:
                            edges(at.plus(1))
                        for n, j in enumerate(PAIRS):
                            e.wait_ge(s_sub, at.of(len(PAIRS), n + 1))
                            e.activation(S[at.b][:, j:j + 2, CH:2 * CH],
                                         px[n][:, :].rearrange("p (w c) -> p w c", w=2), ACT.Exp).then_inc(s_x, 1)
                        e.wait_ge(s_e, at.of(1, 1))
                        e.activation(S[at.b][:, 0:J0, CH:2 * CH], T[at.b][:, 0:J0, 0:CH], ACT.Exp).then_inc(s_x, 1)
                        e.activation(scale[:, :], drop[:, :], ACT.Exp).then_inc(s_x, 1)

                    e.sem_inc(s_x, NX)
                    e.wait_ge(s_one, 1)
                    e.sem_inc(s_t["act"], BANKS["act"])
                    edges(At(0))
                    walk(e, NB3, exps, head=2)

                @block.vector
                def _(e):
                    ch = Chain(e, s_v)
                    for b in range(2):
                        ch.do(e.memset(ef[b][:, :, :], 0.0))
                    ch.do(e.memset(Wc[:, :], 0.0))
                    ch.do(e.tensor_scalar(minus[:, :], ident[:, :], -1.0, None, ALU.mult))
                    ch.sync()
                    for b in range(2):
                        ch.do(e.memset(ef[b][0:D + 1, :, :], 1.0))
                    ch.do(e.memset(S[1][:, J3 - 1, 0:CH], -BIG))
                    ch.do(e.memset(S[1][:, J3 - 1, CH:], 0.0))
                    ch.tell(s_one)
                    e.sem_inc(s_t["dve"], BANKS["dve"])

                    def edge(at, n):
                        j = TAKES["dve"][n]
                        if n == 0:
                            e.wait_ge(s_got[at.b], at.half(16 * J3, 16 * J3))
                        e.wait_ge(s_col["dve"], at.of(len(TAKES["dve"]), n + 1))
                        e.tensor_tensor(per_matrix(T[at.b][:, j, :]), per_matrix(bank("dve", at, n)[:, :]),
                                        got[at.b][:, j, :][:, None, :, None].to_broadcast([P, 2, D, D]),
                                        ALU.mult).then_inc(s_t["dve"], 1)

                    def sums(at, j):
                        Sb = S[at.b]
                        return ch.do(e.scalar_tensor_tensor(
                            out=Sb[:, j, CH:], in0=carried[:, :] if j == 0 else Sb[:, j - 1, CH:],
                            scalar=same[:, bass.ds(at.of(J3, j), 1)], in1=Sb[:, j, CH:], op0=ALU.mult, op1=ALU.add))

                    def a_block(at):
                        Sb, Tb, So = S[at.b], T[at.b], S[1 - at.b]
                        prev, first, last = at.plus(-1), at.k == 0, at.k == NB3 - 1
                        products(e, at)
                        if at.k >= 2:
                            e.wait_ge(s_sc[at.b], at.half(16 * J3, 0))
                        s_prev = None
                        todo = [] if last else list(range(len(TAKES["dve"])))
                        for j in range(J3):
                            m_now = ch.do(e.scalar_tensor_tensor(
                                out=Sb[:, j, 0:CH], in0=So[:, J3 - 1, 0:CH] if j == 0 else Sb[:, j - 1, 0:CH],
                                scalar=apart[:, bass.ds(at.of(J3, j), 1)], in1=Tb[:, j, 0:CH], op0=ALU.add, op1=ALU.max))
                            if not first:
                                if s_prev:
                                    ch.wait(s_prev)
                                s_prev = sums(prev, j)
                            if todo and j % 3 == 2:
                                edge(at.plus(1), todo.pop(0))
                            ch.wait(m_now)
                        if not first:
                            ch.tell(s_state)
                        for j in range(J3 - 2, -1, -1):
                            m_now = ch.do(e.scalar_tensor_tensor(
                                out=Sb[:, j, 0:CH], in0=Sb[:, j + 1, 0:CH], scalar=apart[:, bass.ds(at.of(J3, j + 1), 1)],
                                in1=Sb[:, j, 0:CH], op0=ALU.add, op1=ALU.max))
                            if todo and j % 2 == 1 and j > 1:
                                edge(at.plus(1), todo.pop(0))
                            ch.wait(m_now)
                            if j in PAIRS:
                                e.sem_inc(s_max, 1)
                        ch.do(e.tensor_copy(eidx[at.b][:, :], end_to[:, at.cols(J3)]))
                        ch.do(e.tensor_tensor(Tb[:, 0:J0, 0:CH], Tb[:, 0:J0, 0:CH], Sb[:, 0:J0, 0:CH], ALU.subtract))
                        ch.to(e.tensor_tensor(drop[:, :], So[:, J3 - 1, 0:CH], Sb[:, 0, 0:CH], ALU.subtract))
                        ch.do(e.tensor_scalar(drop[:, :], drop[:, :], 0.0, None, ALU.min))
                        ch.tell(s_e)
                        for n in todo:
                            edge(at.plus(1), n)
                        for cols, n in ((slice(J0, J3), len(PAIRS)), (slice(0, J0), NX)):
                            e.wait_ge(s_x, at.of(NX, NX + n))
                            ch.do(e.tensor_tensor(Sb[:, cols, 2 * CH:], Tb[:, cols, CH:], Sb[:, cols, CH:2 * CH], ALU.mult))
                        ch.do(e.tensor_tensor(carried[:, :].rearrange("p (t c) -> p t c", t=2),
                                              So[:, J3 - 1, CH:].rearrange("p (t c) -> p t c", t=2),
                                              scale[:, None, :].to_broadcast([P, 2, CH]), ALU.mult))
                        ch.tell(s_step)

                    for n in range(len(TAKES["dve"])):
                        edge(At(0), n)
                    walk(e, NB3, a_block, ch, 3 * J3 - 1 + 7, head=2)
                    for j in range(J3):
                        sums(At(NB3 - 1), j)
                        ch.sync()
                    ch.tell(s_state)
            banks.close()

            TT = sbl("TT", [P, 6, P])
            Mx = sbl("Mx", [P, 2, P])
            ea, eb = sbl("ea", [P, 2, P]), sbl("eb", [P, 2, P])
            apT = sbl("apT", [P, P])
            sh = sbl("sh", [P, 6, P])
            cin = sbl("cin", [P, S3])
            own = sbl("own", [P, S3])
            top = sbl("top", [P, CH])
            e1, e2 = sbl("e1", [P, CH]), sbl("e2", [P, CH])
            last_state = S[1][:, J3 - 1, :]
            pT, pB = psl("turn0"), psl("turn1")
            pC, pD = psl("back0"), psl("back1")
            s_u, s_pt, s_d, s_ex, s_sh, s_pb, s_own, s_mrg, s_put = seml("u", "pt", "d", "ex", "sh", "pb", "own", "mrg", "put")
            with nc.Block() as block:
                @block.tensor
                def _(e):
                    for k in range(6):
                        e.transpose((pT, pB)[k // 4][:, k % 4 * P:(k % 4 + 1) * P],
                                    last_state[:, k * P:(k + 1) * P], ident[:, :]).then_inc(s_pt, 1)
                    e.wait_ge(s_sh, 1)
                    for k in range(6):
                        e.transpose((pC, pD)[k // 4][:, k % 4 * P:(k % 4 + 1) * P], sh[:, k, :], ident[:, :]).then_inc(s_pb, 1)

                @block.gpsimd
                def _(e):
                    e.indirect_dma_start(out=own[:, :], out_offset=None, in_=state3,
                                         in_offset=indices(first_node, 0)).then_inc(s_own, 16)
                    e.wait_ge(s_own, 16)
                    e.wait_ge(s_mrg, 1)
                    e.indirect_dma_start(out=state3, out_offset=indices(carry_to, 0), in_=own[:, :],
                                         in_offset=None, bounds_check=NP - 1, oob_is_err=False).then_inc(s_put, 16)
                    e.wait_ge(s_put, 16)

                @block.scalar
                def _(e):
                    e.wait_ge(s_d, 1)
                    e.activation(ea[:, :, :], ea[:, :, :], ACT.Exp).then_inc(s_ex, 1)
                    e.activation(eb[:, :, :], eb[:, :, :], ACT.Exp).then_inc(s_ex, 1)
                    e.wait_ge(s_d, 2)
                    e.activation(e1[:, :], e1[:, :], ACT.Exp).then_inc(s_ex, 1)
                    e.activation(e2[:, :], e2[:, :], ACT.Exp).then_inc(s_ex, 1)

                @block.vector
                def _(e):
                    ch = Chain(e, s_u)
                    ch.do(e.tensor_scalar(apT[:, :], through[:, :], BIG, -BIG, ALU.mult, ALU.add))
                    ch.do(e.memset(sh[:, 0:2, 0:1], -BIG))
                    ch.do(e.memset(sh[:, 2:6, 0:1], 0.0))
                    ch.do(e.memset(ea[:, :, 0:1], 0.0))
                    e.wait_ge(s_pt, 6)
                    ch.do(e.tensor_copy(TT[:, 0:4, :].rearrange("p k n -> p (k n)"), pT[:, :]))
                    ch.to(e.tensor_copy(TT[:, 4:6, :].rearrange("p k n -> p (k n)"), pB[:, 0:2 * P]))
                    for k in range(2):
                        ch.do(e.tensor_tensor_scan(Mx[:, k, :], apT[:, :], TT[:, k, :], -BIG, ALU.add, ALU.max))
                    ch.sync()
                    ch.do(e.tensor_tensor(ea[:, :, 1:P], Mx[:, :, 0:P - 1], Mx[:, :, 1:P], ALU.subtract))
                    ch.do(e.tensor_tensor(eb[:, :, :], TT[:, 0:2, :], Mx[:, :, :], ALU.subtract))
                    ch.sync()
                    ch.do(e.tensor_scalar(ea[:, :, :], ea[:, :, :], 0.0, None, ALU.min))
                    ch.tell(s_d)
                    e.wait_ge(s_ex, 2)
                    ch.do(e.tensor_tensor(ea[:, :, :], ea[:, :, :],
                                          through[:, None, :].to_broadcast([P, 2, P]), ALU.mult))
                    for t in range(2):
                        ch.do(e.tensor_tensor(TT[:, 2 + 2 * t:4 + 2 * t, :], TT[:, 2 + 2 * t:4 + 2 * t, :], eb[:, :, :], ALU.mult))
                    ch.sync()
                    ch.do(e.tensor_copy(sh[:, 0:2, 1:P], Mx[:, :, 0:P - 1]))
                    for k in range(2, 6):
                        ch.do(e.tensor_tensor_scan(sh[:, k, 1:P], ea[:, k % 2, 0:P - 1], TT[:, k, 0:P - 1], 0.0,
                                                   ALU.mult, ALU.add))
                    ch.tell(s_sh)
                    e.wait_ge(s_pb, 6)
                    ch.do(e.tensor_copy(cin[:, 0:4 * P], pC[:, :]))
                    ch.to(e.tensor_copy(cin[:, 4 * P:], pD[:, 0:2 * P]))
                    e.wait_ge(s_own, 16)
                    ch.to(e.tensor_tensor(top[:, :], cin[:, 0:CH], own[:, 0:CH], ALU.max))
                    ch.do(e.tensor_tensor(e1[:, :], own[:, 0:CH], top[:, :], ALU.subtract))
                    ch.do(e.tensor_tensor(e2[:, :], cin[:, 0:CH], top[:, :], ALU.subtract))
                    ch.tell(s_d)
                    e.wait_ge(s_ex, 4)
                    for t in (1, 2):
                        ch.do(e.tensor_tensor(own[:, t * CH:(t + 1) * CH], own[:, t * CH:(t + 1) * CH], e1[:, :], ALU.mult))
                        ch.do(e.tensor_tensor(cin[:, t * CH:(t + 1) * CH], cin[:, t * CH:(t + 1) * CH], e2[:, :], ALU.mult))
                    ch.sync()
                    ch.do(e.tensor_tensor(own[:, CH:], own[:, CH:], cin[:, CH:], ALU.add))
                    ch.do(e.tensor_copy(own[:, 0:CH], top[:, :]))
                    ch.tell(s_mrg)

        c, sbl, psl, seml = stage("attn_nodes")
        with c:
            G = 7
            st = [sbl(f"st{q}", [P, G, 2 * CH]) for q in range(2)]
            s_v, s_ld0, s_ld1, s_done = seml("v", "ld0", "ld1", "done")
            s_ld = (s_ld0, s_ld1)
            rows = by_node(state3)
            with nc.Block() as block:
                @block.sync
                def _(e):
                    for k in range(C // G):
                        if k >= 2:
                            e.wait_ge(s_done, k - 1)
                        e.dma_start(st[k % 2][:, :, :], rows[:, k * G:(k + 1) * G, CH:]).then_inc(s_ld[k % 2], 16)

                @block.vector
                def _(e):
                    ch = Chain(e, s_v)
                    for k in range(C // G):
                        e.wait_ge(s_ld[k % 2], 16 * (k // 2 + 1))
                        den, num = st[k % 2][:, :, 0:CH], st[k % 2][:, :, CH:]
                        ch.to(e.tensor_scalar(den, den, 1e-30, None, ALU.max))
                        ch.to(e.reciprocal(den, den))
                        ch.to(e.tensor_tensor(num, num, den, ALU.mult))
                        ch.to(e.tensor_reduce(agg[:, k * G:(k + 1) * G, :],
                                              num.rearrange("p g (i o) -> p g o i", i=D), AX.X, ALU.add))
                        e.sem_inc(s_done, 1)
                    ch.to(e.tensor_tensor(x[:, :, :], x[:, :, :], agg[:, :, :], ALU.add))

        c, sbl, psl, seml = stage("store")
        s_out, = seml("out")
        with nc.Block() as block:
            @block.sync
            def _(e):
                e.dma_start(out, x[:, :, :]).then_inc(s_out, 16)
                e.wait_ge(s_out, 16)


_WEIGHTS = ["L0_gnn_W_gcn", "L0_gnn_W1", "L0_gnn_W2", "L1_gnn_W1", "L1_gnn_W2", "L3_gnn_W_msg", "L3_gnn_W_attn"]
_COLUMNS = ["L0_gnn_b1"]
_ROWS = ["L0_gnn_b2", "L1_gnn_b1", "L1_gnn_b2", "L1_gnn_bias", "L1_gnn_gamma", "L1_gnn_beta", "L2_gnn_b1",
         "L2_gnn_b2", "L3_gnn_b_msg", "L3_gnn_b_attn"]


def kernel(**inputs):
    import numpy as np
    import concourse.bacc as bacc
    from concourse.bass_utils import run_bass_kernel_spmd

    got = {k: np.asarray(v) for k, v in inputs.items()}
    pad = P * L - E

    def edges(v):
        v = np.concatenate([v, np.zeros((pad, v.shape[1]), v.dtype)])
        return np.ascontiguousarray(v.reshape(P, L, -1).transpose(2, 1, 0))

    src = np.concatenate([got["src"], np.full(pad, NP - 1, np.int32)])
    dst = np.concatenate([[-1], got["dst"], np.full(pad, NP - 1), [-1]]).astype(np.int32)
    nodes = np.concatenate([got["x"], np.zeros((NP - N, D), np.float32)])
    arrays = {
        "x": np.ascontiguousarray(nodes.reshape(C, P, D).transpose(1, 0, 2)),
        "src": src.reshape(P, L),
        "dst": np.stack([dst[p * L:p * L + L + 2] for p in range(P)]),
        "ef16": edges(got["edge_attr_16"]),
        "ef6": edges(got["edge_attr_6"]),
        "L2_W1T": np.ascontiguousarray(got["L2_gnn_W1"].T),
        "L2_W2T": np.ascontiguousarray(got["L2_gnn_W2"].T),
    }
    arrays.update({k: got[k] for k in _WEIGHTS})
    arrays.update({k: got[k].reshape(-1, 1) for k in _COLUMNS})
    arrays.update({k: got[k].reshape(1, -1) for k in _ROWS})
    nc = bacc.Bacc("TRN2", target_bir_lowering=False, num_devices=1)
    a = {k: nc.dram_tensor(f"in_{k}", v.shape, mybir.dt.from_np(v.dtype), kind="ExternalInput").ap()
         for k, v in arrays.items()}
    out = nc.dram_tensor("out_x", (P, C, D), F32, kind="ExternalOutput").ap()
    gnn_kernel(nc, a, out)
    r = run_bass_kernel_spmd(nc, [{f"in_{k}": v for k, v in arrays.items()}], core_ids=[0])
    res = r.results[0]["out_x"]
    return np.ascontiguousarray(res.transpose(1, 0, 2).reshape(NP, D)[:N])
```
